# Optimizing a Trainium2 kernel written in Bass

```python
import numpy as np
import jax
import jax.numpy as jnp

def _softmax(x, axis=-1):
    return jax.nn.softmax(x, axis=axis)

def _gelu(x):
    return jax.nn.gelu(x, approximate=True)

def _silu(x):
    return jax.nn.silu(x)

def _sigmoid(x):
    return jax.nn.sigmoid(x)

def _layernorm(x, axis=-1, eps=1e-05):
    m = jnp.mean(x, axis=axis, keepdims=True)
    v = jnp.var(x, axis=axis, keepdims=True)
    return (x - m) / jnp.sqrt(v + eps)

def _scatter_add(tgt, idx, src, axis=0):
    return tgt.at[idx].add(src)

def _segment_sum(src, seg, n):
    return jax.ops.segment_sum(src, seg, n)
kernel_name = 'mk_xattn_ffn_d4_seqx_r4_899dbc'

def setup_inputs(seed: int=0):
    np.random.seed(seed)
    _w = jnp.asarray

    def _rec_inputs():
        import jax
        import jax.numpy as jnp
        _rk = jax.random.key(seed)
        x = -0.0002928 + 1 * jax.random.normal(jax.random.fold_in(_rk, 1), (8, 256, 256), jnp.float32)
        _lenS = 256 - jax.random.randint(jax.random.fold_in(_rk, 7), (8,), 0, max(1, 256 // 4) + 1, jnp.int32)
        _lenS2 = 256 - jax.random.randint(jax.random.fold_in(_rk, 8), (8,), 0, max(1, 256 // 4) + 1, jnp.int32)
        _ctx_1024P = jax.random.normal(jax.random.fold_in(_rk, 11), (8, 16, 256), jnp.float32)
        _ctx_1024c = jax.random.dirichlet(jax.random.fold_in(_rk, 511), 0.3 * jnp.ones((16,), jnp.float32), (8, 256))
        _ctx_1024t = jnp.einsum('bsk,bkd->bsd', _ctx_1024c, _ctx_1024P)
        _ctx_1024t = _ctx_1024t * jax.lax.rsqrt(jnp.mean(jnp.square(_ctx_1024t)) + 1e-12) * 0.953939
        ctx_1024 = -1.39393e-06 + 0.999914 * (_ctx_1024t + 0.3 * jax.random.normal(jax.random.fold_in(_rk, 611), (8, 256, 256), jnp.float32))
        _validS = jnp.arange(256)[None, :] < _lenS[:, None]
        _validS2 = jnp.arange(256)[None, :] < _lenS2[:, None]
        _causal = jnp.tril(jnp.ones((256, 256), dtype=bool))
        mask_BxSxS2_ik1 = jnp.where(jnp.broadcast_to(_validS2[:, None, :], (8, 256, 256)), 1, 0).astype(jnp.int32)
        return (x, ctx_1024, mask_BxSxS2_ik1)
    x, ctx_1024, mask_BxSxS2_ik1 = _rec_inputs()

    def _L0_xattn_setup():
        import jax, jax.numpy as jnp
        import numpy as np
        H = 16
        NEG = -10000000000.0
        key = jax.random.key(seed)
        ks = jax.random.split(key, 12)
        B, S, D = (2, 512, 256)
        sc = 1.0 / np.sqrt(D)
        inp = {'q': jax.random.normal(ks[0], (B, S, D), jnp.float32), 'k': jax.random.normal(ks[1], (B, S, D), jnp.float32), 'v': jax.random.normal(ks[2], (B, S, D), jnp.float32), 'Wq': jax.random.normal(ks[3], (D, D), jnp.float32) * sc, 'bq': jax.random.normal(ks[4], (D,), jnp.float32) * 0.02, 'Wk': jax.random.normal(ks[5], (D, D), jnp.float32) * sc, 'bk': jax.random.normal(ks[6], (D,), jnp.float32) * 0.02, 'Wv': jax.random.normal(ks[7], (D, D), jnp.float32) * sc, 'bv': jax.random.normal(ks[8], (D,), jnp.float32) * 0.02, 'Wo': jax.random.normal(ks[9], (D, D), jnp.float32) * sc, 'bo': jax.random.normal(ks[10], (D,), jnp.float32) * 0.02, 'mask': jax.random.randint(ks[11], (B, S, S), 0, 2, jnp.int32)}
        return inp
    _L0_xattn_all = _L0_xattn_setup()
    _L0_xattn_in = {k: v for k, v in _L0_xattn_all.items() if k in ('Wq', 'bq', 'Wk', 'bk', 'Wv', 'bv', 'Wo', 'bo')}
    del _L0_xattn_all

    def _L0_ffn_setup():
        import jax, jax.numpy as jnp
        import numpy as np
        D_MODEL = 256
        D_FF = 1024
        N_EXPERTS = 8
        INIT_SCALE = 0.1

        def _trunc_normal(key, shape, std):
            return std * jax.random.truncated_normal(key, -2.0, 2.0, shape, dtype=jnp.float32)
        key = jax.random.key(seed)
        ks = jax.random.split(key, 5)
        x = jax.random.normal(ks[0], (4, 256, D_MODEL), dtype=jnp.float32)
        router_W = _trunc_normal(ks[1], (D_MODEL, N_EXPERTS), INIT_SCALE / np.sqrt(D_MODEL))
        router_b = jnp.zeros((N_EXPERTS,), dtype=jnp.float32)
        W1 = _trunc_normal(ks[2], (N_EXPERTS, D_MODEL, D_FF), INIT_SCALE / np.sqrt(D_MODEL))
        b1 = jnp.zeros((N_EXPERTS, D_FF), dtype=jnp.float32)
        W2 = _trunc_normal(ks[3], (N_EXPERTS, D_FF, D_MODEL), INIT_SCALE / np.sqrt(D_FF))
        b2 = jnp.zeros((N_EXPERTS, D_MODEL), dtype=jnp.float32)
        return {'x': x, 'router_W': router_W, 'router_b': router_b, 'W1': W1, 'b1': b1, 'W2': W2, 'b2': b2}
    _L0_ffn_all = _L0_ffn_setup()
    _L0_ffn_in = {k: v for k, v in _L0_ffn_all.items() if k in ('router_W', 'router_b', 'W1', 'b1', 'W2', 'b2')}
    del _L0_ffn_all

    def _L1_xattn_setup():
        import math
        import jax, jax.numpy as jnp
        import numpy as np
        H = 16
        D_MODEL = 256
        D_K = 64
        D_V = 64
        key = jax.random.key(seed)
        ks = jax.random.split(key, 7)
        b, n = (2, 512)
        scale = 1.0 / math.sqrt(D_MODEL)
        return {'q': jax.random.normal(ks[0], (b, n, D_MODEL), jnp.float32), 'k': jax.random.normal(ks[1], (b, n, D_MODEL), jnp.float32), 'v': jax.random.normal(ks[2], (b, n, D_MODEL), jnp.float32), 'w_q': jax.random.normal(ks[3], (H * D_K, D_MODEL), jnp.float32) * scale, 'w_k': jax.random.normal(ks[4], (H * D_K, D_MODEL), jnp.float32) * scale, 'w_v': jax.random.normal(ks[5], (H * D_V, D_MODEL), jnp.float32) * scale, 'w_o': jax.random.normal(ks[6], (D_MODEL, H * D_V), jnp.float32) * scale}
    _L1_xattn_all = _L1_xattn_setup()
    _L1_xattn_in = {k: v for k, v in _L1_xattn_all.items() if k in ('w_q', 'w_k', 'w_v', 'w_o')}
    del _L1_xattn_all

    def _L1_ffn_setup():
        import jax, jax.numpy as jnp
        import numpy as np
        JITTER_EPS = 0.01

        def phi_routing(logits, jitter_eps=JITTER_EPS):
            m, sel = jax.lax.top_k(logits, 2)
            T, E = logits.shape
            m1 = m[:, :1]
            factor1 = jnp.maximum(jnp.abs(logits), m1)
            mask1 = (m1 - logits) / factor1 > 2.0 * jitter_eps
            p1 = jax.nn.softmax(jnp.where(mask1, -jnp.inf, logits), axis=-1)
            mult1 = jnp.take_along_axis(p1, sel[:, :1], axis=-1)
            m2 = m[:, 1:2]
            factor2 = jnp.maximum(jnp.abs(logits), m2)
            mask2 = (m2 - logits) / factor2 > 2.0 * jitter_eps
            drop_top1 = jnp.arange(E)[None, :] == sel[:, :1]
            p2 = jax.nn.softmax(jnp.where(mask2 | drop_top1, -jnp.inf, logits), axis=-1)
            mult2 = jnp.take_along_axis(p2, sel[:, 1:2], axis=-1)
            return (jnp.concatenate([mult1, mult2], axis=-1), sel)
        key = jax.random.key(seed)
        k = jax.random.split(key, 5)
        B, S, H, F, E = (1, 128, 256, 1024, 8)
        return {'hidden_states': jax.random.normal(k[0], (B, S, H), jnp.float32), 'gate_w': jax.random.normal(k[1], (E, H), jnp.float32) * 0.02, 'w1': jax.random.normal(k[2], (E, F, H), jnp.float32) * 0.02, 'w2': jax.random.normal(k[3], (E, H, F), jnp.float32) * 0.02, 'w3': jax.random.normal(k[4], (E, F, H), jnp.float32) * 0.02}
    _L1_ffn_all = _L1_ffn_setup()
    _L1_ffn_in = {k: v for k, v in _L1_ffn_all.items() if k in ('gate_w', 'w1', 'w2', 'w3')}
    del _L1_ffn_all

    def _L2_xattn_setup():
        import jax, jax.numpy as jnp
        import numpy as np
        from math import sqrt
        key = jax.random.key(seed)
        kq, kk, kv = jax.random.split(key, 3)
        B, S, D = (8, 1024, 256)
        q = jax.random.normal(kq, (B, S, D), dtype=jnp.float32)
        k = jax.random.normal(kk, (B, S, D), dtype=jnp.float32)
        v = jax.random.normal(kv, (B, S, D), dtype=jnp.float32)
        return {'q': q, 'k': k, 'v': v}
    _L2_xattn_all = _L2_xattn_setup()
    _L2_xattn_in = {k: v for k, v in _L2_xattn_all.items() if k in ()}
    del _L2_xattn_all

    def _L2_ffn_setup():
        import jax, jax.numpy as jnp
        import numpy as np
        B, S, K, N = (8, 2048, 256, 256)
        key = jax.random.key(seed)
        k1, k2, k3, k4 = jax.random.split(key, 4)
        x = jax.random.normal(k1, (B, S, K), dtype=jnp.float32)
        CB = jnp.clip(jnp.round(jax.random.normal(k2, (N, K), dtype=jnp.float32) * 42.0), -127.0, 127.0)
        SCB = jax.random.uniform(k3, (N,), dtype=jnp.float32, minval=0.5, maxval=2.0)
        bias = jax.random.normal(k4, (N,), dtype=jnp.float32) * 0.02
        return {'x': x, 'CB': CB, 'SCB': SCB, 'bias': bias}
    _L2_ffn_all = _L2_ffn_setup()
    _L2_ffn_in = {k: v for k, v in _L2_ffn_all.items() if k in ('CB', 'SCB', 'bias')}
    del _L2_ffn_all

    def _L3_xattn_setup():
        import jax, jax.numpy as jnp
        import numpy as np
        import math
        B, SQ, SK, D = (4, 512, 512, 256)
        key = jax.random.key(seed)
        ks = jax.random.split(key, 9)
        s = 1.0 / math.sqrt(D)
        return {'q': jax.random.normal(ks[0], (B, SQ, D), jnp.float32), 'k': jax.random.normal(ks[1], (B, SK, D), jnp.float32), 'v': jax.random.normal(ks[2], (B, SK, D), jnp.float32), 'Wq': jax.random.normal(ks[3], (D, D), jnp.float32) * s, 'bq': jax.random.normal(ks[4], (D,), jnp.float32) * s, 'Wk': jax.random.normal(ks[5], (D, D), jnp.float32) * s, 'bk': jax.random.normal(ks[6], (D,), jnp.float32) * s, 'Wv': jax.random.normal(ks[7], (D, D), jnp.float32) * s, 'bv': jax.random.normal(ks[8], (D,), jnp.float32) * s}
    _L3_xattn_all = _L3_xattn_setup()
    _L3_xattn_in = {k: v for k, v in _L3_xattn_all.items() if k in ('Wq', 'bq', 'Wk', 'bk', 'Wv', 'bv')}
    del _L3_xattn_all

    def _L3_ffn_setup():
        import jax, jax.numpy as jnp
        import numpy as np
        B, S, D_MODEL, D_HIDDEN = (4, 512, 256, 1024)

        def act_quant(x):
            scale = 127.0 / jnp.clip(jnp.max(jnp.abs(x), axis=-1, keepdims=True), 1e-05)
            return jnp.clip(jnp.round(x * scale), -128, 127) / scale

        def weight_quant(w):
            scale = 1.0 / jnp.clip(jnp.mean(jnp.abs(w)), 1e-05)
            return jnp.clip(jnp.round(w * scale), -1, 1) / scale

        def bit_linear(x, w):
            xq = x + jax.lax.stop_gradient(act_quant(x) - x)
            wq = w + jax.lax.stop_gradient(weight_quant(w) - w)
            return jnp.einsum('bsd,hd->bsh', xq, wq)

        def depthwise_conv1d(x_bcl, w, b):
            y = jax.lax.conv_general_dilated(x_bcl, w, window_strides=(1,), padding=[(1, 1)], dimension_numbers=('NCH', 'OIH', 'NCH'), feature_group_count=x_bcl.shape[1])
            return y + b[None, :, None]
        key = jax.random.key(seed)
        ks = jax.random.split(key, 5)
        lim1 = 1.0 / np.sqrt(D_MODEL)
        lim2 = 1.0 / np.sqrt(D_HIDDEN)
        limc = 1.0 / np.sqrt(3.0)
        return {'x': jax.random.normal(ks[0], (B, S, D_MODEL), dtype=jnp.float32), 'w1': jax.random.uniform(ks[1], (D_HIDDEN, D_MODEL), jnp.float32, -lim1, lim1), 'conv_w': jax.random.uniform(ks[2], (D_HIDDEN, 1, 3), jnp.float32, -limc, limc), 'conv_b': jax.random.uniform(ks[3], (D_HIDDEN,), jnp.float32, -limc, limc), 'w2': jax.random.uniform(ks[4], (D_MODEL, D_HIDDEN), jnp.float32, -lim2, lim2)}
    _L3_ffn_all = _L3_ffn_setup()
    _L3_ffn_in = {k: v for k, v in _L3_ffn_all.items() if k in ('w1', 'conv_w', 'conv_b', 'w2')}
    del _L3_ffn_all
    return {'x': x, 'ctx_1024': ctx_1024, 'mask_BxSxS2_ik1': mask_BxSxS2_ik1, 'L0_xattn_Wq': _L0_xattn_in['Wq'], 'L0_xattn_bq': _L0_xattn_in['bq'], 'L0_xattn_Wk': _L0_xattn_in['Wk'], 'L0_xattn_bk': _L0_xattn_in['bk'], 'L0_xattn_Wv': _L0_xattn_in['Wv'], 'L0_xattn_bv': _L0_xattn_in['bv'], 'L0_xattn_Wo': _L0_xattn_in['Wo'], 'L0_xattn_bo': _L0_xattn_in['bo'], 'L0_ffn_router_W': _L0_ffn_in['router_W'], 'L0_ffn_router_b': _L0_ffn_in['router_b'], 'L0_ffn_W1': _L0_ffn_in['W1'], 'L0_ffn_b1': _L0_ffn_in['b1'], 'L0_ffn_W2': _L0_ffn_in['W2'], 'L0_ffn_b2': _L0_ffn_in['b2'], 'L1_xattn_w_q': _L1_xattn_in['w_q'], 'L1_xattn_w_k': _L1_xattn_in['w_k'], 'L1_xattn_w_v': _L1_xattn_in['w_v'], 'L1_xattn_w_o': _L1_xattn_in['w_o'], 'L1_ffn_gate_w': _L1_ffn_in['gate_w'], 'L1_ffn_w1': _L1_ffn_in['w1'], 'L1_ffn_w2': _L1_ffn_in['w2'], 'L1_ffn_w3': _L1_ffn_in['w3'], 'L2_ffn_CB': _L2_ffn_in['CB'], 'L2_ffn_SCB': _L2_ffn_in['SCB'], 'L2_ffn_bias': _L2_ffn_in['bias'], 'L3_xattn_Wq': _L3_xattn_in['Wq'], 'L3_xattn_bq': _L3_xattn_in['bq'], 'L3_xattn_Wk': _L3_xattn_in['Wk'], 'L3_xattn_bk': _L3_xattn_in['bk'], 'L3_xattn_Wv': _L3_xattn_in['Wv'], 'L3_xattn_bv': _L3_xattn_in['bv'], 'L3_ffn_w1': _L3_ffn_in['w1'], 'L3_ffn_conv_w': _L3_ffn_in['conv_w'], 'L3_ffn_conv_b': _L3_ffn_in['conv_b'], 'L3_ffn_w2': _L3_ffn_in['w2']}

def reference(x, ctx_1024, mask_BxSxS2_ik1, L0_xattn_Wq, L0_xattn_bq, L0_xattn_Wk, L0_xattn_bk, L0_xattn_Wv, L0_xattn_bv, L0_xattn_Wo, L0_xattn_bo, L0_ffn_router_W, L0_ffn_router_b, L0_ffn_W1, L0_ffn_b1, L0_ffn_W2, L0_ffn_b2, L1_xattn_w_q, L1_xattn_w_k, L1_xattn_w_v, L1_xattn_w_o, L1_ffn_gate_w, L1_ffn_w1, L1_ffn_w2, L1_ffn_w3, L2_ffn_CB, L2_ffn_SCB, L2_ffn_bias, L3_xattn_Wq, L3_xattn_bq, L3_xattn_Wk, L3_xattn_bk, L3_xattn_Wv, L3_xattn_bv, L3_ffn_w1, L3_ffn_conv_w, L3_ffn_conv_b, L3_ffn_w2):
    import jax
    import jax.numpy as jnp

    def _L0_xattn_ref(q, k, v, Wq, bq, Wk, bk, Wv, bv, Wo, bo, mask):
        import jax, jax.numpy as jnp
        import numpy as np
        H = 16
        NEG = -10000000000.0
        B, S, D = q.shape
        dk = D // H
        qh = (q @ Wq.T + bq).reshape(B, S, H, dk).transpose(0, 2, 1, 3)
        kh = (k @ Wk.T + bk).reshape(B, S, H, dk).transpose(0, 2, 1, 3)
        vh = (v @ Wv.T + bv).reshape(B, S, H, dk).transpose(0, 2, 1, 3)
        scores = jnp.einsum('bhqd,bhkd->bhqk', qh, kh) / jnp.sqrt(jnp.float32(dk))
        scores = jnp.where(mask[:, None, :, :] == 0, jnp.float32(NEG), scores)
        attn = jax.nn.softmax(scores, axis=-1)
        ctx = jnp.einsum('bhqk,bhkd->bhqd', attn, vh)
        concat = ctx.transpose(0, 2, 1, 3).reshape(B, S, D)
        return concat @ Wo.T + bo

    def _L0_ffn_ref(x, router_W, router_b, W1, b1, W2, b2):
        import jax, jax.numpy as jnp
        import numpy as np
        D_MODEL = 256
        D_FF = 1024
        N_EXPERTS = 8
        INIT_SCALE = 0.1

        def _trunc_normal(key, shape, std):
            return std * jax.random.truncated_normal(key, -2.0, 2.0, shape, dtype=jnp.float32)
        logits = jnp.einsum('bsd,de->bse', x.astype(jnp.float32), router_W) + router_b
        probs = jax.nn.softmax(logits, axis=-1)
        top1 = jnp.argmax(probs, axis=-1)
        mask = jax.nn.one_hot(top1, N_EXPERTS, dtype=x.dtype)
        gates = mask * probs.astype(x.dtype)
        h = jax.nn.relu(jnp.einsum('bsd,edf->besf', x, W1) + b1[:, None, :])
        y = jnp.einsum('besf,efd->besd', h, W2) + b2[:, None, :]
        out = jnp.einsum('bse,besd->bsd', gates, y)
        return out

    def _L1_xattn_ref(q, k, v, w_q, w_k, w_v, w_o):
        import math
        import jax, jax.numpy as jnp
        import numpy as np
        H = 16
        D_MODEL = 256
        D_K = 64
        D_V = 64
        b, n, _ = q.shape
        qh = (q @ w_q.T).reshape(b, n, H, D_K).transpose(0, 2, 1, 3)
        kh = (k @ w_k.T).reshape(b, n, H, D_K).transpose(0, 2, 1, 3)
        vh = (v @ w_v.T).reshape(b, n, H, D_V).transpose(0, 2, 1, 3)
        scores = jnp.einsum('bhid,bhjd->bhij', qh, kh) / math.sqrt(D_K)
        causal = jnp.tril(jnp.ones((n, n), dtype=bool))
        scores = jnp.where(causal[None, None], scores, -jnp.inf)
        attn = jax.nn.softmax(scores, axis=-1)
        out = jnp.einsum('bhij,bhjd->bhid', attn, vh)
        out = out.transpose(0, 2, 1, 3).reshape(b, n, H * D_V)
        return out @ w_o.T

    def _L1_ffn_ref(hidden_states, gate_w, w1, w2, w3):
        import jax, jax.numpy as jnp
        import numpy as np
        JITTER_EPS = 0.01

        def phi_routing(logits, jitter_eps=JITTER_EPS):
            m, sel = jax.lax.top_k(logits, 2)
            T, E = logits.shape
            m1 = m[:, :1]
            factor1 = jnp.maximum(jnp.abs(logits), m1)
            mask1 = (m1 - logits) / factor1 > 2.0 * jitter_eps
            p1 = jax.nn.softmax(jnp.where(mask1, -jnp.inf, logits), axis=-1)
            mult1 = jnp.take_along_axis(p1, sel[:, :1], axis=-1)
            m2 = m[:, 1:2]
            factor2 = jnp.maximum(jnp.abs(logits), m2)
            mask2 = (m2 - logits) / factor2 > 2.0 * jitter_eps
            drop_top1 = jnp.arange(E)[None, :] == sel[:, :1]
            p2 = jax.nn.softmax(jnp.where(mask2 | drop_top1, -jnp.inf, logits), axis=-1)
            mult2 = jnp.take_along_axis(p2, sel[:, 1:2], axis=-1)
            return (jnp.concatenate([mult1, mult2], axis=-1), sel)
        B, S, H = hidden_states.shape
        E = w1.shape[0]
        x = hidden_states.reshape(-1, H)
        logits = x @ gate_w.T
        routing_weights, selected = phi_routing(logits)
        T = x.shape[0]
        wte = jnp.zeros((T, E), x.dtype).at[jnp.arange(T)[:, None], selected].add(routing_weights)
        out = jnp.zeros_like(x)
        for e in range(E):
            h = jax.nn.silu(x @ w1[e].T) * (x @ w3[e].T)
            out = out + wte[:, e:e + 1] * (h @ w2[e].T)
        return out.reshape(B, S, H)

    def _L2_xattn_ref(q, k, v):
        import jax, jax.numpy as jnp
        import numpy as np
        from math import sqrt
        S = q.shape[1]
        scale = 1.0 / sqrt(S)
        qn = q * scale
        kn = k * scale
        kv_mat = jnp.einsum('bsd,bse->bde', kn, v)
        out = jnp.einsum('bsd,bde->bse', qn, kv_mat)
        return out

    def _L2_ffn_ref(x, CB, SCB, bias):
        import jax, jax.numpy as jnp
        import numpy as np
        B, S, K, N = (8, 2048, 256, 256)
        out = jnp.einsum('bsk,nk->bsn', x, CB)
        out = out * (SCB * (1.0 / 127.0)) + bias
        return out

    def _L3_xattn_ref(q, k, v, Wq, bq, Wk, bk, Wv, bv):
        import jax, jax.numpy as jnp
        import numpy as np
        import math
        B, SQ, SK, D = (4, 512, 512, 256)
        qp = jnp.einsum('bsd,ed->bse', q, Wq) + bq
        kp = jnp.einsum('bsd,ed->bse', k, Wk) + bk
        vp = jnp.einsum('bsd,ed->bse', v, Wv) + bv
        scale = 1.0 / jnp.sqrt(jnp.asarray(kp.shape[-1], qp.dtype))
        scores = jnp.einsum('bqd,bkd->bqk', qp, kp) * scale
        attn = jax.nn.softmax(scores, axis=-1)
        return jnp.einsum('bqk,bkd->bqd', attn, vp)

    def _L3_ffn_ref(x, w1, conv_w, conv_b, w2):
        import jax, jax.numpy as jnp
        import numpy as np
        B, S, D_MODEL, D_HIDDEN = (4, 512, 256, 1024)

        def act_quant(x):
            scale = 127.0 / jnp.clip(jnp.max(jnp.abs(x), axis=-1, keepdims=True), 1e-05)
            return jnp.clip(jnp.round(x * scale), -128, 127) / scale

        def weight_quant(w):
            scale = 1.0 / jnp.clip(jnp.mean(jnp.abs(w)), 1e-05)
            return jnp.clip(jnp.round(w * scale), -1, 1) / scale

        def bit_linear(x, w):
            xq = x + jax.lax.stop_gradient(act_quant(x) - x)
            wq = w + jax.lax.stop_gradient(weight_quant(w) - w)
            return jnp.einsum('bsd,hd->bsh', xq, wq)

        def depthwise_conv1d(x_bcl, w, b):
            y = jax.lax.conv_general_dilated(x_bcl, w, window_strides=(1,), padding=[(1, 1)], dimension_numbers=('NCH', 'OIH', 'NCH'), feature_group_count=x_bcl.shape[1])
            return y + b[None, :, None]
        h = bit_linear(x, w1)
        h = depthwise_conv1d(h.transpose(0, 2, 1), conv_w, conv_b)
        h = h.transpose(0, 2, 1)
        h = jax.nn.silu(h)
        return bit_linear(h, w2)
    x = x + _L0_xattn_ref(_layernorm(x, axis=-1), ctx_1024, ctx_1024, L0_xattn_Wq, L0_xattn_bq, L0_xattn_Wk, L0_xattn_bk, L0_xattn_Wv, L0_xattn_bv, L0_xattn_Wo, L0_xattn_bo, mask_BxSxS2_ik1)
    x = x + _L0_ffn_ref(_layernorm(x, axis=-1), L0_ffn_router_W, L0_ffn_router_b, L0_ffn_W1, L0_ffn_b1, L0_ffn_W2, L0_ffn_b2)
    x = x + _L1_xattn_ref(_layernorm(x, axis=-1), ctx_1024, ctx_1024, L1_xattn_w_q, L1_xattn_w_k, L1_xattn_w_v, L1_xattn_w_o)
    x = x + _L1_ffn_ref(_layernorm(x, axis=-1), L1_ffn_gate_w, L1_ffn_w1, L1_ffn_w2, L1_ffn_w3)
    x = x + _L2_xattn_ref(_layernorm(x, axis=-1), ctx_1024, ctx_1024)
    x = x + _L2_ffn_ref(_layernorm(x, axis=-1), L2_ffn_CB, L2_ffn_SCB, L2_ffn_bias)
    x = x + _L3_xattn_ref(_layernorm(x, axis=-1), ctx_1024, ctx_1024, L3_xattn_Wq, L3_xattn_bq, L3_xattn_Wk, L3_xattn_bk, L3_xattn_Wv, L3_xattn_bv)
    x = x + _L3_ffn_ref(_layernorm(x, axis=-1), L3_ffn_w1, L3_ffn_conv_w, L3_ffn_conv_b, L3_ffn_w2)
    return x

_drawn_inputs = setup_inputs


def setup_inputs(seed=0):
    import zlib

    import numpy as np

    out = dict(_drawn_inputs(seed))
    spreads = {'L0_ffn_router_b': (0.0, 0.635), 'L0_ffn_b1': (0.0, 0.8), 'L0_ffn_b2': (0.0, 0.611)}
    factors = {'L0_xattn_bq': 8.0,
     'L0_xattn_bk': 64.0,
     'L0_xattn_bv': 4.775,
     'L0_xattn_bo': 3.858,
     'L0_ffn_router_W': 5.932,
     'L0_ffn_W1': 8.0,
     'L0_ffn_W2': 8.0,
     'L2_ffn_bias': 21.701,
     'L3_xattn_Wq': 2.759,
     'L3_xattn_bq': 8.0,
     'L3_xattn_Wk': 2.764,
     'L3_xattn_bk': 64.0,
     'L3_xattn_bv': 8.0,
     'L3_ffn_w1': 8.0,
     'L3_ffn_conv_w': 8.0,
     'L3_ffn_conv_b': 7.703,
     'L3_ffn_w2': 5.761}
    for name, (base, spread) in spreads.items():
        noise = np.random.default_rng([zlib.crc32(name.encode()), seed]).standard_normal(out[name].shape)
        drawn = base * np.exp(spread * noise) if base else spread * noise
        out[name] = jnp.asarray(drawn.astype(out[name].dtype))
    for name, factor in factors.items():
        out[name] = (out[name] * factor).astype(out[name].dtype)
    return out
```

```python
from contextlib import ExitStack, contextmanager

import concourse.bass as bass
from concourse import mybir

F32 = mybir.dt.float32
BF16 = mybir.dt.bfloat16
I32 = mybir.dt.int32
ALU = mybir.AluOpType
ACT = mybir.ActivationFunctionType
AX = mybir.AxisListType

P = 128
B, S, D = 8, 256, 256
DK = D // P
TT = B * S // P
TB = S // P
H = 16
D0, D1 = D // H, 64
E, F = 8, 1024
FT = F // P
EPS = 1e-5
NEG = -float(2 ** 100)
MAGIC = 1.5 * 2 ** 23
CH = 512
NCH = B * S // CH


class Stages:

    def __init__(self, nc):
        self.nc, self.ours, self.cleared = nc, [], []

    def semaphore(self, name):
        self.ours.append(self.nc.alloc_semaphore(name=name))
        return self.ours[-1]

    @contextmanager
    def stage(self):
        with ExitStack() as ctx:
            yield ctx
        for s in self.cleared:
            self.nc.release_semaphore(s)
        for s in self.ours:
            self.nc.gpsimd.sem_clear(s)
        self.cleared, self.ours = self.ours, []


def layer_norm(nc, top, tag, x, xt, ident, first=None, router=None):
    with top.stage() as ctx:
        def sb(name, shape, dt=F32):
            return ctx.enter_context(nc.sbuf_tensor(tag + name, shape, dt))

        def sem(name):
            return top.semaphore(tag + name)

        stats = sb("stats", [P, TT, 6])
        total, diff, m2, mean, diff2, var, vareps, rstd, root, guess = (
            sb(n, [P, TT]) for n in ("total", "diff", "m2", "mean", "diff2", "var", "vareps", "rstd", "root", "guess"))
        xn = sb("xn", [P, TB, D])
        xs = sb("xs", [P, TB, DK, P]) if router else None
        tp = ctx.enter_context(nc.psum_tensor(tag + "tp", [P, TB, 512], F32))
        lg = ctx.enter_context(nc.psum_tensor(tag + "lg", [P, TB, 512], F32)) if router else None
        stats_done, comb, normed, transposed, evacuated, staged, logits_done, logits_out, rooted = (
            sem(n) for n in ("stats_done", "comb", "normed", "transposed", "evacuated", "staged",
                             "logits_done", "logits_out", "rooted"))
        block = ctx.enter_context(nc.Block())

        @block.vector
        def _(dve):
            if first:
                dve.wait_ge(first, 16)
            with dve.Fori(0, TT) as t:
                dve.bn_stats(stats[:, t, :], x[:, t, :]).then_inc(stats_done, 1)
            dve.wait_ge(stats_done, TT)
            dve.tensor_tensor(total[:, :], stats[:, :, 1], stats[:, :, 4], ALU.add).then_inc(comb, 1)
            dve.tensor_tensor(diff[:, :], stats[:, :, 1], stats[:, :, 4], ALU.subtract).then_inc(comb, 1)
            dve.tensor_tensor(m2[:, :], stats[:, :, 2], stats[:, :, 5], ALU.add).then_inc(comb, 1)
            dve.wait_ge(comb, 3)
            dve.tensor_scalar(mean[:, :], total[:, :], 0.5, None, ALU.mult).then_inc(comb, 1)
            dve.tensor_tensor(diff2[:, :], diff[:, :], diff[:, :], ALU.mult).then_inc(comb, 1)
            dve.wait_ge(comb, 5)
            dve.scalar_tensor_tensor(out=var[:, :], in0=diff2[:, :], scalar=D / 4.0, in1=m2[:, :],
                                     op0=ALU.mult, op1=ALU.add).then_inc(comb, 1)
            dve.wait_ge(comb, 6)
            dve.tensor_scalar(vareps[:, :], var[:, :], 1.0 / D, EPS, ALU.mult, ALU.add).then_inc(comb, 1)
            dve.wait_ge(comb, 7)
            dve.wait_ge(rooted, 1)
            dve.reciprocal(guess[:, :], root[:, :]).then_inc(comb, 1)
            dve.wait_ge(comb, 8)
            dve.tensor_tensor(total[:, :], guess[:, :], guess[:, :], ALU.mult).then_inc(comb, 1)
            dve.wait_ge(comb, 9)
            dve.tensor_tensor(diff[:, :], total[:, :], vareps[:, :], ALU.mult).then_inc(comb, 1)
            dve.wait_ge(comb, 10)
            dve.tensor_scalar(total[:, :], diff[:, :], -0.5, 1.5, ALU.mult, ALU.add).then_inc(comb, 1)
            dve.wait_ge(comb, 11)
            dve.tensor_tensor(rstd[:, :], guess[:, :], total[:, :], ALU.mult).then_inc(comb, 1)
            dve.wait_ge(comb, 12)
            with dve.Fori(0, B) as b:
                for j in range(TB):
                    dve.wait_ge(transposed, b * TB + j + 1)
                    dve.tensor_scalar(xn[:, j, :], x[:, b * TB + j, :], mean[:, bass.ds(b * TB + j, 1)],
                                      rstd[:, bass.ds(b * TB + j, 1)], ALU.subtract, ALU.mult).then_inc(normed, 1)
                if router:
                    for j in range(TB):
                        dve.wait_ge(logits_done, b * TB + j + 1)
                        dve.wait_ge(evacuated, b * TB + j + TB + 1)
                        dve.tensor_copy(xs[:, j, :, :], xt[:, :, bass.ds((b * TB + j) * P, P)]).then_inc(staged, 1)
                    for j in range(TB):
                        dve.wait_ge(logits_done, b * TB + j + TB + 1)
                        dve.tensor_copy(router[1][:, b * TB + j, :], lg[:, j, 0:E]).then_inc(logits_out, 1)

        @block.tensor
        def _(pe):
            pe.sem_inc(transposed, TB)
            if router:
                pe.sem_inc(logits_done, TB)
            with pe.Fori(0, B) as b:
                for j in range(TB):
                    pe.wait_ge(normed, b * TB + j + 1)
                    pe.wait_ge(evacuated, b * TB + j + 1)
                    for k in range(DK):
                        mm = pe.transpose(tp[:, j, k * P:(k + 1) * P], xn[:, j, k * P:(k + 1) * P], ident[:, :])
                    mm.then_inc(transposed, 1)
                if router:
                    for j in range(TB):
                        pe.wait_ge(staged, b * TB + j + 1)
                        pe.wait_ge(logits_out, b * TB)
                        for k in range(DK):
                            mm = pe.matmul(lg[:, j, 0:E], xs[:, j, k, :], router[0][:, k, :],
                                           start=(k == 0), stop=(k == DK - 1))
                        mm.then_inc(logits_done, 1)

        @block.scalar
        def _(act):
            act.sem_inc(evacuated, TB)
            act.wait_ge(comb, 7)
            act.activation(root[:, :], vareps[:, :], ACT.Sqrt).then_inc(rooted, 1)
            with act.Fori(0, B) as b:
                for j in range(TB):
                    act.wait_ge(transposed, b * TB + j + TB + 1)
                    act.activation(xt[:, :, bass.ds((b * TB + j) * P, P)],
                                   tp[:, j, 0:D].rearrange("p (k n) -> p k n", k=DK), ACT.Copy).then_inc(evacuated, 1)


def attention0(nc, top, x, xt, io, consts):
    G, NG, W = 4, H // 4, 32
    U = H // 2
    with top.stage() as ctx:
        def sb(name, shape, dt=F32):
            return ctx.enter_context(nc.sbuf_tensor("a0_" + name, shape, dt))

        def sem(name):
            return top.semaphore("a0_" + name)

        wq, wk, wv = (sb(n, [P, DK, NG * P]) for n in ("wq", "wk", "wv"))
        wo = sb("wo", [P, NG, D])
        bq, bk = sb("bq", [P, NG]), sb("bk", [P, NG])
        bv = sb("bv", [1, H * W])
        sel = sb("sel", [P, P])
        ctxT = sb("ctxT", [P, DK, S])
        mask, maskT = sb("mask", [P, TB, S], I32), sb("maskT", [P, TB, S], I32)
        neg, negT = sb("neg", [P, TB, S], BF16), sb("negT", [P, TB, S], BF16)
        qT, kT = sb("qT", [P, NG, S]), sb("kT", [P, NG, S])
        V = sb("V", [P, TB, H, W])
        top_s = sb("top_s", [P, TB, G, NG])
        mT = sb("mT", [H, S])
        pT = sb("pT", [P, 2, 2, TB, S])
        oraw, recip, onorm = sb("oraw", [P, NG, S]), sb("recip", [P, NG, S]), sb("onorm", [P, NG, S])
        ps = ctx.enter_context(nc.psum_tensor("a0_ps", [P, 2, 4, 512], F32))
        O = ps[:, 1, 0:2, :].rearrange("p a (c n) -> p (a c) n", c=2)

        (weights, ctx_loaded, mask_loaded, q_proj, k_proj, v_proj, q_out, k_out, v_out, neg_ready,
         s_ready, max_done, mt_ready, mt_out, mrow_landed, st_ready, exp_done, pv_done, o_out,
         l_ready, recip_done, norm_done, wo_ready, resid_done) = (sem(n) for n in (
             "weights", "ctx_loaded", "mask_loaded", "q_proj", "k_proj", "v_proj", "q_out", "k_out", "v_out",
             "neg_ready", "s_ready", "max_done", "mt_ready", "mt_out", "mrow_landed", "st_ready",
             "exp_done", "pv_done", "o_out", "l_ready", "recip_done", "norm_done", "wo_ready", "resid_done"))
        block = ctx.enter_context(nc.Block())

        @block.sync
        def _(sp):
            for dst, name in ((wq, "a0_wq"), (wk, "a0_wk"), (wv, "a0_wv"), (wo, "a0_wo")):
                sp.dma_start(dst[:, :, :], io[name].rearrange("k p n -> p k n")).then_inc(weights, 16)
            for dst, name in ((bq, "a0_bq"), (bk, "a0_bk"), (bv, "a0_bv"), (sel, "a0_sel")):
                sp.dma_start(dst[:, :], io[name]).then_inc(weights, 16)
            with sp.Fori(0, B) as b:
                sp.wait_ge(v_proj, 2 * b)
                sp.dma_start(ctxT[:, :, :], io["ctxT"][bass.ds(b, 1)].rearrange("b (k p) s -> p (b k) s", p=P)
                             ).then_inc(ctx_loaded, 16)
                sp.wait_ge(neg_ready, 2 * b)
                sp.dma_start(mask[:, :, :], io["mask"][bass.ds(b, 1)].rearrange("b (t p) s -> p (b t) s", p=P)
                             ).then_inc(mask_loaded, 16)
                sp.dma_start(maskT[:, :, :], io["maskT"][bass.ds(b, 1)].rearrange("b (t p) s -> p (b t) s", p=P)
                             ).then_inc(mask_loaded, 16)
                sp.wait_ge(mt_out, b + 1)
                for g in range(G):
                    sp.dma_start(qT[W * g + D0:W * g + D0 + 1, :, :], mT[NG * g:NG * (g + 1), :]
                                 ).then_inc(mrow_landed, 16)

        @block.tensor
        def _(pe):
            pe.sem_inc(pv_done, 2)
            pe.wait_ge(weights, 16 * 8)
            with pe.Fori(0, B) as b:
                pe.wait_ge(exp_done, 8 * b)
                for n in range(NG):
                    for k in range(DK):
                        mm = pe.matmul(ps[:, 0, n // 2, (n % 2) * S:(n % 2 + 1) * S], wq[:, k, n * P:(n + 1) * P],
                                       xt[:, k, bass.ds(b * S, S)], start=(k == 0), stop=(k == DK - 1))
                    if n % 2:
                        mm.then_inc(q_proj, 1)
                pe.wait_ge(ctx_loaded, 16 * b + 16)
                for n in range(NG):
                    for k in range(DK):
                        mm = pe.matmul(ps[:, 0, 2 + n // 2, (n % 2) * S:(n % 2 + 1) * S], wk[:, k, n * P:(n + 1) * P],
                                       ctxT[:, k, :], start=(k == 0), stop=(k == DK - 1))
                    if n % 2:
                        mm.then_inc(k_proj, 1)
                pe.wait_ge(o_out, 2 * b)
                for t in range(TB):
                    for k in range(DK):
                        pe.matmul(ps[:, 1, t, :], ctxT[:, k, t * P:(t + 1) * P], wv[:, k, :],
                                  start=(k == 0), stop=False)
                    pe.matmul(ps[:, 1, t, :], consts["ones"][0:1, 0:P], bv[:, :], start=False, stop=True
                              ).then_inc(v_proj, 1)
                for n in range(NG):
                    pe.wait_ge(q_out, 4 * b + 4)
                    pe.wait_ge(k_out, 4 * b + 4)
                    pe.wait_ge(neg_ready, 2 * b + 2)
                    if n == 1:
                        pe.wait_ge(v_out, 2 * b + 2)
                        pe.wait_ge(resid_done, b)
                    if n >= 2:
                        pe.wait_ge(max_done, 4 * b + n - 1)
                    for g in range(G):
                        r = slice(W * g, W * g + D0)
                        for t in range(TB):
                            pe.matmul(ps[:, n % 2, g, t * S:(t + 1) * S], qT[r, n, t * P:(t + 1) * P], kT[r, n, :],
                                      start=True, stop=False)
                            mm = pe.matmul(ps[:, n % 2, g, t * S:(t + 1) * S], consts["identb"][:, :], neg[:, t, :],
                                           start=False, stop=True)
                    mm.then_inc(s_ready, 1)
                pe.wait_ge(max_done, 4 * b + 4)
                for t in range(TB):
                    mm = pe.transpose(ps[0:H, 1, 2, t * P:(t + 1) * P],
                                      top_s[:, t, :, :].rearrange("p g n -> p (g n)"), consts["ident"][:, :])
                mm.then_inc(mt_ready, 1)
                pe.wait_ge(mrow_landed, 64 * b + 64)
                for u in range(U + 1):
                    if u < U:
                        if u >= 2:
                            pe.wait_ge(exp_done, U * b + u - 1)
                        n, g0 = u // 2, 2 * (u % 2)
                        for t in range(TB):
                            for j in range(2):
                                r = slice(W * (g0 + j), W * (g0 + j) + D0 + 1)
                                pe.matmul(ps[:, 0, g0 + j, t * S:(t + 1) * S], kT[r, n, t * P:(t + 1) * P], qT[r, n, :],
                                          start=True, stop=False)
                                mm = pe.matmul(ps[:, 0, g0 + j, t * S:(t + 1) * S], consts["identb"][:, :],
                                               negT[:, t, :], start=False, stop=True)
                        mm.then_inc(st_ready, 1)
                    if u > 0:
                        m = u - 1
                        n, g0 = m // 2, 2 * (m % 2)
                        pe.wait_ge(exp_done, U * b + m + 1)
                        for j in range(2):
                            for t in range(TB):
                                mm = pe.matmul(O[W * (g0 + j):W * (g0 + j + 1), n, :], V[:, t, 4 * n + g0 + j, :],
                                               pT[:, m % 2, j, t, :], start=(t == 0), stop=(t == TB - 1))
                        mm.then_inc(pv_done, 1)
                for c in range(2):
                    pe.wait_ge(o_out, 2 * b + c + 1)
                    if c == 1:
                        pe.wait_ge(recip_done, 2 * b + 1)
                    pe.matmul(ps[:, 1, 2, :], sel[:, :], oraw[:, 2 * c:2 * c + 2, :].rearrange("p a n -> p (a n)"),
                              start=True, stop=True).then_inc(l_ready, 1)
                pe.wait_ge(norm_done, 2 * b + 2)
                for t in range(TB):
                    for n in range(NG):
                        mm = pe.matmul(ps[:, 1, 3, t * S:(t + 1) * S], onorm[:, n, t * P:(t + 1) * P], wo[:, n, :],
                                       start=(n == 0), stop=(n == NG - 1))
                mm.then_inc(wo_ready, 1)

        @block.scalar
        def _(act):
            act.wait_ge(weights, 16 * 8)
            with act.Fori(0, B) as b:
                for n in range(NG):
                    act.wait_ge(q_proj, 2 * b + n // 2 + 1)
                    act.wait_ge(pv_done, U * b + 2)
                    act.activation(qT[:, n, :], ps[:, 0, n // 2, (n % 2) * S:(n % 2 + 1) * S], ACT.Identity,
                                   bias=bq[:, n:n + 1]).then_inc(q_out, 1)
                for t in range(TB):
                    act.wait_ge(v_proj, 2 * b + t + 1)
                    act.activation(V[:, t, :, :].rearrange("p h w -> p (h w)"), ps[:, 1, t, :], ACT.Copy
                                   ).then_inc(v_out, 1)
                act.wait_ge(mt_ready, b + 1)
                act.wait_ge(mrow_landed, 64 * b)
                act.mul(mT[:, :], ps[0:H, 1, 2, 0:S], -1.0).then_inc(mt_out, 1)
                for u in range(U):
                    act.wait_ge(st_ready, U * b + u + 1)
                    act.wait_ge(pv_done, U * b + u + 1)
                    act.activation(pT[:, u % 2, :, :, :].rearrange("p j t n -> p j (t n)"),
                                   ps[:, 0, 2 * (u % 2):2 * (u % 2) + 2, :], ACT.Exp,
                                   scale=float(D0) ** -0.5).then_inc(exp_done, 1)

        @block.vector
        def _(dve):
            dve.wait_ge(weights, 16 * 8)
            with dve.Fori(0, B) as b:
                dve.wait_ge(mask_loaded, 32 * b + 32)
                dve.wait_ge(pv_done, U * b + 2)
                for dst, src in ((neg, mask), (negT, maskT)):
                    dve.tensor_scalar(dst[:, :, :], src[:, :, :], 0.0, NEG, ALU.is_equal, ALU.mult
                                      ).then_inc(neg_ready, 1)
                for n in range(NG):
                    dve.wait_ge(k_proj, 2 * b + n // 2 + 1)
                    dve.tensor_scalar(kT[:, n, :], ps[:, 0, 2 + n // 2, (n % 2) * S:(n % 2 + 1) * S],
                                      bk[:, n:n + 1], None, ALU.add).then_inc(k_out, 1)
                dve.wait_ge(mt_ready, b)
                for n in range(NG):
                    dve.wait_ge(s_ready, 4 * b + n + 1)
                    dve.tensor_reduce(top_s[:, :, :, n].rearrange("p t g -> p g t"),
                                      ps[:, n % 2, :, :].rearrange("p g (t k) -> p g t k", t=TB),
                                      AX.X, ALU.max).then_inc(max_done, 1)
                for c in range(2):
                    dve.wait_ge(pv_done, U * b + 4 * c + 6)
                    dve.wait_ge(l_ready, 2 * b)
                    dve.tensor_copy(oraw[:, 2 * c:2 * c + 2, :].rearrange("p a n -> p (a n)"), ps[:, 1, c, :]
                                    ).then_inc(o_out, 1)
                for c in range(2):
                    pair = slice(2 * c, 2 * c + 2)
                    dve.wait_ge(l_ready, 2 * b + c + 1)
                    dve.reciprocal(recip[:, pair, :].rearrange("p a n -> p (a n)"), ps[:, 1, 2, :]
                                   ).then_inc(recip_done, 1)
                    dve.wait_ge(recip_done, 2 * b + c + 1)
                    dve.wait_ge(wo_ready, b)
                    dve.tensor_tensor(onorm[:, pair, :], oraw[:, pair, :], recip[:, pair, :], ALU.mult
                                      ).then_inc(norm_done, 1)
                dve.wait_ge(wo_ready, b + 1)
                xs = x[:, bass.ds(b * TB, TB), :]
                dve.tensor_tensor(xs, ps[:, 1, 3, :].rearrange("p (t d) -> p t d", t=TB), xs, ALU.add
                                  ).then_inc(resid_done, 1)


def attention1(nc, top, x, xt, io, consts):
    U, W = H // 2, D1
    TRI = S + P
    with top.stage() as ctx:
        def sb(name, shape, dt=F32):
            return ctx.enter_context(nc.sbuf_tensor("a1_" + name, shape, dt))

        def sem(name):
            return top.semaphore("a1_" + name)

        wq, wk, wv = (sb(n, [P, DK, H * W]) for n in ("wq", "wk", "wv"))
        wo = sb("wo", [P, U, D])
        sel = sb("sel", [W + 1, W])
        ctxT = sb("ctxT", [P, DK, S])
        qT, kT = sb("qT", [W + 1, H, S]), sb("kT", [W + 1, H, S])
        V = sb("V", [P, TB, H, W + 1])
        top_s = sb("top_s", [P, TB, H])
        mT = sb("mT", [H, S])
        pT = sb("pT", [P, 2, 2, TRI])
        oraw = sb("oraw", [W + 1, 2, 2, S])
        recip = sb("recip", [W, 2, S])
        onorm = sb("onorm", [P, U, S])
        ps = ctx.enter_context(nc.psum_tensor("a1_ps", [P, 2, 4, 512], F32))

        (weights, ones_set, ctx_loaded, q_proj, k_proj, v_proj, q_out, k_out, v_out,
         s_ready, max_done, mt_ready, mt_out, mrow_landed, st_ready, exp_done, pv_done, o_out,
         l_ready, recip_done, norm_done, wo_ready, resid_done) = (sem(n) for n in (
             "weights", "ones_set", "ctx_loaded", "q_proj", "k_proj", "v_proj", "q_out", "k_out", "v_out",
             "s_ready", "max_done", "mt_ready", "mt_out", "mrow_landed", "st_ready",
             "exp_done", "pv_done", "o_out", "l_ready", "recip_done", "norm_done", "wo_ready", "resid_done"))
        block = ctx.enter_context(nc.Block())

        @block.sync
        def _(sp):
            for dst, name in ((wq, "a1_wq"), (wk, "a1_wk"), (wv, "a1_wv"), (wo, "a1_wo")):
                sp.dma_start(dst[:, :, :], io[name].rearrange("k p n -> p k n")).then_inc(weights, 16)
            sp.dma_start(sel[:, :], io["a1_sel"]).then_inc(weights, 16)
            with sp.Fori(0, B) as b:
                sp.wait_ge(v_proj, 4 * b)
                sp.dma_start(ctxT[:, :, :], io["ctxT"][bass.ds(b, 1)].rearrange("b (k p) s -> p (b k) s", p=P)
                             ).then_inc(ctx_loaded, 16)
                sp.wait_ge(mt_out, b + 1)
                sp.dma_start(qT[W:W + 1, :, :], mT[:, :]).then_inc(mrow_landed, 16)

        @block.tensor
        def _(pe):
            pe.sem_inc(pv_done, 2)
            pe.wait_ge(weights, 16 * 5)
            with pe.Fori(0, B) as b:
                pe.wait_ge(ctx_loaded, 16 * b + 16)
                pe.wait_ge(exp_done, 8 * b)
                for c in range(U):
                    if c >= 4:
                        pe.wait_ge(q_out, 16 * b + 2 * (c - 3))
                    for k in range(DK):
                        mm = pe.matmul(ps[:, 0, c % 4, 0:S], wq[:, k, c * P:(c + 1) * P],
                                       xt[:, k, bass.ds(b * S, S)], start=(k == 0), stop=(k == DK - 1))
                    mm.then_inc(q_proj, 1)
                    if c == 0:
                        pe.wait_ge(resid_done, b)
                    if c >= 4:
                        pe.wait_ge(k_out, 16 * b + 2 * (c - 3))
                    for k in range(DK):
                        mm = pe.matmul(ps[:, 1, c % 4, 0:S], wk[:, k, c * P:(c + 1) * P],
                                       ctxT[:, k, :], start=(k == 0), stop=(k == DK - 1))
                    mm.then_inc(k_proj, 1)
                pe.wait_ge(q_out, 16 * b + 16)
                for t in range(TB):
                    for f in range(2):
                        for k in range(DK):
                            mm = pe.matmul(ps[:, 0, 2 * t + f, :], ctxT[:, k, t * P:(t + 1) * P],
                                           wv[:, k, f * 512:(f + 1) * 512], start=(k == 0), stop=(k == DK - 1))
                        mm.then_inc(v_proj, 1)
                pe.wait_ge(ones_set, 3)
                for n in range(4):
                    pe.wait_ge(q_out, 16 * b + 16)
                    pe.wait_ge(k_out, 16 * b + 16)
                    if n == 1:
                        pe.wait_ge(v_out, 4 * b + 4)
                    if n >= 2:
                        pe.wait_ge(max_done, 8 * b + 2 * (n - 1))
                    for j in range(4):
                        h = 4 * n + j
                        pe.matmul(ps[:, 1 - n % 2, j, 0:P], qT[0:W, h, 0:P], kT[0:W, h, 0:P], start=True, stop=False)
                        pe.matmul(ps[:, 1 - n % 2, j, 0:P], consts["identb"][:, :], consts["tri"][:, 0, :],
                                  start=False, stop=True)
                        pe.matmul(ps[:, 1 - n % 2, j, P:TRI], qT[0:W, h, P:S], kT[0:W, h, :], start=True, stop=False)
                        mm = pe.matmul(ps[:, 1 - n % 2, j, S:TRI], consts["identb"][:, :], consts["tri"][:, 0, :],
                                       start=False, stop=True)
                    mm.then_inc(s_ready, 1)
                pe.wait_ge(max_done, 8 * b + 8)
                for t in range(TB):
                    mm = pe.transpose(ps[0:H, 1, 2, t * P:(t + 1) * P], top_s[:, t, :], consts["ident"][:, :])
                mm.then_inc(mt_ready, 1)
                pe.wait_ge(mrow_landed, 16 * b + 16)
                for u in range(U + 2):
                    if u < U:
                        if u >= 2:
                            pe.wait_ge(exp_done, 8 * b + u - 1)
                        for j in range(2):
                            h, bank = 2 * u + j, ps[:, 0, 2 * (u % 2) + j, :]
                            pe.matmul(bank[:, 0:S], kT[:, h, 0:P], qT[:, h, :], start=True, stop=False)
                            pe.matmul(bank[:, 0:P], consts["identb"][:, :], consts["tri"][:, 1, :],
                                      start=False, stop=True)
                            pe.matmul(bank[:, S:TRI], kT[:, h, P:S], qT[:, h, P:S], start=True, stop=False)
                            mm = pe.matmul(bank[:, S:TRI], consts["identb"][:, :], consts["tri"][:, 1, :],
                                           start=False, stop=True)
                        mm.then_inc(st_ready, 1)
                    if 1 <= u <= U:
                        m = u - 1
                        pe.wait_ge(exp_done, 8 * b + m + 1)
                        if m >= 2:
                            pe.wait_ge(o_out, 8 * b + m - 1)
                        for j in range(2):
                            h, o = 2 * m + j, ps[0:W + 1, 1, m % 2, j * S:(j + 1) * S]
                            pe.matmul(o, V[:, 0, h, :], pT[:, m % 2, j, 0:S], start=True, stop=False)
                            mm = pe.matmul(o[:, P:S], V[:, 1, h, :], pT[:, m % 2, j, S:TRI],
                                           start=False, stop=True)
                        mm.then_inc(pv_done, 1)
                    if u >= 2:
                        m = u - 2
                        pe.wait_ge(o_out, 8 * b + m + 1)
                        if m >= 1:
                            pe.wait_ge(recip_done, 8 * b + m)
                        pe.matmul(ps[0:W, 1, 2, :], sel[:, :], oraw[:, m % 2, :, :].rearrange("p a n -> p (a n)"),
                                  start=True, stop=True).then_inc(l_ready, 1)
                pe.wait_ge(norm_done, 16 * b + 16)
                for t in range(TB):
                    for c in range(U):
                        mm = pe.matmul(ps[:, 1, 3, t * S:(t + 1) * S], onorm[:, c, t * P:(t + 1) * P], wo[:, c, :],
                                       start=(c == 0), stop=(c == U - 1))
                mm.then_inc(wo_ready, 1)

        @block.scalar
        def _(act):
            with act.Fori(0, B) as b:
                for c in range(U):
                    act.wait_ge(q_proj, 8 * b + c + 1)
                    act.wait_ge(pv_done, 8 * b + 2)
                    for j in range(2):
                        act.activation(qT[0:W, 2 * c + j, :], ps[j * W:(j + 1) * W, 0, c % 4, 0:S], ACT.Copy
                                       ).then_inc(q_out, 1)
                for t in range(TB):
                    for f in range(2):
                        act.wait_ge(v_proj, 4 * b + 2 * t + f + 1)
                        act.activation(V[:, t, 8 * f:8 * f + 8, 0:W],
                                       ps[:, 0, 2 * t + f, :].rearrange("p (h w) -> p h w", w=W), ACT.Copy
                                       ).then_inc(v_out, 1)
                act.wait_ge(mt_ready, b + 1)
                act.wait_ge(mrow_landed, 16 * b)
                act.mul(mT[:, :], ps[0:H, 1, 2, 0:S], -1.0).then_inc(mt_out, 1)
                for u in range(U):
                    act.wait_ge(st_ready, 8 * b + u + 1)
                    act.wait_ge(pv_done, 8 * b + u + 1)
                    act.activation(pT[:, u % 2, :, :], ps[:, 0, 2 * (u % 2):2 * (u % 2) + 2, 0:TRI], ACT.Exp,
                                   scale=float(D1) ** -0.5).then_inc(exp_done, 1)

        @block.vector
        def _(dve):
            dve.memset(V[:, 0, :, W:W + 1], 1.0).then_inc(ones_set, 1)
            dve.memset(V[:, 1, :, W:W + 1], 1.0).then_inc(ones_set, 1)
            dve.memset(kT[W:W + 1, :, :], 1.0).then_inc(ones_set, 1)
            with dve.Fori(0, B) as b:
                for c in range(U):
                    dve.wait_ge(k_proj, 8 * b + c + 1)
                    dve.wait_ge(pv_done, 8 * b + 2)
                    for j in range(2):
                        dve.tensor_copy(kT[0:W, 2 * c + j, :], ps[j * W:(j + 1) * W, 1, c % 4, 0:S]
                                        ).then_inc(k_out, 1)
                dve.wait_ge(mt_ready, b)
                for n in range(4):
                    dve.wait_ge(s_ready, 4 * b + n + 1)
                    dve.tensor_reduce(top_s[:, 0, 4 * n:4 * n + 4], ps[:, 1 - n % 2, :, 0:P], AX.X, ALU.max
                                      ).then_inc(max_done, 1)
                    dve.tensor_reduce(top_s[:, 1, 4 * n:4 * n + 4], ps[:, 1 - n % 2, :, P:TRI], AX.X, ALU.max
                                      ).then_inc(max_done, 1)
                for u in range(U + 1):
                    if u < U:
                        dve.wait_ge(pv_done, 8 * b + u + 3)
                        if u >= 2:
                            dve.wait_ge(norm_done, 16 * b + 2 * (u - 1))
                        dve.tensor_copy(oraw[:, u % 2, :, :].rearrange("p a n -> p (a n)"),
                                        ps[0:W + 1, 1, u % 2, :]).then_inc(o_out, 1)
                    if u > 0:
                        m = u - 1
                        dve.wait_ge(l_ready, 8 * b + m + 1)
                        dve.wait_ge(norm_done, 16 * b + 2 * m)
                        dve.reciprocal(recip[:, :, :].rearrange("p a n -> p (a n)"), ps[0:W, 1, 2, :]
                                       ).then_inc(recip_done, 1)
                        dve.wait_ge(recip_done, 8 * b + m + 1)
                        dve.wait_ge(wo_ready, b)
                        for j in range(2):
                            dve.tensor_tensor(onorm[j * W:(j + 1) * W, m, :], oraw[0:W, m % 2, j, :],
                                              recip[:, j, :], ALU.mult).then_inc(norm_done, 1)
                dve.wait_ge(wo_ready, b + 1)
                xs = x[:, bass.ds(b * TB, TB), :]
                dve.tensor_tensor(xs, ps[:, 1, 3, :].rearrange("p (t d) -> p t d", t=TB), xs, ALU.add
                                  ).then_inc(resid_done, 1)


def chained(engine, sem):
    count = [0]

    def step(ins):
        count[0] += 1
        ins.then_inc(sem, 1)
        engine.wait_ge(sem, count[0])
    return step


def gates0(nc, top, logits, gates, io):
    with top.stage() as ctx:
        def sb(name, shape, dt=F32):
            return ctx.enter_context(nc.sbuf_tensor("g0_" + name, shape, dt))

        bias, rank = sb("bias", [P, E]), sb("rank", [P, E])
        lb, ex, pr, eq = (sb(n, [P, TT, E]) for n in ("lb", "ex", "pr", "eq"))
        m, s, r = (sb(n, [P, TT]) for n in ("m", "s", "r"))
        loaded, chain, shifted, exped = (top.semaphore("g0_" + n) for n in (
            "loaded", "chain", "shifted", "exped"))
        block = ctx.enter_context(nc.Block())

        def over_e(a):
            return a[:, :].unsqueeze(2).to_broadcast([P, TT, E])

        def over_t(a):
            return a[:, :].unsqueeze(1).to_broadcast([P, TT, E])

        @block.sync
        def _(sp):
            sp.dma_start(bias[:, :], io["f0_rb"]).then_inc(loaded, 16)
            sp.dma_start(rank[:, :], io["rank"]).then_inc(loaded, 16)

        @block.scalar
        def _(act):
            act.wait_ge(shifted, 1)
            act.activation(ex[:, :, :], lb[:, :, :], ACT.Exp).then_inc(exped, 1)

        @block.vector
        def _(dve):
            dve.wait_ge(loaded, 32)
            step = chained(dve, chain)
            step(dve.tensor_tensor(lb[:, :, :], logits[:, :, :], over_t(bias), ALU.add))
            step(dve.tensor_reduce(m[:, :], lb[:, :, :], AX.X, ALU.max))
            dve.tensor_tensor(lb[:, :, :], lb[:, :, :], over_e(m), ALU.subtract).then_inc(shifted, 1)
            dve.wait_ge(exped, 1)
            step(dve.tensor_reduce(s[:, :], ex[:, :, :], AX.X, ALU.add))
            step(dve.reciprocal(r[:, :], s[:, :]))
            step(dve.tensor_tensor(pr[:, :, :], ex[:, :, :], over_e(r), ALU.mult))
            step(dve.tensor_reduce(m[:, :], pr[:, :, :], AX.X, ALU.max))
            step(dve.tensor_tensor(eq[:, :, :], pr[:, :, :], over_e(m), ALU.is_equal))
            step(dve.tensor_tensor(eq[:, :, :], eq[:, :, :], over_t(rank), ALU.mult))
            step(dve.tensor_reduce(s[:, :], eq[:, :, :], AX.X, ALU.max))
            step(dve.tensor_tensor(eq[:, :, :], eq[:, :, :], over_e(s), ALU.is_equal))
            step(dve.tensor_tensor(gates[:, :, :], eq[:, :, :], pr[:, :, :], ALU.mult))


def gates1(nc, top, logits, gates, io):
    with top.stage() as ctx:
        def sb(name, shape, dt=F32):
            return ctx.enter_context(nc.sbuf_tensor("g1_" + name, shape, dt))

        rank = sb("rank", [P, E])
        ab, hot1, rest, hot2, t1, t2, ex1, ex2, keep = (
            sb(n, [P, TT, E]) for n in ("ab", "hot1", "rest", "hot2", "t1", "t2", "ex1", "ex2", "keep"))
        m1, m2, s, r1, r2 = (sb(n, [P, TT]) for n in ("m1", "m2", "s", "r1", "r2"))
        loaded, chain, shifted, exped = (top.semaphore("g1_" + n) for n in (
            "loaded", "chain", "shifted", "exped"))
        block = ctx.enter_context(nc.Block())

        def over_e(a):
            return a[:, :].unsqueeze(2).to_broadcast([P, TT, E])

        @block.sync
        def _(sp):
            sp.dma_start(rank[:, :], io["rank"]).then_inc(loaded, 16)

        @block.scalar
        def _(act):
            act.wait_ge(shifted, 1)
            act.activation(ex1[:, :, :], t1[:, :, :], ACT.Exp).then_inc(exped, 1)
            act.activation(ex2[:, :, :], t2[:, :, :], ACT.Exp).then_inc(exped, 1)

        @block.vector
        def _(dve):
            dve.wait_ge(loaded, 16)
            step = chained(dve, chain)

            def first_hot(out, values, largest):
                step(dve.tensor_tensor(out[:, :, :], values[:, :, :], over_e(largest), ALU.is_equal))
                step(dve.tensor_tensor(out[:, :, :], out[:, :, :],
                                       rank[:, :].unsqueeze(1).to_broadcast([P, TT, E]), ALU.mult))
                step(dve.tensor_reduce(s[:, :], out[:, :, :], AX.X, ALU.max))
                step(dve.tensor_tensor(out[:, :, :], out[:, :, :], over_e(s), ALU.is_equal))

            def share(r, m, ex, dropped):
                step(dve.tensor_tensor(keep[:, :, :], ab[:, :, :], over_e(m), ALU.max))
                step(dve.tensor_scalar(keep[:, :, :], keep[:, :, :], 0.02, None, ALU.mult))
                step(dve.tensor_tensor(rest[:, :, :], over_e(m), logits[:, :, :], ALU.subtract))
                step(dve.tensor_tensor(keep[:, :, :], rest[:, :, :], keep[:, :, :], ALU.is_le))
                if dropped is not None:
                    step(dve.tensor_tensor(rest[:, :, :], keep[:, :, :], dropped[:, :, :], ALU.mult))
                    step(dve.tensor_tensor(keep[:, :, :], keep[:, :, :], rest[:, :, :], ALU.subtract))
                step(dve.tensor_tensor(keep[:, :, :], keep[:, :, :], ex[:, :, :], ALU.mult))
                step(dve.tensor_reduce(s[:, :], keep[:, :, :], AX.X, ALU.add))
                step(dve.reciprocal(r[:, :], s[:, :]))

            step(dve.tensor_reduce(m1[:, :], logits[:, :, :], AX.X, ALU.max))
            first_hot(hot1, logits, m1)
            step(dve.scalar_tensor_tensor(out=rest[:, :, :], in0=hot1[:, :, :], scalar=NEG, in1=logits[:, :, :],
                                          op0=ALU.mult, op1=ALU.add))
            step(dve.tensor_reduce(m2[:, :], rest[:, :, :], AX.X, ALU.max))
            first_hot(hot2, rest, m2)
            step(dve.tensor_tensor(t1[:, :, :], logits[:, :, :], over_e(m1), ALU.subtract))
            step(dve.tensor_tensor(t2[:, :, :], logits[:, :, :], over_e(m2), ALU.subtract))
            step(dve.scalar_tensor_tensor(out=ab[:, :, :], in0=logits[:, :, :], scalar=-1.0, in1=logits[:, :, :],
                                          op0=ALU.mult, op1=ALU.max))
            dve.tensor_scalar(t2[:, :, :], t2[:, :, :], 0.0, None, ALU.min).then_inc(shifted, 1)
            dve.wait_ge(exped, 2)
            share(r1, m1, ex1, None)
            share(r2, m2, ex2, hot1)
            step(dve.tensor_tensor(hot1[:, :, :], hot1[:, :, :], over_e(r1), ALU.mult))
            step(dve.tensor_tensor(hot2[:, :, :], hot2[:, :, :], over_e(r2), ALU.mult))
            step(dve.tensor_tensor(gates[:, :, :], hot1[:, :, :], hot2[:, :, :], ALU.add))


def experts(nc, top, tag, x, xt, gates, io, consts, gated):
    NW = 3 if gated else 2
    with top.stage() as ctx:
        def sb(name, shape, dt=F32):
            return ctx.enter_context(nc.sbuf_tensor(tag + name, shape, dt))

        def sem(name):
            return top.semaphore(tag + name)

        w1 = sb("w1", [P, 2, DK, F])
        w3 = sb("w3", [P, 2, DK, F]) if gated else None
        w2 = sb("w2", [P, 2, FT, D])
        b1 = None if gated else sb("b1", [P, E, FT])
        b2 = None if gated else sb("b2", [1, E, D])
        hT = sb("hT", [P, FT, CH])
        act_o = sb("act_o", [P, 2, CH]) if gated else None
        ph = ctx.enter_context(nc.psum_tensor(tag + "ph", [P, 4, CH], F32))
        py = ctx.enter_context(nc.psum_tensor(tag + "py", [P, 2, 2, D], F32))
        (bias_loaded, w_loaded0, w_loaded1, h_ready, silu_done, h_out, y_ready, y_out) = (sem(n) for n in (
            "bias_loaded", "w_loaded0", "w_loaded1", "h_ready", "silu_done", "h_out", "y_ready", "y_out"))
        w_loaded = (w_loaded0, w_loaded1)
        NT = CH // P
        NY = NT // 2
        block = ctx.enter_context(nc.Block())

        @block.sync
        def _(sp):
            if not gated:
                sp.dma_start(b1[:, :, :], io[tag + "b1"]).then_inc(bias_loaded, 16)
                sp.dma_start(b2[:, :, :], io[tag + "b2"]).then_inc(bias_loaded, 16)
            with sp.Fori(0, E // 2) as pair:
                for s in range(2):
                    sp.wait_ge(y_ready, (2 * pair + s + 1) * NCH * NY)
                    e = pair * 2 + s
                    sp.dma_start(w1[:, s, :, :], io[tag + "w1"][bass.ds(e, 1)].rearrange("e (k p) f -> p (e k) f", p=P)
                                 ).then_inc(w_loaded[s], 16)
                    if gated:
                        sp.dma_start(w3[:, s, :, :], io[tag + "w3"][bass.ds(e, 1)].rearrange(
                            "e (k p) f -> p (e k) f", p=P)).then_inc(w_loaded[s], 16)
                    sp.dma_start(w2[:, s, :, :], io[tag + "w2"][bass.ds(e, 1)].rearrange("e (k p) d -> p (e k) d", p=P)
                                 ).then_inc(w_loaded[s], 16)

        @block.tensor
        def _(pe):
            pe.sem_inc(y_ready, 2 * NCH * NY)
            with pe.Fori(0, E // 2) as pair:
                for s in range(2):
                    with pe.Fori(0, NCH) as c:
                        pe.wait_ge(w_loaded[s], 16 * NW * (pair + 1))
                        done = (2 * pair + s) * NCH + c
                        for f in range(FT):
                            if gated:
                                if f >= 2:
                                    pe.wait_ge(h_out, done * FT + f - 1)
                                for w, bank in ((w1, 2 * (f % 2)), (w3, 2 * (f % 2) + 1)):
                                    for k in range(DK):
                                        mm = pe.matmul(ph[:, bank, :], w[:, s, k, f * P:(f + 1) * P],
                                                       xt[:, k, bass.ds(c * CH, CH)], start=(k == 0),
                                                       stop=(k == DK - 1))
                                mm.then_inc(h_ready, 1)
                            else:
                                if f >= 4:
                                    pe.wait_ge(h_out, done * FT + f - 3)
                                for k in range(DK):
                                    mm = pe.matmul(ph[:, f % 4, :], w1[:, s, k, f * P:(f + 1) * P],
                                                   xt[:, k, bass.ds(c * CH, CH)], start=(k == 0),
                                                   stop=(k == DK - 1))
                                mm.then_inc(h_ready, 1)
                        pe.wait_ge(h_out, done * FT + FT)
                        for t in range(NT):
                            if t % 2 == 0:
                                pe.wait_ge(y_out, done * NT + t + 2)
                            for f in range(FT):
                                mm = pe.matmul(py[:, t // 2, t % 2, :], hT[:, f, t * P:(t + 1) * P], w2[:, s, f, :],
                                               start=(f == 0), stop=(gated and f == FT - 1))
                            if not gated:
                                mm = pe.matmul(py[:, t // 2, t % 2, :], consts["ones"][0:1, 0:P],
                                               b2[:, pair * 2 + s, :], start=False, stop=True)
                            if t % 2:
                                mm.then_inc(y_ready, 1)

        @block.scalar
        def _(act):
            if not gated:
                act.wait_ge(bias_loaded, 32)
            with act.Fori(0, E) as e:
                with act.Fori(0, NCH) as c:
                    done = e * NCH + c
                    for f in range(FT):
                        act.wait_ge(h_ready, done * FT + f + 1)
                        if gated:
                            act.wait_ge(h_out, done * FT + max(f - 1, 0))
                            act.activation(act_o[:, f % 2, :], ph[:, 2 * (f % 2), :], ACT.Silu).then_inc(silu_done, 1)
                        else:
                            if f == 0:
                                act.wait_ge(y_ready, (done + 2 * NCH) * NY)
                            act.activation(hT[:, f, :], ph[:, f % 4, :], ACT.Relu,
                                           bias=b1[:, e, f:f + 1]).then_inc(h_out, 1)

        @block.vector
        def _(dve):
            dve.sem_inc(y_out, NT)
            with dve.Fori(0, E) as e:
                with dve.Fori(0, NCH) as c:
                    done = e * NCH + c
                    if gated:
                        for f in range(FT):
                            dve.wait_ge(silu_done, done * FT + f + 1)
                            if f == 0:
                                dve.wait_ge(y_ready, (done + 2 * NCH) * NY)
                            dve.tensor_tensor(hT[:, f, :], ph[:, 2 * (f % 2) + 1, :], act_o[:, f % 2, :], ALU.mult
                                              ).then_inc(h_out, 1)
                    for t in range(NT):
                        dve.wait_ge(y_ready, (done + 2 * NCH) * NY + t // 2 + 1)
                        xs = x[:, c * NT + t, :]
                        dve.scalar_tensor_tensor(out=xs, in0=py[:, t // 2, t % 2, :],
                                                 scalar=gates[:, c * NT + t, bass.ds(e, 1)], in1=xs,
                                                 op0=ALU.mult, op1=ALU.add).then_inc(y_out, 1)


def linear_attention(nc, top, x, xt, io):
    with top.stage() as ctx:
        def sb(name, shape, dt=F32):
            return ctx.enter_context(nc.sbuf_tensor("a2_" + name, shape, dt))

        cx, xb, kv = (sb(n, [P, 2, TB, D]) for n in ("cx", "xb", "kv"))
        pk = ctx.enter_context(nc.psum_tensor("a2_pk", [P, 2, DK, D], F32))
        po = ctx.enter_context(nc.psum_tensor("a2_po", [P, 2, TB, D], F32))
        loaded0, loaded1, copied, kv_ready, kv_out, o_ready, resid_done = (
            top.semaphore("a2_" + n) for n in (
                "loaded0", "loaded1", "copied", "kv_ready", "kv_out", "o_ready", "resid_done"))
        block = ctx.enter_context(nc.Block())

        @block.sync
        def _(sp):
            with sp.Fori(0, B // 2) as pair:
                for s, sem in enumerate((loaded0, loaded1)):
                    sp.wait_ge(kv_ready, 2 * pair + s + 1 - 1)
                    sp.dma_start(cx[:, s, :, :], io["ctx"][bass.ds(pair * 2 + s, 1)].rearrange(
                        "b (t p) d -> p (b t) d", p=P)).then_inc(sem, 16)

        @block.gpsimd
        def _(pool):
            with pool.Fori(0, B // 2) as pair:
                for s in range(2):
                    pool.wait_ge(o_ready, 2 * pair + s + 1)
                    pool.tensor_copy(xb[:, s, :, :], xt[:, :, bass.ds((pair * 2 + s) * S, S)]).then_inc(copied, 1)

        @block.tensor
        def _(pe):
            pe.sem_inc(o_ready, 2)
            pe.sem_inc(kv_ready, 1)
            with pe.Fori(0, B // 2) as pair:
                for s, sem in enumerate((loaded0, loaded1)):
                    b = pair * 2 + s
                    pe.wait_ge(sem, 16 * pair + 16)
                    pe.wait_ge(kv_out, b + 1)
                    for k in range(DK):
                        for t in range(TB):
                            mm = pe.matmul(pk[:, s, k, :], cx[:, s, t, k * P:(k + 1) * P], cx[:, s, t, :],
                                           start=(t == 0), stop=(t == TB - 1))
                    mm.then_inc(kv_ready, 1)
                    pe.wait_ge(kv_out, b + 3)
                    pe.wait_ge(copied, b + 1)
                    pe.wait_ge(resid_done, b + 1)
                    for t in range(TB):
                        for k in range(DK):
                            mm = pe.matmul(po[:, s, t, :], xb[:, s, k, t * P:(t + 1) * P], kv[:, s, k, :],
                                           start=(k == 0), stop=(k == DK - 1))
                    mm.then_inc(o_ready, 1)

        @block.scalar
        def _(act):
            act.sem_inc(kv_out, 2)
            with act.Fori(0, B // 2) as pair:
                for s in range(2):
                    b = pair * 2 + s
                    act.wait_ge(kv_ready, b + 2)
                    act.wait_ge(o_ready, b + 1)
                    act.mul(kv[:, s, :, :], pk[:, s, :, :], 1.0 / S).then_inc(kv_out, 1)

        @block.vector
        def _(dve):
            dve.sem_inc(resid_done, 2)
            with dve.Fori(0, B // 2) as pair:
                for s in range(2):
                    b = pair * 2 + s
                    dve.wait_ge(o_ready, b + 3)
                    xs = x[:, bass.ds(b * TB, TB), :]
                    dve.tensor_tensor(xs, po[:, s, :, :], xs, ALU.add).then_inc(resid_done, 1)


def scaled_linear(nc, top, x, xt, io):
    with top.stage() as ctx:
        def sb(name, shape, dt=F32):
            return ctx.enter_context(nc.sbuf_tensor("f2_" + name, shape, dt))

        cb = sb("cb", [P, DK, D])
        scb, scale, bias = (sb(n, [P, D]) for n in ("scb", "scale", "bias"))
        xb, o1, o2 = (sb(n, [P, 2, TB, D]) for n in ("xb", "o1", "o2"))
        po = ctx.enter_context(nc.psum_tensor("f2_po", [P, 2, TB, D], F32))
        loaded, scaled, copied, o_ready, o1_done, o2_done, resid_done = (
            top.semaphore("f2_" + n) for n in (
                "loaded", "scaled", "copied", "o_ready", "o1_done", "o2_done", "resid_done"))
        block = ctx.enter_context(nc.Block())

        @block.sync
        def _(sp):
            sp.dma_start(cb[:, :, :], io["f2_cb"].rearrange("(k p) n -> p k n", p=P)).then_inc(loaded, 16)
            sp.dma_start(scb[:, :], io["f2_scb"]).then_inc(loaded, 16)
            sp.dma_start(bias[:, :], io["f2_bias"]).then_inc(loaded, 16)

        @block.gpsimd
        def _(pool):
            with pool.Fori(0, B // 2) as pair:
                for s in range(2):
                    pool.wait_ge(o_ready, 2 * pair + s + 1)
                    pool.tensor_copy(xb[:, s, :, :], xt[:, :, bass.ds((pair * 2 + s) * S, S)]).then_inc(copied, 1)

        @block.tensor
        def _(pe):
            pe.sem_inc(o_ready, 2)
            pe.wait_ge(loaded, 48)
            with pe.Fori(0, B // 2) as pair:
                for s in range(2):
                    b = pair * 2 + s
                    pe.wait_ge(copied, b + 1)
                    pe.wait_ge(o1_done, b + 1)
                    for t in range(TB):
                        for k in range(DK):
                            mm = pe.matmul(po[:, s, t, :], xb[:, s, k, t * P:(t + 1) * P], cb[:, k, :],
                                           start=(k == 0), stop=(k == DK - 1))
                    mm.then_inc(o_ready, 1)

        @block.vector
        def _(dve):
            dve.sem_inc(o1_done, 2)
            dve.wait_ge(loaded, 48)
            dve.tensor_scalar(scale[:, :], scb[:, :], 1.0 / 127.0, None, ALU.mult).then_inc(scaled, 1)
            dve.wait_ge(scaled, 1)
            with dve.Fori(0, B // 2) as pair:
                for s in range(2):
                    b = pair * 2 + s
                    dve.wait_ge(o_ready, b + 3)
                    dve.wait_ge(o2_done, b)
                    dve.tensor_tensor(o1[:, s, :, :], po[:, s, :, :],
                                      scale[:, :].unsqueeze(1).to_broadcast([P, TB, D]), ALU.mult).then_inc(o1_done, 1)
                    dve.wait_ge(o1_done, b + 3)
                    dve.wait_ge(resid_done, b)
                    dve.tensor_tensor(o2[:, s, :, :], o1[:, s, :, :],
                                      bias[:, :].unsqueeze(1).to_broadcast([P, TB, D]), ALU.add).then_inc(o2_done, 1)
                    dve.wait_ge(o2_done, b + 1)
                    xs = x[:, bass.ds(b * TB, TB), :]
                    dve.tensor_tensor(xs, o2[:, s, :, :], xs, ALU.add).then_inc(resid_done, 1)


def attention3(nc, top, x, xt, io, consts):
    with top.stage() as ctx:
        def sb(name, shape, dt=F32):
            return ctx.enter_context(nc.sbuf_tensor("a3_" + name, shape, dt))

        wq, wk, wv = (sb(n, [P, DK, D]) for n in ("wq", "wk", "wv"))
        bq, bk = sb("bq", [P, DK]), sb("bk", [P, DK])
        bv = sb("bv", [1, D])
        ctxT = sb("ctxT", [P, DK, S])
        qT, kT = sb("qT", [P, DK, S]), sb("kT", [P, DK, S])
        V = sb("V", [P, TB, D])
        top_s, shift, l, rl = (sb(n, [P, TB]) for n in ("top_s", "shift", "l", "rl"))
        pr, pT = sb("pr", [P, TB, S]), sb("pT", [P, TB, S])
        bank = [ctx.enter_context(nc.psum_tensor(f"a3_{n}", [P, 2, S], F32)) for n in ("q", "k", "v", "s", "t", "o")]
        pq, pk, pv, pS, pt, po = bank
        (weights, ctx_loaded, q_proj, k_proj, v_proj, q_out, k_out, v_out, s_ready, max_done, shift_done,
         exp_done, t_ready, t_out, l_done, o_ready, resid_done) = (
            top.semaphore("a3_" + n) for n in (
                "weights", "ctx_loaded", "q_proj", "k_proj", "v_proj", "q_out", "k_out", "v_out", "s_ready",
                "max_done", "shift_done", "exp_done", "t_ready", "t_out", "l_done", "o_ready", "resid_done"))
        block = ctx.enter_context(nc.Block())

        @block.sync
        def _(sp):
            for dst, name in ((wq, "a3_wq"), (wk, "a3_wk"), (wv, "a3_wv")):
                sp.dma_start(dst[:, :, :], io[name].rearrange("(k p) n -> p k n", p=P)).then_inc(weights, 16)
            for dst, name in ((bq, "a3_bq"), (bk, "a3_bk"), (bv, "a3_bv")):
                sp.dma_start(dst[:, :], io[name]).then_inc(weights, 16)
            with sp.Fori(0, B) as b:
                sp.wait_ge(v_proj, b)
                sp.dma_start(ctxT[:, :, :], io["ctxT"][bass.ds(b, 1)].rearrange("b (k p) s -> p (b k) s", p=P)
                             ).then_inc(ctx_loaded, 16)

        @block.tensor
        def _(pe):
            pe.wait_ge(weights, 16 * 6)
            with pe.Fori(0, B) as b:
                pe.wait_ge(q_out, 2 * b)
                for n in range(DK):
                    for k in range(DK):
                        mm = pe.matmul(pq[:, n, :], wq[:, k, n * P:(n + 1) * P], xt[:, k, bass.ds(b * S, S)],
                                       start=(k == 0), stop=(k == DK - 1))
                mm.then_inc(q_proj, 1)
                pe.wait_ge(ctx_loaded, 16 * b + 16)
                pe.wait_ge(k_out, 2 * b)
                for n in range(DK):
                    for k in range(DK):
                        mm = pe.matmul(pk[:, n, :], wk[:, k, n * P:(n + 1) * P], ctxT[:, k, :],
                                       start=(k == 0), stop=(k == DK - 1))
                mm.then_inc(k_proj, 1)
                pe.wait_ge(v_out, b)
                for t in range(TB):
                    for k in range(DK):
                        pe.matmul(pv[:, t, :], ctxT[:, k, t * P:(t + 1) * P], wv[:, k, :],
                                  start=(k == 0), stop=False)
                    mm = pe.matmul(pv[:, t, :], consts["ones"][0:1, 0:P], bv[:, :], start=False, stop=True)
                mm.then_inc(v_proj, 1)
                pe.wait_ge(q_out, 2 * b + 2)
                pe.wait_ge(k_out, 2 * b + 2)
                pe.wait_ge(exp_done, 2 * b)
                for t in range(TB):
                    for k in range(DK):
                        mm = pe.matmul(pS[:, t, :], qT[:, k, t * P:(t + 1) * P], kT[:, k, :],
                                       start=(k == 0), stop=(k == DK - 1))
                mm.then_inc(s_ready, 1)
                pe.wait_ge(exp_done, 2 * b + 2)
                pe.wait_ge(t_out, b)
                for t in range(TB):
                    for q in range(TB):
                        mm = pe.transpose(pt[:, t, q * P:(q + 1) * P], pr[:, q, t * P:(t + 1) * P],
                                          consts["ident"][:, :])
                mm.then_inc(t_ready, 1)
                pe.wait_ge(t_out, b + 1)
                pe.wait_ge(v_out, b + 1)
                pe.wait_ge(resid_done, 2 * b)
                for q in range(TB):
                    for t in range(TB):
                        mm = pe.matmul(po[:, q, :], pT[:, t, q * P:(q + 1) * P], V[:, t, :],
                                       start=(t == 0), stop=(t == TB - 1))
                mm.then_inc(o_ready, 1)

        @block.scalar
        def _(act):
            act.wait_ge(weights, 16 * 6)
            with act.Fori(0, B) as b:
                act.wait_ge(q_proj, b + 1)
                act.wait_ge(s_ready, b)
                for n in range(DK):
                    act.activation(qT[:, n, :], pq[:, n, :], ACT.Identity, bias=bq[:, n:n + 1]).then_inc(q_out, 1)
                act.wait_ge(v_proj, b + 1)
                act.wait_ge(o_ready, b)
                act.activation(V[:, :, :], pv[:, :, :], ACT.Copy).then_inc(v_out, 1)
                act.wait_ge(shift_done, b + 1)
                act.wait_ge(t_ready, b)
                act.wait_ge(l_done, b)
                for q in range(TB):
                    act.activation(pr[:, q, :], pS[:, q, :], ACT.Exp, bias=shift[:, q:q + 1],
                                   scale=float(D) ** -0.5, accum_out=l[:, q:q + 1]).then_inc(exp_done, 1)

        @block.vector
        def _(dve):
            dve.wait_ge(weights, 16 * 6)
            with dve.Fori(0, B) as b:
                dve.wait_ge(k_proj, b + 1)
                dve.wait_ge(s_ready, b)
                for n in range(DK):
                    dve.tensor_scalar(kT[:, n, :], pk[:, n, :], bk[:, n:n + 1], None, ALU.add).then_inc(k_out, 1)
                dve.wait_ge(s_ready, b + 1)
                dve.tensor_reduce(top_s[:, :], pS[:, :, :], AX.X, ALU.max).then_inc(max_done, 1)
                dve.wait_ge(max_done, b + 1)
                dve.tensor_scalar(shift[:, :], top_s[:, :], -float(D) ** -0.5, None, ALU.mult).then_inc(shift_done, 1)
                dve.wait_ge(exp_done, 2 * b + 2)
                dve.wait_ge(resid_done, 2 * b)
                dve.reciprocal(rl[:, :], l[:, :]).then_inc(l_done, 1)
                dve.wait_ge(t_ready, b + 1)
                dve.wait_ge(o_ready, b)
                dve.tensor_copy(pT[:, :, :], pt[:, :, :]).then_inc(t_out, 1)
                dve.wait_ge(o_ready, b + 1)
                dve.wait_ge(l_done, b + 1)
                for q in range(TB):
                    xs = x[:, b * TB + q, :]
                    dve.scalar_tensor_tensor(out=xs, in0=po[:, q, :], scalar=rl[:, q:q + 1], in1=xs,
                                             op0=ALU.mult, op1=ALU.add).then_inc(resid_done, 1)


def bit_ffn(nc, top, x, ident, io, consts, out):
    with top.stage() as ctx:
        def sb(name, shape, dt=F32):
            return ctx.enter_context(nc.sbuf_tensor("f3_" + name, shape, dt))

        def sem(name):
            return top.semaphore("f3_" + name)

        w1, w1t, w2, w2t = sb("w1", [P, DK * F]), sb("w1t", [P, DK * F]), sb("w2", [P, FT * D]), sb("w2t", [P, FT * D])
        w1q, w2q = sb("w1q", [P, DK, F], BF16), sb("w2q", [P, FT, D], BF16)
        asum, unit, scale = sb("asum", [P, 2]), sb("unit", [P, 2]), sb("scale", [P, 2])
        cw, cb = sb("cw", [P, FT, 3]), sb("cb", [P, FT])
        stats = sb("stats", [P, TT, 6])
        total, diff, m2, mean, diff2, var, vareps, rstd, hi, lo, amax, amaxc, rec, qs, qr, root, guess = (
            sb(n, [P, TT]) for n in ("total", "diff", "m2", "mean", "diff2", "var", "vareps", "rstd", "hi", "lo",
                                     "amax", "amaxc", "rec", "qs", "qr", "root", "guess"))
        xn = sb("xn", [P, TT, D])
        q1, q2 = sb("q1", [P, TB, D]), sb("q2", [P, TB, D])
        xq = sb("xq", [P, TB, D], BF16)
        xqT = sb("xqT", [P, DK, S], BF16)
        rb = sb("rb", [P, TB, P])
        rs = sb("rs", [P, S])
        h = sb("h", [P, FT, S + 2])
        y0, y1, y2, sT = (sb(n, [P, FT, S]) for n in ("y0", "y1", "y2", "sT"))
        shi, slo, sax, saxc, srec, sqs, sqr = (sb(n, [P, TB]) for n in ("shi", "slo", "sax", "saxc", "srec", "sqs", "sqr"))
        s1, s2 = sb("s1", [P, TB, F]), sb("s2", [P, TB, F])
        sq = sb("sq", [P, TB, F], BF16)
        sqT = sb("sqT", [P, FT, S], BF16)
        ptr = ctx.enter_context(nc.psum_tensor("f3_ptr", [P, DK, S], BF16))
        pr = ctx.enter_context(nc.psum_tensor("f3_pr", [P, 512], F32))
        pn = ctx.enter_context(nc.psum_tensor("f3_pn", [P, TB, F], F32))
        pb = pn[:, 0, :].bitcast(BF16).rearrange("p (f n) -> p f n", f=FT)
        ph = pn[:, :, :].rearrange("p t (a n) -> p (t a) n", a=2)
        po = ctx.enter_context(nc.psum_tensor("f3_po", [P, TB, D], F32))
        (loaded, wchain, asum_done, sum_ready, stats_done, comb, normed, chain, q_done, q_sub, rb_done, pads, trans1,
         xqT_out, r_ready, rs_done, h_ready, h_done, y0_done, y1_done, y2_done, silu_done, trans2, red_done,
         s1_done, s2_done, sq_done, trans3, sqT_out, o_ready, resid_done, stored, rooted) = (sem(n) for n in (
             "loaded", "wchain", "asum_done", "sum_ready", "stats_done", "comb", "normed", "chain", "q_done", "q_sub",
             "rb_done", "pads", "trans1", "xqT_out", "r_ready", "rs_done", "h_ready", "h_done", "y0_done", "y1_done",
             "y2_done", "silu_done", "trans2", "red_done", "s1_done", "s2_done", "sq_done", "trans3", "sqT_out",
             "o_ready", "resid_done", "stored", "rooted"))
        block = ctx.enter_context(nc.Block())

        @block.sync
        def _(sp):
            sp.dma_start(w1[:, :].rearrange("p (k f) -> p k f", k=DK), io["f3_w1"].rearrange("(k p) f -> p k f", p=P)
                         ).then_inc(loaded, 16)
            sp.dma_start(w2[:, :].rearrange("p (k d) -> p k d", k=FT), io["f3_w2"].rearrange("(k p) d -> p k d", p=P)
                         ).then_inc(loaded, 16)
            sp.dma_start(cw[:, :, :], io["f3_cw"].rearrange("(t p) k -> p t k", p=P)).then_inc(loaded, 16)
            sp.dma_start(cb[:, :], io["f3_cb"]).then_inc(loaded, 16)
            with sp.Fori(0, B) as b:
                sp.wait_ge(resid_done, 2 * b + 2)
                sp.dma_start(out[bass.ds(b, 1)].rearrange("b (t p) d -> p (b t) d", p=P), x[:, bass.ds(b * TB, TB), :]
                             ).then_inc(stored, 16)
            sp.wait_ge(stored, 16 * B)

        @block.vector
        def _(dve):
            wstep = chained(dve, wchain)
            dve.memset(h[:, :, 0:1], 0.0).then_inc(pads, 1)
            dve.memset(h[:, :, S + 1:S + 2], 0.0).then_inc(pads, 1)
            dve.wait_ge(loaded, 64)
            dve.tensor_reduce(asum[:, 0:1], w1[:, :], AX.X, ALU.add, apply_absolute_value=True).then_inc(asum_done, 1)
            dve.tensor_reduce(asum[:, 1:2], w2[:, :], AX.X, ALU.add, apply_absolute_value=True).then_inc(asum_done, 1)
            dve.wait_ge(sum_ready, 1)
            step = wstep
            step(dve.tensor_scalar(unit[:, :], pr[:, 0:2], 1.0 / (D * F), 1e-5, ALU.mult, ALU.max))
            step(dve.reciprocal(scale[:, :], unit[:, :]))
            for n, (w, wt, wq) in enumerate(((w1, w1t, w1q), (w2, w2t, w2q))):
                step(dve.tensor_scalar(wt[:, :], w[:, :], scale[:, n:n + 1], MAGIC, ALU.mult, ALU.add))
                step(dve.tensor_scalar(w[:, :], wt[:, :], MAGIC, 1.0, ALU.subtract, ALU.min))
                step(dve.tensor_scalar(wq[:, :, :].rearrange("p a b -> p (a b)"), w[:, :], -1.0, None, ALU.max))
            with dve.Fori(0, TT) as t:
                dve.bn_stats(stats[:, t, :], x[:, t, :]).then_inc(stats_done, 1)
            dve.wait_ge(stats_done, TT)
            step = chained(dve, comb)
            step(dve.tensor_tensor(total[:, :], stats[:, :, 1], stats[:, :, 4], ALU.add))
            step(dve.tensor_tensor(diff[:, :], stats[:, :, 1], stats[:, :, 4], ALU.subtract))
            step(dve.tensor_tensor(m2[:, :], stats[:, :, 2], stats[:, :, 5], ALU.add))
            step(dve.tensor_scalar(mean[:, :], total[:, :], 0.5, None, ALU.mult))
            step(dve.tensor_tensor(diff2[:, :], diff[:, :], diff[:, :], ALU.mult))
            step(dve.scalar_tensor_tensor(out=var[:, :], in0=diff2[:, :], scalar=D / 4.0, in1=m2[:, :],
                                          op0=ALU.mult, op1=ALU.add))
            step(dve.tensor_scalar(vareps[:, :], var[:, :], 1.0 / D, EPS, ALU.mult, ALU.add))
            dve.wait_ge(rooted, 1)
            step(dve.reciprocal(guess[:, :], root[:, :]))
            step(dve.tensor_tensor(total[:, :], guess[:, :], guess[:, :], ALU.mult))
            step(dve.tensor_tensor(diff[:, :], total[:, :], vareps[:, :], ALU.mult))
            step(dve.tensor_scalar(total[:, :], diff[:, :], -0.5, 1.5, ALU.mult, ALU.add))
            step(dve.tensor_tensor(rstd[:, :], guess[:, :], total[:, :], ALU.mult))
            with dve.Fori(0, TT) as t:
                dve.tensor_scalar(xn[:, t, :], x[:, t, :], mean[:, bass.ds(t, 1)], rstd[:, bass.ds(t, 1)],
                                  ALU.subtract, ALU.mult).then_inc(normed, 1)
            dve.wait_ge(normed, TT)
            step = chained(dve, chain)
            step(dve.tensor_reduce(amax[:, :], xn[:, :, :], AX.X, ALU.max, apply_absolute_value=True))
            step(dve.tensor_scalar(amaxc[:, :], amax[:, :], 1e-5, None, ALU.max))
            step(dve.reciprocal(rec[:, :], amaxc[:, :]))
            step(dve.tensor_scalar(qs[:, :], rec[:, :], 127.0, None, ALU.mult))
            step(dve.tensor_scalar(qr[:, :], amaxc[:, :], 1.0 / 127.0, None, ALU.mult))
            with dve.Fori(0, B) as b:
                for t in range(TB):
                    dve.wait_ge(q_sub, 2 * b)
                    dve.tensor_scalar(q1[:, t, :], xn[:, b * TB + t, :], qs[:, bass.ds(b * TB + t, 1)], MAGIC,
                                      ALU.mult, ALU.add).then_inc(q_done, 1)
                for t in range(TB):
                    dve.wait_ge(q_done, 4 * b + t + 1)
                    if t == 1:
                        dve.wait_ge(q_done, 4 * b + 3)
                    dve.tensor_scalar(q2[:, t, :], q1[:, t, :], MAGIC + 127.0, MAGIC - 128.0, ALU.min, ALU.max
                                      ).then_inc(q_done, 1)
                for t in range(TB):
                    dve.wait_ge(r_ready, b)
                    dve.tensor_scalar(rb[:, t, :], consts["ones"][:, :], qr[:, bass.ds(b * TB + t, 1)], None, ALU.mult
                                      ).then_inc(rb_done, 1)
                dve.wait_ge(r_ready, b + 1)
                dve.wait_ge(h_done, 8 * b)
                dve.tensor_scalar(rs[:, :], pr[:, 0:S], unit[:, 0:1], None, ALU.mult).then_inc(rs_done, 1)
                dve.wait_ge(rs_done, b + 1)
                for f in range(FT):
                    dve.wait_ge(h_ready, 8 * b + f + 1)
                    dve.wait_ge(y2_done, 8 * b)
                    dve.wait_ge(y0_done, 8 * b)
                    dve.tensor_tensor(h[:, f, 1:S + 1], ph[:, f % 4, 0:S], rs[:, :], ALU.mult).then_inc(h_done, 1)
                dve.wait_ge(silu_done, b)
                dve.wait_ge(pads, 2)
                for f in range(FT):
                    dve.wait_ge(h_done, 8 * b + f + 1)
                    dve.wait_ge(y0_done, 8 * b + f + 1)
                    dve.scalar_tensor_tensor(out=y1[:, f, :], in0=h[:, f, 0:S], scalar=cw[:, f, 0:1], in1=y0[:, f, :],
                                             op0=ALU.mult, op1=ALU.add).then_inc(y1_done, 1)
                for f in range(FT):
                    dve.wait_ge(y1_done, 8 * b + f + 1)
                    dve.scalar_tensor_tensor(out=y2[:, f, :], in0=h[:, f, 2:S + 2], scalar=cw[:, f, 2:3],
                                             in1=y1[:, f, :], op0=ALU.mult, op1=ALU.add).then_inc(y2_done, 1)
                dve.wait_ge(trans2, b + 1)
                dve.wait_ge(resid_done, 2 * b)
                chain_at = 5 * b
                dve.tensor_reduce(sax[:, :], pn[:, :, :], AX.X, ALU.max, apply_absolute_value=True
                                  ).then_inc(red_done, 1)
                dve.wait_ge(red_done, chain_at + 1)
                dve.tensor_scalar(saxc[:, :], sax[:, :], 1e-5, None, ALU.max).then_inc(red_done, 1)
                dve.wait_ge(red_done, chain_at + 2)
                dve.reciprocal(srec[:, :], saxc[:, :]).then_inc(red_done, 1)
                dve.wait_ge(red_done, chain_at + 3)
                dve.tensor_scalar(sqs[:, :], srec[:, :], 127.0, None, ALU.mult).then_inc(red_done, 1)
                dve.tensor_scalar(sqr[:, :], saxc[:, :], 1.0 / 127.0, unit[:, 1:2], ALU.mult, ALU.mult
                                  ).then_inc(red_done, 1)
                dve.wait_ge(red_done, chain_at + 5)
                for t in range(TB):
                    dve.wait_ge(s2_done, 2 * b)
                    dve.tensor_scalar(s1[:, t, :], pn[:, t, :], sqs[:, t:t + 1], MAGIC, ALU.mult, ALU.add
                                      ).then_inc(s1_done, 1)
                for t in range(TB):
                    dve.wait_ge(s1_done, 2 * b + t + 1)
                    dve.wait_ge(sq_done, 2 * b)
                    dve.tensor_scalar(s2[:, t, :], s1[:, t, :], MAGIC + 127.0, MAGIC - 128.0, ALU.min, ALU.max
                                      ).then_inc(s2_done, 1)
                dve.wait_ge(trans3, b + 1)
                dve.wait_ge(o_ready, b)
                dve.tensor_copy(sqT[:, :, :], pb).then_inc(sqT_out, 1)
                for t in range(TB):
                    xs = x[:, b * TB + t, :]
                    dve.wait_ge(o_ready, b + 1)
                    dve.scalar_tensor_tensor(out=xs, in0=po[:, t, :], scalar=sqr[:, t:t + 1], in1=xs,
                                             op0=ALU.mult, op1=ALU.add).then_inc(resid_done, 1)

        @block.scalar
        def _(act):
            act.wait_ge(comb, 7)
            act.activation(root[:, :], vareps[:, :], ACT.Sqrt).then_inc(rooted, 1)
            with act.Fori(0, B) as b:
                act.wait_ge(q_done, 4 * b + 4)
                act.wait_ge(trans1, b)
                act.activation(xq[:, :, :], q2[:, :, :], ACT.Copy, bias=-MAGIC).then_inc(q_sub, 2)
                act.wait_ge(trans1, b + 1)
                act.wait_ge(h_ready, 8 * b)
                act.activation(xqT[:, :, :], ptr[:, :, :], ACT.Copy).then_inc(xqT_out, 1)
                for f in range(FT):
                    act.wait_ge(h_done, 8 * b + f + 1)
                    act.wait_ge(y1_done, 8 * b)
                    act.activation(y0[:, f, :], h[:, f, 1:S + 1], ACT.Identity, bias=cb[:, f:f + 1],
                                   scale=cw[:, f, 1:2]).then_inc(y0_done, 1)
                act.wait_ge(y2_done, 8 * b + 8)
                act.wait_ge(trans2, b)
                act.activation(sT[:, :, :], y2[:, :, :], ACT.Silu).then_inc(silu_done, 1)
                act.wait_ge(s2_done, 2 * b + 2)
                act.wait_ge(trans3, b)
                act.activation(sq[:, :, :], s2[:, :, :], ACT.Copy, bias=-MAGIC).then_inc(sq_done, 2)

        @block.tensor
        def _(pe):
            pe.wait_ge(asum_done, 2)
            pe.matmul(pr[:, 0:2], consts["ones"][:, :], asum[:, :], start=True, stop=True).then_inc(sum_ready, 1)
            pe.wait_ge(wchain, 8)
            with pe.Fori(0, B) as b:
                pe.wait_ge(rb_done, 2 * b + 2)
                pe.wait_ge(rs_done, b)
                for t in range(TB):
                    mm = pe.matmul(pr[:, t * P:(t + 1) * P], rb[:, t, :], ident[:, :], start=True, stop=True)
                mm.then_inc(r_ready, 1)
                pe.wait_ge(q_sub, 2 * b + 2)
                pe.wait_ge(xqT_out, b)
                for k in range(DK):
                    for t in range(TB):
                        mm = pe.transpose(ptr[:, k, t * P:(t + 1) * P], xq[:, t, k * P:(k + 1) * P],
                                          consts["identb"][:, :])
                mm.then_inc(trans1, 1)
                pe.wait_ge(xqT_out, b + 1)
                pe.wait_ge(sqT_out, b)
                for f in range(FT):
                    if f >= 4:
                        pe.wait_ge(h_done, 8 * b + f - 3)
                    for k in range(DK):
                        mm = pe.matmul(ph[:, f % 4, 0:S], w1q[:, k, f * P:(f + 1) * P], xqT[:, k, :],
                                       start=(k == 0), stop=(k == DK - 1))
                    mm.then_inc(h_ready, 1)
                pe.wait_ge(silu_done, b + 1)
                for t in range(TB):
                    for f in range(FT):
                        mm = pe.transpose(pn[:, t, f * P:(f + 1) * P], sT[:, f, t * P:(t + 1) * P], ident[:, :])
                mm.then_inc(trans2, 1)
                pe.wait_ge(sq_done, 2 * b + 2)
                pe.wait_ge(s1_done, 2 * b + 2)
                for f in range(FT):
                    for t in range(TB):
                        mm = pe.transpose(pb[:, f, t * P:(t + 1) * P], sq[:, t, f * P:(f + 1) * P],
                                          consts["identb"][:, :])
                mm.then_inc(trans3, 1)
                pe.wait_ge(sqT_out, b + 1)
                pe.wait_ge(resid_done, 2 * b)
                for t in range(TB):
                    for f in range(FT):
                        mm = pe.matmul(po[:, t, :], sqT[:, f, t * P:(t + 1) * P], w2q[:, f, :],
                                       start=(f == 0), stop=(f == FT - 1))
                mm.then_inc(o_ready, 1)


def build(nc, io, out, sublayers=8, first=0):
    with ExitStack() as top:
        def sb(name, shape, dt=F32):
            return top.enter_context(nc.sbuf_tensor(name, shape, dt))

        x, xt = sb("x", [P, TT, D]), sb("xt", [P, DK, B * S])
        logits, gates = sb("logits", [P, TT, E]), sb("gates", [P, TT, E])
        rw0, rw1 = sb("rw0", [P, DK, E]), sb("rw1", [P, DK, E])
        ident, identb = sb("ident", [P, P]), sb("identb", [P, P], BF16)
        ones = sb("ones", [P, P])
        trif, tri = sb("trif", [P, 2, P]), sb("tri", [P, 2, P], BF16)
        x_loaded, consts_loaded, consts_made = (top.enter_context(nc.semaphore(n)) for n in (
            "x_loaded", "consts_loaded", "consts_made"))
        stages = Stages(nc)
        consts = {"ident": ident, "identb": identb, "ones": ones, "tri": tri}

        with nc.Block() as block:
            @block.sync
            def _(sp):
                sp.dma_start(ident[:, :], io["ident"]).then_inc(consts_loaded, 16)
                sp.dma_start(trif[:, :, :], io["tri"].rearrange("t p n -> p t n")).then_inc(consts_loaded, 16)
                sp.dma_start(rw0[:, :, :], io["f0_rw"].rearrange("(k p) e -> p k e", p=P)).then_inc(consts_loaded, 16)
                sp.dma_start(rw1[:, :, :], io["f1_rw"].rearrange("(k p) e -> p k e", p=P)).then_inc(consts_loaded, 16)
                sp.dma_start(x[:, :, :], io["x"].rearrange("b (t p) d -> p (b t) d", p=P)).then_inc(x_loaded, 16)
                sp.wait_ge(consts_loaded, 64)
                sp.wait_ge(x_loaded, 16)

            @block.vector
            def _(dve):
                dve.memset(ones[:, :], 1.0).then_inc(consts_made, 1)
                dve.wait_ge(consts_loaded, 64)
                dve.tensor_copy(identb[:, :], ident[:, :]).then_inc(consts_made, 1)
                dve.tensor_scalar(tri[:, :, :], trif[:, :, :], NEG, None, ALU.mult).then_inc(consts_made, 1)

        if first <= 0 < sublayers:
            layer_norm(nc, stages, "n0_", x, xt, ident, first=x_loaded)
            attention0(nc, stages, x, xt, io, consts)
        if first <= 1 < sublayers:
            layer_norm(nc, stages, "n1_", x, xt, ident, router=(rw0, logits))
            gates0(nc, stages, logits, gates, io)
            experts(nc, stages, "f0_", x, xt, gates, io, consts, gated=False)
        if first <= 2 < sublayers:
            layer_norm(nc, stages, "n2_", x, xt, ident)
            attention1(nc, stages, x, xt, io, consts)
        if first <= 3 < sublayers:
            layer_norm(nc, stages, "n3_", x, xt, ident, router=(rw1, logits))
            gates1(nc, stages, logits, gates, io)
            experts(nc, stages, "f1_", x, xt, gates, io, consts, gated=True)
        if first <= 4 < sublayers:
            layer_norm(nc, stages, "n4_", x, xt, ident)
            linear_attention(nc, stages, x, xt, io)
        if first <= 5 < sublayers:
            layer_norm(nc, stages, "n5_", x, xt, ident)
            scaled_linear(nc, stages, x, xt, io)
        if first <= 6 < sublayers:
            layer_norm(nc, stages, "n6_", x, xt, ident)
            attention3(nc, stages, x, xt, io, consts)
        if sublayers > 7:
            bit_ffn(nc, stages, x, ident, io, consts, out)
        else:
            stored = top.enter_context(nc.semaphore("stored"))
            with nc.Block() as block:
                @block.sync
                def _(sp):
                    sp.dma_start(out.rearrange("b (t p) d -> p (b t) d", p=P), x[:, :, :]).then_inc(stored, 16)
                    sp.wait_ge(stored, 16)


def lay_out(i):
    import numpy as np

    def t(a):
        return np.ascontiguousarray(np.swapaxes(a, -1, -2))

    def rows(a):
        return np.ascontiguousarray(np.broadcast_to(a, (P, a.shape[0])))

    def padded(a):
        out = np.zeros(a.shape[:-1] + (H, 32), np.float32)
        out[..., :D0] = a.reshape(a.shape[:-1] + (H, D0))
        return out

    f = {k: np.asarray(v) for k, v in i.items()}
    io = {"x": f["x"], "ctx": f["ctx_1024"], "ctxT": t(f["ctx_1024"]),
          "mask": f["mask_BxSxS2_ik1"], "maskT": t(f["mask_BxSxS2_ik1"])}
    for n in "qkv":
        io["a0_w" + n] = padded(t(f["L0_xattn_W" + n])).reshape(DK, P, H * 32)
    for n, extra in (("q", 0.0), ("k", 1.0)):
        b = padded(f["L0_xattn_b" + n])
        b[:, D0] = extra
        io["a0_b" + n] = t(b.reshape(H * 32 // P, P))
    b = padded(f["L0_xattn_bv"])
    b[:, D0] = 1.0
    io["a0_bv"] = b.reshape(1, H * 32)
    wo = padded(f["L0_xattn_Wo"])
    wo[:, 0, D0] = f["L0_xattn_bo"]
    io["a0_wo"] = t(wo.reshape(D, H * 32)).reshape(H * 32 // P, P, D)
    sel = np.zeros((4, 32, 4, 32), np.float32)
    for g in range(4):
        sel[g, D0, g, :] = 1.0
    io["a0_sel"] = sel.reshape(P, P)
    for n in "qkv":
        io["a1_w" + n] = t(f["L1_xattn_w_" + n]).reshape(DK, P, H * D1)
    io["a1_wo"] = t(f["L1_xattn_w_o"]).reshape(H * D1 // P, P, D)
    sel = np.zeros((D1 + 1, D1), np.float32)
    sel[D1] = 1.0
    io["a1_sel"] = sel
    io["ident"] = np.eye(P, dtype=np.float32)
    io["tri"] = np.stack([np.triu(np.ones((P, P), np.float32), 1), np.tril(np.ones((P, P), np.float32), -1)])
    io["rank"] = rows(np.arange(E, 0, -1).astype(np.float32))
    io["f0_rw"], io["f0_rb"] = f["L0_ffn_router_W"], rows(f["L0_ffn_router_b"])
    io["f0_w1"], io["f0_b1"] = f["L0_ffn_W1"], f["L0_ffn_b1"].reshape(E, FT, P).transpose(2, 0, 1)
    io["f0_w2"], io["f0_b2"] = f["L0_ffn_W2"], f["L0_ffn_b2"][None]
    io["f1_rw"] = t(f["L1_ffn_gate_w"])
    io["f1_w1"], io["f1_w3"], io["f1_w2"] = t(f["L1_ffn_w1"]), t(f["L1_ffn_w3"]), t(f["L1_ffn_w2"])
    io["f2_cb"], io["f2_scb"], io["f2_bias"] = t(f["L2_ffn_CB"]), rows(f["L2_ffn_SCB"]), rows(f["L2_ffn_bias"])
    for n in "qkv":
        io["a3_w" + n] = t(f["L3_xattn_W" + n])
    io["a3_bq"], io["a3_bk"] = (t(f["L3_xattn_b" + n].reshape(DK, P)) for n in "qk")
    io["a3_bv"] = f["L3_xattn_bv"][None]
    io["f3_w1"], io["f3_w2"] = t(f["L3_ffn_w1"]), t(f["L3_ffn_w2"])
    io["f3_cw"], io["f3_cb"] = f["L3_ffn_conv_w"].reshape(F, 3), t(f["L3_ffn_conv_b"].reshape(FT, P))
    return {k: np.ascontiguousarray(v) for k, v in io.items()}


def kernel(**inputs):
    import concourse.bacc as bacc
    from concourse.bass_utils import run_bass_kernel_spmd

    nc = bacc.Bacc("TRN2", target_bir_lowering=False, num_devices=1)
    arrays = lay_out(inputs)
    io = {k: nc.dram_tensor("in_" + k, v.shape, mybir.dt.from_np(v.dtype), kind="ExternalInput").ap()
          for k, v in arrays.items()}
    out = nc.dram_tensor("out", (B, S, D), F32, kind="ExternalOutput").ap()
    build(nc, io, out)
    r = run_bass_kernel_spmd(nc, [{"in_" + k: v for k, v in arrays.items()}], core_ids=[0])
    return r.results[0]["out"]
```

```python
from contextlib import ExitStack, contextmanager

import concourse.bass as bass
from concourse import mybir

F32 = mybir.dt.float32
BF16 = mybir.dt.bfloat16
I32 = mybir.dt.int32
U32 = mybir.dt.uint32
ALU = mybir.AluOpType
ACT = mybir.ActivationFunctionType
AX = mybir.AxisListType

P = 128
B, S, D = 8, 256, 256
DK = D // P
TT = B * S // P
TB = S // P
H = 16
D0, D1 = D // H, 64
E, F = 8, 1024
FT = F // P
EPS = 1e-5
NEG = -float(2 ** 100)
MAGIC = 1.5 * 2 ** 23


class Stages:

    def __init__(self, nc):
        self.nc, self.ours, self.cleared = nc, [], []

    def for_indirect(self, name):
        return self.nc.alloc_semaphore(name=name)

    def semaphore(self, name):
        self.ours.append(self.nc.alloc_semaphore(name=name))
        return self.ours[-1]

    @contextmanager
    def stage(self):
        with ExitStack() as ctx:
            yield ctx
        for s in self.cleared:
            self.nc.release_semaphore(s)
        for s in self.ours:
            self.nc.gpsimd.sem_clear(s)
        self.cleared, self.ours = self.ours, []


def layer_norm(nc, top, tag, x, xt, ident, first=None, router=None):
    with top.stage() as ctx:
        def sb(name, shape, dt=F32):
            return ctx.enter_context(nc.sbuf_tensor(tag + name, shape, dt))

        def sem(name):
            return top.semaphore(tag + name)

        stats = sb("stats", [P, TT, 6])
        total, diff, m2, mean, diff2, var, vareps, rstd, root, guess = (
            sb(n, [P, TT]) for n in ("total", "diff", "m2", "mean", "diff2", "var", "vareps", "rstd", "root", "guess"))
        xn = sb("xn", [P, TB, D])
        xs = sb("xs", [P, TB, DK, P]) if router else None
        tp = ctx.enter_context(nc.psum_tensor(tag + "tp", [P, TB, 512], F32))
        lg = ctx.enter_context(nc.psum_tensor(tag + "lg", [P, TB, 512], F32)) if router else None
        stats_done, comb, normed, transposed, evacuated, kept, logits_done, logits_out, rooted = (
            sem(n) for n in ("stats_done", "comb", "normed", "transposed", "evacuated", "kept",
                             "logits_done", "logits_out", "rooted"))
        block = ctx.enter_context(nc.Block())

        @block.vector
        def _(dve):
            if first:
                dve.wait_ge(first, 16)
            with dve.Fori(0, TT) as t:
                dve.bn_stats(stats[:, t, :], x[:, t, :]).then_inc(stats_done, 1)
            dve.wait_ge(stats_done, TT)
            dve.tensor_tensor(total[:, :], stats[:, :, 1], stats[:, :, 4], ALU.add).then_inc(comb, 1)
            dve.tensor_tensor(diff[:, :], stats[:, :, 1], stats[:, :, 4], ALU.subtract).then_inc(comb, 1)
            dve.tensor_tensor(m2[:, :], stats[:, :, 2], stats[:, :, 5], ALU.add).then_inc(comb, 1)
            dve.wait_ge(comb, 3)
            dve.tensor_scalar(mean[:, :], total[:, :], 0.5, None, ALU.mult).then_inc(comb, 1)
            dve.tensor_tensor(diff2[:, :], diff[:, :], diff[:, :], ALU.mult).then_inc(comb, 1)
            dve.wait_ge(comb, 5)
            dve.scalar_tensor_tensor(out=var[:, :], in0=diff2[:, :], scalar=D / 4.0, in1=m2[:, :],
                                     op0=ALU.mult, op1=ALU.add).then_inc(comb, 1)
            dve.wait_ge(comb, 6)
            dve.tensor_scalar(vareps[:, :], var[:, :], 1.0 / D, EPS, ALU.mult, ALU.add).then_inc(comb, 1)
            dve.wait_ge(comb, 7)
            dve.wait_ge(rooted, 1)
            dve.reciprocal(guess[:, :], root[:, :]).then_inc(comb, 1)
            dve.wait_ge(comb, 8)
            dve.tensor_tensor(total[:, :], guess[:, :], guess[:, :], ALU.mult).then_inc(comb, 1)
            dve.wait_ge(comb, 9)
            dve.tensor_tensor(diff[:, :], total[:, :], vareps[:, :], ALU.mult).then_inc(comb, 1)
            dve.wait_ge(comb, 10)
            dve.tensor_scalar(total[:, :], diff[:, :], -0.5, 1.5, ALU.mult, ALU.add).then_inc(comb, 1)
            dve.wait_ge(comb, 11)
            dve.tensor_tensor(rstd[:, :], guess[:, :], total[:, :], ALU.mult).then_inc(comb, 1)
            dve.wait_ge(comb, 12)
            with dve.Fori(0, B) as b:
                for j in range(TB):
                    dve.wait_ge(transposed, b * TB + j + 1)
                    if router:
                        dve.wait_ge(kept, b * TB + j + 1)
                    dve.tensor_scalar(xn[:, j, :], x[:, b * TB + j, :], mean[:, bass.ds(b * TB + j, 1)],
                                      rstd[:, bass.ds(b * TB + j, 1)], ALU.subtract, ALU.mult).then_inc(normed, 1)

        if router:
            @block.gpsimd
            def _(pool):
                pool.sem_inc(kept, TB)
                with pool.Fori(0, B) as b:
                    for j in range(TB):
                        pool.wait_ge(normed, b * TB + j + 1)
                        pool.tensor_copy(router[2][:, b * TB + j, :], xn[:, j, :]).then_inc(kept, 1)

        @block.tensor
        def _(pe):
            pe.sem_inc(transposed, TB)
            if router:
                pe.sem_inc(logits_done, TB)
            with pe.Fori(0, B) as b:
                for j in range(TB):
                    pe.wait_ge(normed, b * TB + j + 1)
                    pe.wait_ge(evacuated, b * TB + j + 1)
                    for k in range(DK):
                        mm = pe.transpose(tp[:, j, k * P:(k + 1) * P], xn[:, j, k * P:(k + 1) * P], ident[:, :])
                    mm.then_inc(transposed, 1)
                if router:
                    for j in range(TB):
                        pe.wait_ge(evacuated, b * TB + j + TB + 1)
                        pe.wait_ge(logits_out, b * TB + j + 1)
                        for k in range(DK):
                            mm = pe.matmul(lg[:, j, 0:E], xs[:, j, k, :], router[0][:, k, :],
                                           start=(k == 0), stop=(k == DK - 1))
                        mm.then_inc(logits_done, 1)

        @block.scalar
        def _(act):
            act.sem_inc(evacuated, TB)
            if router:
                act.sem_inc(logits_out, TB)
            act.wait_ge(comb, 7)
            act.activation(root[:, :], vareps[:, :], ACT.Sqrt).then_inc(rooted, 1)
            with act.Fori(0, B) as b:
                for j in range(TB):
                    act.wait_ge(transposed, b * TB + j + TB + 1)
                    if router:
                        act.wait_ge(logits_done, b * TB + j + 1)
                    act.activation(xs[:, j, :, :] if router else xt[:, :, bass.ds((b * TB + j) * P, P)],
                                   tp[:, j, 0:D].rearrange("p (k n) -> p k n", k=DK), ACT.Copy).then_inc(evacuated, 1)
                if router:
                    for j in range(TB):
                        act.wait_ge(logits_done, b * TB + j + TB + 1)
                        act.activation(router[1][:, b * TB + j, :], lg[:, j, 0:E], ACT.Copy).then_inc(logits_out, 1)


def attention0(nc, top, x, xt, io, consts):
    G, NG, W = 4, H // 4, 32
    U = H // 2
    PARTS = ((0, 0, 0, 1, 1, 2), (0, 1, 2, 0, 1, 0))
    R = len(PARTS[0]) * D0
    LAND = 16 * 2 * len(PARTS[0])
    HB = P // D0
    with top.stage() as ctx:
        def sb(name, shape, dt=F32):
            return ctx.enter_context(nc.sbuf_tensor("a0_" + name, shape, dt))

        wq, wk, wv = (sb(n, [P, DK, D]) for n in ("wq", "wk", "wv"))
        wo = sb("wo", [P, NG, D])
        bqk = sb("bqk", [P, 2, DK])
        bv = sb("bv", [P, D])
        sel = sb("sel", [P, P])
        ctxT = sb("ctxT", [P, 2, DK, S])
        mask, maskT = sb("mask", [P, TB, S], I32), sb("maskT", [P, TB, S], I32)
        neg, negT = sb("neg", [P, 2, TB, S], BF16), sb("negT", [P, 2, TB, S], BF16)
        part = sb("part", [P, 3, 2, DK, S], BF16)
        rest = sb("rest", [P, 2, DK, S])
        qs, ks = sb("qs", [P, 2, H, S], BF16), sb("ks", [P, 2, H, S], BF16)
        V = sb("V", [P, 2, TB, H, W])
        top_s = sb("top_s", [P, TB, H])
        mpart, mrest = sb("mpart", [H, 3, S], BF16), sb("mrest", [H, S])
        pT = sb("pT", [P, 2, 2, TB, S])
        recip = sb("recip", [P, 2, 512])
        oraw, onorm = sb("oraw", [P, NG, S]), sb("onorm", [P, NG, S])
        ps = ctx.enter_context(nc.psum_tensor("a0_ps", [P, 8, 512], F32))
        O = ps[:, 4:6, :].rearrange("p a (c n) -> p (a c) n", c=2)

        (weights, ctx_in0, ctx_in1, mask_in, ones_set, q_proj, k_proj, v_proj, hi_done, rest_done, mid_done, lo_done,
         stacked, v_out, neg_ready, s_ready, max_done, mt_ready, mhi_done, mrest_done, mmid_done, mlo_done,
         mrow_landed, st_ready, exp_done, pv_done, o_out, l_ready, recip_done, norm_done, wo_ready, resid_done) = (
             top.semaphore("a0_" + n) for n in (
                 "weights", "ctx_in0", "ctx_in1", "mask_in", "ones_set", "q_proj", "k_proj", "v_proj", "hi_done",
                 "rest_done", "mid_done", "lo_done", "stacked", "v_out", "neg_ready", "s_ready", "max_done",
                 "mt_ready", "mhi_done", "mrest_done", "mmid_done", "mlo_done", "mrow_landed", "st_ready",
                 "exp_done", "pv_done", "o_out", "l_ready", "recip_done", "norm_done", "wo_ready", "resid_done"))
        ctx_in = (ctx_in0, ctx_in1)
        block = ctx.enter_context(nc.Block())

        def every_batch(engine, body):
            with engine.Fori(0, B // 2 - 1) as pair:
                body(pair * 2, 0, pair, False)
                body(pair * 2 + 1, 1, pair, False)
            body(B - 2, 0, B // 2 - 1, False)
            body(B - 1, 1, B // 2 - 1, True)

        @block.sync
        def _(sp):
            sp.sem_inc(stacked, 16)
            sp.sem_inc(mrow_landed, 16)

            def load(b, s):
                sp.wait_ge(v_proj, b + 1)
                sp.dma_start(ctxT[:, s, :, :], io["ctxT"][bass.ds(b, 1)].rearrange("b (k p) s -> p (b k) s", p=P)
                             ).then_inc(ctx_in[s], 16)
                sp.wait_ge(neg_ready, b + 1)
                sp.dma_start(mask[:, :, :], io["mask"][bass.ds(b, 1)].rearrange("b (t p) s -> p (b t) s", p=P)
                             ).then_inc(mask_in, 16)
                sp.dma_start(maskT[:, :, :], io["maskT"][bass.ds(b, 1)].rearrange("b (t p) s -> p (b t) s", p=P)
                             ).then_inc(mask_in, 16)

            def stack(b, s):
                for n, ready in enumerate((hi_done, mid_done, lo_done)):
                    for w, dst in enumerate((qs, ks)):
                        sp.wait_ge(ready, b * 2 + (w + 1))
                        for t, which in enumerate(PARTS[w]):
                            if which == n:
                                for k in range(DK):
                                    sp.dma_start(dst[t * D0:(t + 1) * D0, s, k * HB:(k + 1) * HB, :],
                                                 part[:, n, w, k, :]
                                                 ).then_inc(stacked, 8 * 2)

            def shift_rows(b, s):
                sp.wait_ge(mlo_done, b + 1)
                for n in range(3):
                    sp.dma_start(qs[R + n:R + n + 1, s, :, :], mpart[:, n, :]).then_inc(mrow_landed, 16)

            def feed(b, s, half, last):
                if not last:
                    sp.wait_ge(pv_done, b * U + 2)
                    stack(b + 1, 1 - s)
                    shift_rows(b + 1, 1 - s)

            for dst, name in ((wq, "a0_wq"), (wk, "a0_wk"), (wv, "a0_wv"), (wo, "a0_wo")):
                sp.dma_start(dst[:, :, :], io[name].rearrange("k p n -> p k n")).then_inc(weights, 16)
            sp.dma_start(bqk[:, :, :], io["a0_bqk"]).then_inc(weights, 16)
            for dst, name in ((bv, "a0_bv"), (sel, "a0_sel")):
                sp.dma_start(dst[:, :], io[name]).then_inc(weights, 16)
            load(0, 0)
            load(1, 1)
            stack(0, 0)
            shift_rows(0, 0)
            with sp.Fori(0, B // 2 - 1) as pair:
                for s in range(2):
                    load(pair * 2 + (2 + s), s)
                    feed(pair * 2 + s, s, pair, False)
            feed(B - 2, 0, 0, False)

        @block.tensor
        def _(pe):
            pe.sem_inc(v_proj, 2)
            pe.sem_inc(pv_done, 2)
            pe.sem_inc(l_ready, 1)
            pe.sem_inc(wo_ready, 1)
            pe.wait_ge(weights, 16 * 7)

            def project(b, s, half, left=1):
                pe.wait_ge(ctx_in[s], half * 16 + 16)
                pe.wait_ge(norm_done, left)
                for n, (w, src, done) in enumerate(((wq, xt, q_proj), (wk, ctxT, k_proj))):
                    for c in range(DK):
                        for k in range(DK):
                            mm = pe.matmul(ps[:, 6 + n, c * S:(c + 1) * S], w[:, k, c * P:(c + 1) * P],
                                           xt[:, k, bass.ds(b * S, S)] if src is xt else ctxT[:, s, k, :],
                                           start=(k == 0), stop=(k == DK - 1))
                    mm.then_inc(done, 1)
                pe.wait_ge(rest_done, b * 2 + 1)
                for t in range(TB):
                    for k in range(DK):
                        mm = pe.matmul(ps[:, 6, t * S:(t + 1) * S], ctxT[:, s, k, t * P:(t + 1) * P], wv[:, k, :],
                                       start=(k == 0), stop=(k == DK - 1))
                mm.then_inc(v_proj, 1)

            def scores(b, s, before):
                pe.wait_ge(stacked, (b + 1) * LAND * 2 + 16)
                pe.wait_ge(neg_ready, b + 2)
                pe.wait_ge(ones_set, 4)
                for u in range(U):
                    if u >= 2:
                        pe.wait_ge(max_done, b * U + (u - 1))
                    elif before is not None:
                        pe.wait_ge(exp_done, before * U + (U - 1 + u))
                    for j in range(2):
                        h, bank = 2 * u + j, ps[:, 2 * (u % 2) + j, :]
                        for t in range(TB):
                            pe.matmul(bank[:, t * S:(t + 1) * S], qs[0:R, s, h, t * P:(t + 1) * P], ks[0:R, s, h, :],
                                      start=True, stop=False)
                            mm = pe.matmul(bank[:, t * S:(t + 1) * S], consts["identb"][:, :], neg[:, s, t, :],
                                           start=False, stop=True)
                    mm.then_inc(s_ready, 1)

            def turn_maxima(b):
                pe.wait_ge(max_done, b * U + U)
                for t in range(TB):
                    mm = pe.transpose(ps[0:H, 4, t * P:(t + 1) * P], top_s[:, t, :], consts["ident"][:, :])
                mm.then_inc(mt_ready, 1)

            def weigh(b, s):
                pe.wait_ge(mrow_landed, (b + 1) * 48 + 16)
                pe.wait_ge(v_out, b + 1)
                for u in range(U + 1):
                    if u < U:
                        if u >= 2:
                            pe.wait_ge(exp_done, b * U + (u - 1))
                        else:
                            pe.wait_ge(max_done, b * U + (U - 1 + u))
                        for j in range(2):
                            h, bank = 2 * u + j, ps[:, 2 * (u % 2) + j, :]
                            for t in range(TB):
                                pe.matmul(bank[:, t * S:(t + 1) * S], ks[0:R + 3, s, h, t * P:(t + 1) * P],
                                          qs[0:R + 3, s, h, :], start=True, stop=False)
                                mm = pe.matmul(bank[:, t * S:(t + 1) * S], consts["identb"][:, :], negT[:, s, t, :],
                                               start=False, stop=True)
                        mm.then_inc(st_ready, 1)
                    if u > 0:
                        m = u - 1
                        n, g0 = m // 2, 2 * (m % 2)
                        pe.wait_ge(exp_done, b * U + (m + 1))
                        if m == U // 2:
                            pe.wait_ge(resid_done, b + 1)
                        for j in range(2):
                            for t in range(TB):
                                mm = pe.matmul(O[W * (g0 + j):W * (g0 + j + 1), n, :], V[:, s, t, 4 * n + g0 + j, :],
                                               pT[:, m % 2, j, t, :], start=(t == 0), stop=(t == TB - 1))
                        mm.then_inc(pv_done, 1)

            def spread_sums(b):
                for c in range(2):
                    pe.wait_ge(o_out, b * 2 + (c + 1))
                    pe.matmul(ps[:, 6 + c, :], sel[:, :], oraw[:, 2 * c:2 * c + 2, :].rearrange("p a n -> p (a n)"),
                              start=True, stop=True).then_inc(l_ready, 1)

            def output(b):
                pe.wait_ge(norm_done, b * 2 + 3)
                for t in range(TB):
                    for n in range(NG):
                        mm = pe.matmul(ps[:, 5, t * S:(t + 1) * S], onorm[:, n, t * P:(t + 1) * P], wo[:, n, :],
                                       start=(n == 0), stop=(n == NG - 1))
                mm.then_inc(wo_ready, 1)

            def batch(b, s, half, last):
                if not last:
                    project(b + 1, 1 - s, half + s, b * 2 + 1)
                weigh(b, s)
                if not last:
                    scores(b + 1, 1 - s, b)
                pe.wait_ge(v_out, b + 1 if last else b + 2)
                pe.wait_ge(lo_done, b * 2 + 2 if last else b * 2 + 4)
                spread_sums(b)
                if not last:
                    turn_maxima(b + 1)
                output(b)

            project(0, 0, 0)
            scores(0, 0, None)
            turn_maxima(0)
            every_batch(pe, batch)

        @block.scalar
        def _(act):
            act.wait_ge(weights, 16 * 7)

            def split(b):
                act.wait_ge(stacked, b * (LAND * 2) + 16)
                for n, done in enumerate((q_proj, k_proj)):
                    act.wait_ge(done, b + 1)
                    for c in range(DK):
                        a = act.activation(part[:, 0, n, c, :], ps[:, 6 + n, c * S:(c + 1) * S], ACT.Identity,
                                           bias=bqk[:, n, c:c + 1])
                    a.then_inc(hi_done, 1)
                for n in range(2):
                    act.wait_ge(rest_done, b * 2 + (n + 1))
                    act.activation(part[:, 1, n, :, :], rest[:, n, :, :], ACT.Copy).then_inc(mid_done, 1)

            def split_maxima(b):
                act.wait_ge(mt_ready, b + 1)
                act.wait_ge(mrow_landed, b * 48 + 16)
                act.mul(mpart[:, 0, :], ps[0:H, 4, 0:S], -1.0).then_inc(mhi_done, 1)
                act.wait_ge(mrest_done, b + 1)
                act.activation(mpart[:, 1, :], mrest[:, :], ACT.Copy).then_inc(mmid_done, 1)

            def batch(b, s, half, last):
                if not last:
                    split(b + 1)
                for u in range(U):
                    act.wait_ge(st_ready, b * U + (u + 1))
                    act.wait_ge(pv_done, b * U + (u + 1))
                    act.activation(pT[:, u % 2, :, :, :].rearrange("p j t n -> p j (t n)"),
                                   ps[:, 2 * (u % 2):2 * (u % 2) + 2, :], ACT.Exp,
                                   scale=float(D0) ** -0.5).then_inc(exp_done, 1)
                if not last:
                    split_maxima(b + 1)

            split(0)
            split_maxima(0)
            every_batch(act, batch)

        @block.vector
        def _(dve):
            dve.sem_inc(neg_ready, 1)
            dve.sem_inc(norm_done, 1)
            dve.sem_inc(resid_done, 1)
            for s in range(2):
                dve.memset(V[:, s, :, :, :], 0.0).then_inc(ones_set, 1)
            dve.memset(ks[R:P, :, :, :], 1.0).then_inc(ones_set, 1)
            dve.wait_ge(ones_set, 3)
            dve.memset(V[:, :, :, :, D0:D0 + 1].rearrange("p s t h w -> p (s t) h w"), 1.0).then_inc(ones_set, 1)
            dve.wait_ge(weights, 16 * 7)

            def prepare(b, s, half):
                dve.wait_ge(mask_in, b * 32 + 32)
                dve.tensor_scalar(neg[:, s, :, :], mask[:, :, :], 0.0, NEG, ALU.is_equal, ALU.mult)
                dve.tensor_scalar(negT[:, s, :, :], maskT[:, :, :], 0.0, NEG, ALU.is_equal, ALU.mult
                                  ).then_inc(neg_ready, 1)
                for n in range(2):
                    dve.wait_ge(hi_done, b * 2 + (n + 1))
                    for c in range(DK):
                        a = dve.scalar_tensor_tensor(out=rest[:, n, c, :], in0=ps[:, 6 + n, c * S:(c + 1) * S],
                                                     scalar=bqk[:, n, c:c + 1], in1=part[:, 0, n, c, :],
                                                     op0=ALU.add, op1=ALU.subtract)
                    a.then_inc(rest_done, 1)
                for n in range(2):
                    dve.wait_ge(mid_done, b * 2 + (n + 1))
                    dve.tensor_tensor(part[:, 2, n, :, :], rest[:, n, :, :], part[:, 1, n, :, :], ALU.subtract
                                      ).then_inc(lo_done, 1)
                dve.wait_ge(v_proj, b + 3)
                dve.wait_ge(ones_set, 4)
                dve.tensor_tensor(V[:, s, :, :, 0:D0], ps[:, 6, :].rearrange("p (t h w) -> p t h w", t=TB, h=H),
                                  bv[:, :].rearrange("p (h w) -> p h w", h=H).unsqueeze(1).to_broadcast([P, TB, H, D0]),
                                  ALU.add).then_inc(v_out, 1)

            def maxima(b):
                for u in range(U):
                    dve.wait_ge(s_ready, b * U + (u + 1))
                    dve.tensor_reduce(top_s[:, :, 2 * u:2 * u + 2].rearrange("p t j -> p j t"),
                                      ps[:, 2 * (u % 2):2 * (u % 2) + 2, :].rearrange("p j (t k) -> p j t k", t=TB),
                                      AX.X, ALU.max).then_inc(max_done, 1)

            def split_maxima(b):
                dve.wait_ge(mhi_done, b + 1)
                dve.scalar_tensor_tensor(out=mrest[:, :], in0=ps[0:H, 4, 0:S], scalar=-1.0, in1=mpart[:, 0, :],
                                         op0=ALU.mult, op1=ALU.subtract).then_inc(mrest_done, 1)
                dve.wait_ge(mmid_done, b + 1)
                dve.tensor_tensor(mpart[:, 2, :], mrest[:, :], mpart[:, 1, :], ALU.subtract).then_inc(mlo_done, 1)

            def batch(b, s, half, last):
                if not last:
                    dve.wait_ge(pv_done, b * U + 2)
                    prepare(b + 1, 1 - s, half)
                for c in range(2):
                    dve.wait_ge(pv_done, b * U + (4 * c + 6))
                    dve.wait_ge(l_ready, b * 2 + 1)
                    dve.tensor_copy(oraw[:, 2 * c:2 * c + 2, :].rearrange("p a n -> p (a n)"), ps[:, 4 + c, :]
                                    ).then_inc(o_out, 1)
                if not last:
                    maxima(b + 1)
                for c in range(2):
                    dve.wait_ge(l_ready, b * 2 + (c + 2))
                    dve.wait_ge(wo_ready, b + 1)
                    dve.reciprocal(recip[:, c, :], ps[:, 6 + c, :]).then_inc(recip_done, 1)
                for c in range(2):
                    dve.wait_ge(recip_done, b * 2 + (c + 1))
                    dve.tensor_tensor(onorm[:, 2 * c:2 * c + 2, :].rearrange("p a n -> p (a n)"),
                                      oraw[:, 2 * c:2 * c + 2, :].rearrange("p a n -> p (a n)"), recip[:, c, :],
                                      ALU.mult).then_inc(norm_done, 1)
                if not last:
                    split_maxima(b + 1)
                dve.wait_ge(wo_ready, b + 2)
                xs = x[:, bass.ds(b * TB, TB), :]
                dve.tensor_tensor(xs, ps[:, 5, :].rearrange("p (t d) -> p t d", t=TB), xs, ALU.add
                                  ).then_inc(resid_done, 1)

            prepare(0, 0, 0)
            maxima(0)
            split_maxima(0)
            every_batch(dve, batch)


def attention1(nc, top, x, xt, io, consts):
    U, W = H // 2, D1
    TRI = S + P
    with top.stage() as ctx:
        def sb(name, shape, dt=F32):
            return ctx.enter_context(nc.sbuf_tensor("a1_" + name, shape, dt))

        def sem(name):
            return top.semaphore("a1_" + name)

        wq, wk, wv = (sb(n, [P, DK, H * W]) for n in ("wq", "wk", "wv"))
        wo = sb("wo", [P, U, D])
        sel = sb("sel", [W + 1, W])
        ctxT = sb("ctxT", [P, DK, S])
        qT, kT = sb("qT", [W + 1, H, S]), sb("kT", [W + 1, H, S])
        V = sb("V", [P, TB, H, W + 1])
        top_s = sb("top_s", [P, TB, H])
        mT = sb("mT", [H, S])
        pT = sb("pT", [P, 2, 2, TRI])
        oraw = sb("oraw", [W + 1, 2, 2, S])
        recip = sb("recip", [W, 2, S])
        onorm = sb("onorm", [P, U, S])
        ps = ctx.enter_context(nc.psum_tensor("a1_ps", [P, 2, 4, 512], F32))

        (weights, ones_set, ctx_loaded, q_proj, k_proj, v_proj, q_out, k_out, v_out,
         s_ready, max_done, mt_ready, mt_out, mrow_landed, st_ready, exp_done, pv_done, o_out,
         l_ready, recip_done, norm_done, wo_ready, resid_done) = (sem(n) for n in (
             "weights", "ones_set", "ctx_loaded", "q_proj", "k_proj", "v_proj", "q_out", "k_out", "v_out",
             "s_ready", "max_done", "mt_ready", "mt_out", "mrow_landed", "st_ready",
             "exp_done", "pv_done", "o_out", "l_ready", "recip_done", "norm_done", "wo_ready", "resid_done"))
        block = ctx.enter_context(nc.Block())

        @block.sync
        def _(sp):
            for dst, name in ((wq, "a1_wq"), (wk, "a1_wk"), (wv, "a1_wv"), (wo, "a1_wo")):
                sp.dma_start(dst[:, :, :], io[name].rearrange("k p n -> p k n")).then_inc(weights, 16)
            sp.dma_start(sel[:, :], io["a1_sel"]).then_inc(weights, 16)
            with sp.Fori(0, B) as b:
                sp.wait_ge(v_proj, 4 * b)
                sp.dma_start(ctxT[:, :, :], io["ctxT"][bass.ds(b, 1)].rearrange("b (k p) s -> p (b k) s", p=P)
                             ).then_inc(ctx_loaded, 16)
                sp.wait_ge(mt_out, b + 1)
                sp.dma_start(qT[W:W + 1, :, :], mT[:, :]).then_inc(mrow_landed, 16)

        @block.tensor
        def _(pe):
            pe.sem_inc(pv_done, 2)
            pe.wait_ge(weights, 16 * 5)
            with pe.Fori(0, B) as b:
                pe.wait_ge(ctx_loaded, 16 * b + 16)
                pe.wait_ge(exp_done, 8 * b)
                for c in range(U):
                    if c >= 4:
                        pe.wait_ge(q_out, 16 * b + 2 * (c - 3))
                    for k in range(DK):
                        mm = pe.matmul(ps[:, 0, c % 4, 0:S], wq[:, k, c * P:(c + 1) * P],
                                       xt[:, k, bass.ds(b * S, S)], start=(k == 0), stop=(k == DK - 1))
                    mm.then_inc(q_proj, 1)
                    if c == 0:
                        pe.wait_ge(resid_done, b)
                    if c >= 4:
                        pe.wait_ge(k_out, 16 * b + 2 * (c - 3))
                    for k in range(DK):
                        mm = pe.matmul(ps[:, 1, c % 4, 0:S], wk[:, k, c * P:(c + 1) * P],
                                       ctxT[:, k, :], start=(k == 0), stop=(k == DK - 1))
                    mm.then_inc(k_proj, 1)
                pe.wait_ge(q_out, 16 * b + 16)
                for t in range(TB):
                    for f in range(2):
                        for k in range(DK):
                            mm = pe.matmul(ps[:, 0, 2 * t + f, :], ctxT[:, k, t * P:(t + 1) * P],
                                           wv[:, k, f * 512:(f + 1) * 512], start=(k == 0), stop=(k == DK - 1))
                        mm.then_inc(v_proj, 1)
                pe.wait_ge(ones_set, 3)
                for n in range(4):
                    pe.wait_ge(q_out, 16 * b + 16)
                    pe.wait_ge(k_out, 16 * b + 16)
                    if n == 1:
                        pe.wait_ge(v_out, 4 * b + 4)
                    if n >= 2:
                        pe.wait_ge(max_done, 8 * b + 2 * (n - 1))
                    for j in range(4):
                        h = 4 * n + j
                        pe.matmul(ps[:, 1 - n % 2, j, 0:P], qT[0:W, h, 0:P], kT[0:W, h, 0:P], start=True, stop=False)
                        pe.matmul(ps[:, 1 - n % 2, j, 0:P], consts["identb"][:, :], consts["tri"][:, 0, :],
                                  start=False, stop=True)
                        pe.matmul(ps[:, 1 - n % 2, j, P:TRI], qT[0:W, h, P:S], kT[0:W, h, :], start=True, stop=False)
                        mm = pe.matmul(ps[:, 1 - n % 2, j, S:TRI], consts["identb"][:, :], consts["tri"][:, 0, :],
                                       start=False, stop=True)
                    mm.then_inc(s_ready, 1)
                pe.wait_ge(max_done, 8 * b + 8)
                for t in range(TB):
                    mm = pe.transpose(ps[0:H, 1, 2, t * P:(t + 1) * P], top_s[:, t, :], consts["ident"][:, :])
                mm.then_inc(mt_ready, 1)
                pe.wait_ge(mrow_landed, 16 * b + 16)
                for u in range(U + 2):
                    if u < U:
                        if u >= 2:
                            pe.wait_ge(exp_done, 8 * b + u - 1)
                        for j in range(2):
                            h, bank = 2 * u + j, ps[:, 0, 2 * (u % 2) + j, :]
                            pe.matmul(bank[:, 0:S], kT[:, h, 0:P], qT[:, h, :], start=True, stop=False)
                            pe.matmul(bank[:, 0:P], consts["identb"][:, :], consts["tri"][:, 1, :],
                                      start=False, stop=True)
                            pe.matmul(bank[:, S:TRI], kT[:, h, P:S], qT[:, h, P:S], start=True, stop=False)
                            mm = pe.matmul(bank[:, S:TRI], consts["identb"][:, :], consts["tri"][:, 1, :],
                                           start=False, stop=True)
                        mm.then_inc(st_ready, 1)
                    if 1 <= u <= U:
                        m = u - 1
                        pe.wait_ge(exp_done, 8 * b + m + 1)
                        if m >= 2:
                            pe.wait_ge(o_out, 8 * b + m - 1)
                        for j in range(2):
                            h, o = 2 * m + j, ps[0:W + 1, 1, m % 2, j * S:(j + 1) * S]
                            pe.matmul(o, V[:, 0, h, :], pT[:, m % 2, j, 0:S], start=True, stop=False)
                            mm = pe.matmul(o[:, P:S], V[:, 1, h, :], pT[:, m % 2, j, S:TRI],
                                           start=False, stop=True)
                        mm.then_inc(pv_done, 1)
                    if u >= 2:
                        m = u - 2
                        pe.wait_ge(o_out, 8 * b + m + 1)
                        if m >= 1:
                            pe.wait_ge(recip_done, 8 * b + m)
                        pe.matmul(ps[0:W, 1, 2, :], sel[:, :], oraw[:, m % 2, :, :].rearrange("p a n -> p (a n)"),
                                  start=True, stop=True).then_inc(l_ready, 1)
                pe.wait_ge(norm_done, 16 * b + 16)
                for t in range(TB):
                    for c in range(U):
                        mm = pe.matmul(ps[:, 1, 3, t * S:(t + 1) * S], onorm[:, c, t * P:(t + 1) * P], wo[:, c, :],
                                       start=(c == 0), stop=(c == U - 1))
                mm.then_inc(wo_ready, 1)

        @block.scalar
        def _(act):
            with act.Fori(0, B) as b:
                for c in range(U):
                    act.wait_ge(q_proj, 8 * b + c + 1)
                    act.wait_ge(pv_done, 8 * b + 2)
                    for j in range(2):
                        act.activation(qT[0:W, 2 * c + j, :], ps[j * W:(j + 1) * W, 0, c % 4, 0:S], ACT.Copy
                                       ).then_inc(q_out, 1)
                for t in range(TB):
                    for f in range(2):
                        act.wait_ge(v_proj, 4 * b + 2 * t + f + 1)
                        act.activation(V[:, t, 8 * f:8 * f + 8, 0:W],
                                       ps[:, 0, 2 * t + f, :].rearrange("p (h w) -> p h w", w=W), ACT.Copy
                                       ).then_inc(v_out, 1)
                act.wait_ge(mt_ready, b + 1)
                act.wait_ge(mrow_landed, 16 * b)
                act.mul(mT[:, :], ps[0:H, 1, 2, 0:S], -1.0).then_inc(mt_out, 1)
                for u in range(U):
                    act.wait_ge(st_ready, 8 * b + u + 1)
                    act.wait_ge(pv_done, 8 * b + u + 1)
                    act.activation(pT[:, u % 2, :, :], ps[:, 0, 2 * (u % 2):2 * (u % 2) + 2, 0:TRI], ACT.Exp,
                                   scale=float(D1) ** -0.5).then_inc(exp_done, 1)

        @block.vector
        def _(dve):
            dve.memset(V[:, 0, :, W:W + 1], 1.0).then_inc(ones_set, 1)
            dve.memset(V[:, 1, :, W:W + 1], 1.0).then_inc(ones_set, 1)
            dve.memset(kT[W:W + 1, :, :], 1.0).then_inc(ones_set, 1)
            with dve.Fori(0, B) as b:
                for c in range(U):
                    dve.wait_ge(k_proj, 8 * b + c + 1)
                    dve.wait_ge(pv_done, 8 * b + 2)
                    for j in range(2):
                        dve.tensor_copy(kT[0:W, 2 * c + j, :], ps[j * W:(j + 1) * W, 1, c % 4, 0:S]
                                        ).then_inc(k_out, 1)
                dve.wait_ge(mt_ready, b)
                for n in range(4):
                    dve.wait_ge(s_ready, 4 * b + n + 1)
                    dve.tensor_reduce(top_s[:, 0, 4 * n:4 * n + 4], ps[:, 1 - n % 2, :, 0:P], AX.X, ALU.max
                                      ).then_inc(max_done, 1)
                    dve.tensor_reduce(top_s[:, 1, 4 * n:4 * n + 4], ps[:, 1 - n % 2, :, P:TRI], AX.X, ALU.max
                                      ).then_inc(max_done, 1)
                for u in range(U + 1):
                    if u < U:
                        dve.wait_ge(pv_done, 8 * b + u + 3)
                        if u >= 2:
                            dve.wait_ge(norm_done, 16 * b + 2 * (u - 1))
                        dve.tensor_copy(oraw[:, u % 2, :, :].rearrange("p a n -> p (a n)"),
                                        ps[0:W + 1, 1, u % 2, :]).then_inc(o_out, 1)
                    if u > 0:
                        m = u - 1
                        dve.wait_ge(l_ready, 8 * b + m + 1)
                        dve.wait_ge(norm_done, 16 * b + 2 * m)
                        dve.reciprocal(recip[:, :, :].rearrange("p a n -> p (a n)"), ps[0:W, 1, 2, :]
                                       ).then_inc(recip_done, 1)
                        dve.wait_ge(recip_done, 8 * b + m + 1)
                        dve.wait_ge(wo_ready, b)
                        for j in range(2):
                            dve.tensor_tensor(onorm[j * W:(j + 1) * W, m, :], oraw[0:W, m % 2, j, :],
                                              recip[:, j, :], ALU.mult).then_inc(norm_done, 1)
                dve.wait_ge(wo_ready, b + 1)
                xs = x[:, bass.ds(b * TB, TB), :]
                dve.tensor_tensor(xs, ps[:, 1, 3, :].rearrange("p (t d) -> p t d", t=TB), xs, ALU.add
                                  ).then_inc(resid_done, 1)


def chained(engine, sem):
    count = [0]

    def step(ins):
        count[0] += 1
        ins.then_inc(sem, 1)
        engine.wait_ge(sem, count[0])
    return step


def gates0(nc, top, logits, hot, weight, io):
    with top.stage() as ctx:
        def sb(name, shape, dt=F32):
            return ctx.enter_context(nc.sbuf_tensor("g0_" + name, shape, dt))

        bias, rank = sb("bias", [P, E]), sb("rank", [P, E])
        lb, ex, pr, eq = (sb(n, [P, TT, E]) for n in ("lb", "ex", "pr", "eq"))
        m, s, r = (sb(n, [P, TT]) for n in ("m", "s", "r"))
        loaded, chain, shifted, exped = (top.semaphore("g0_" + n) for n in (
            "loaded", "chain", "shifted", "exped"))
        block = ctx.enter_context(nc.Block())

        def over_e(a):
            return a[:, :].unsqueeze(2).to_broadcast([P, TT, E])

        def over_t(a):
            return a[:, :].unsqueeze(1).to_broadcast([P, TT, E])

        @block.sync
        def _(sp):
            sp.dma_start(bias[:, :], io["f0_rb"]).then_inc(loaded, 16)
            sp.dma_start(rank[:, :], io["rank"]).then_inc(loaded, 16)

        @block.scalar
        def _(act):
            act.wait_ge(shifted, 1)
            act.activation(ex[:, :, :], lb[:, :, :], ACT.Exp).then_inc(exped, 1)

        @block.vector
        def _(dve):
            dve.wait_ge(loaded, 32)
            step = chained(dve, chain)
            step(dve.tensor_tensor(lb[:, :, :], logits[:, :, :], over_t(bias), ALU.add))
            step(dve.tensor_reduce(m[:, :], lb[:, :, :], AX.X, ALU.max))
            dve.tensor_tensor(lb[:, :, :], lb[:, :, :], over_e(m), ALU.subtract).then_inc(shifted, 1)
            dve.wait_ge(exped, 1)
            step(dve.tensor_reduce(s[:, :], ex[:, :, :], AX.X, ALU.add))
            step(dve.reciprocal(r[:, :], s[:, :]))
            step(dve.tensor_tensor(pr[:, :, :], ex[:, :, :], over_e(r), ALU.mult))
            step(dve.tensor_reduce(weight[:, :], pr[:, :, :], AX.X, ALU.max))
            step(dve.tensor_tensor(eq[:, :, :], pr[:, :, :], over_e(weight), ALU.is_equal))
            step(dve.tensor_tensor(eq[:, :, :], eq[:, :, :], over_t(rank), ALU.mult))
            step(dve.tensor_reduce(s[:, :], eq[:, :, :], AX.X, ALU.max))
            step(dve.tensor_tensor(hot[:, :, :], eq[:, :, :], over_e(s), ALU.is_equal))


def gates1(nc, top, logits, hot1, hot2, r1, r2, io):
    with top.stage() as ctx:
        def sb(name, shape, dt=F32):
            return ctx.enter_context(nc.sbuf_tensor("g1_" + name, shape, dt))

        rank = sb("rank", [P, E])
        ab, rest, t1, t2, ex1, ex2, keep = (
            sb(n, [P, TT, E]) for n in ("ab", "rest", "t1", "t2", "ex1", "ex2", "keep"))
        m1, m2, s = (sb(n, [P, TT]) for n in ("m1", "m2", "s"))
        loaded, chain, shifted, exped = (top.semaphore("g1_" + n) for n in (
            "loaded", "chain", "shifted", "exped"))
        block = ctx.enter_context(nc.Block())

        def over_e(a):
            return a[:, :].unsqueeze(2).to_broadcast([P, TT, E])

        @block.sync
        def _(sp):
            sp.dma_start(rank[:, :], io["rank"]).then_inc(loaded, 16)

        @block.scalar
        def _(act):
            act.wait_ge(shifted, 1)
            act.activation(ex1[:, :, :], t1[:, :, :], ACT.Exp).then_inc(exped, 1)
            act.activation(ex2[:, :, :], t2[:, :, :], ACT.Exp).then_inc(exped, 1)

        @block.vector
        def _(dve):
            dve.wait_ge(loaded, 16)
            step = chained(dve, chain)

            def first_hot(out, values, largest):
                step(dve.tensor_tensor(out[:, :, :], values[:, :, :], over_e(largest), ALU.is_equal))
                step(dve.tensor_tensor(out[:, :, :], out[:, :, :],
                                       rank[:, :].unsqueeze(1).to_broadcast([P, TT, E]), ALU.mult))
                step(dve.tensor_reduce(s[:, :], out[:, :, :], AX.X, ALU.max))
                step(dve.tensor_tensor(out[:, :, :], out[:, :, :], over_e(s), ALU.is_equal))

            def share(r, m, ex, dropped):
                step(dve.tensor_tensor(keep[:, :, :], ab[:, :, :], over_e(m), ALU.max))
                step(dve.tensor_scalar(keep[:, :, :], keep[:, :, :], 0.02, None, ALU.mult))
                step(dve.tensor_tensor(rest[:, :, :], over_e(m), logits[:, :, :], ALU.subtract))
                step(dve.tensor_tensor(keep[:, :, :], rest[:, :, :], keep[:, :, :], ALU.is_le))
                if dropped is not None:
                    step(dve.tensor_tensor(rest[:, :, :], keep[:, :, :], dropped[:, :, :], ALU.mult))
                    step(dve.tensor_tensor(keep[:, :, :], keep[:, :, :], rest[:, :, :], ALU.subtract))
                step(dve.tensor_tensor(keep[:, :, :], keep[:, :, :], ex[:, :, :], ALU.mult))
                step(dve.tensor_reduce(s[:, :], keep[:, :, :], AX.X, ALU.add))
                step(dve.reciprocal(r[:, :], s[:, :]))

            step(dve.tensor_reduce(m1[:, :], logits[:, :, :], AX.X, ALU.max))
            first_hot(hot1, logits, m1)
            step(dve.scalar_tensor_tensor(out=rest[:, :, :], in0=hot1[:, :, :], scalar=NEG, in1=logits[:, :, :],
                                          op0=ALU.mult, op1=ALU.add))
            step(dve.tensor_reduce(m2[:, :], rest[:, :, :], AX.X, ALU.max))
            first_hot(hot2, rest, m2)
            step(dve.tensor_tensor(t1[:, :, :], logits[:, :, :], over_e(m1), ALU.subtract))
            step(dve.tensor_tensor(t2[:, :, :], logits[:, :, :], over_e(m2), ALU.subtract))
            step(dve.scalar_tensor_tensor(out=ab[:, :, :], in0=logits[:, :, :], scalar=-1.0, in1=logits[:, :, :],
                                          op0=ALU.mult, op1=ALU.max))
            dve.tensor_scalar(t2[:, :, :], t2[:, :, :], 0.0, None, ALU.min).then_inc(shifted, 1)
            dve.wait_ge(exped, 2)
            share(r1, m1, ex1, None)
            share(r2, m2, ex2, hot1)


def dispatch(nc, top, tag, xn, hots, dest, table, NT, xs, io, consts, ys=None):
    with top.stage() as ctx:
        def sb(name, shape, dt=F32):
            return ctx.enter_context(nc.sbuf_tensor(tag + name, shape, dt))

        K = len(hots)
        zeros, thr, index = sb("zeros", [P, D]), sb("thr", [P, TT]), sb("index", [P, NT])
        below = sb("below", [P, P])
        belowb, onesb, hotb = sb("belowb", [P, P], BF16), sb("onesb", [P, P], BF16), sb("hotb", [P, TT, E], BF16)
        hot, cnt, pre_a, pre_b, pos, mine = (sb(n, [P, TT, E]) for n in ("hot", "cnt", "pre_a", "pre_b", "pos", "mine"))
        over = sb("over", [P, E, TT])
        tiles, end_a, end_b, base = (sb(n, [P, E]) for n in ("tiles", "end_a", "end_b", "base"))
        destf = sb("destf", [P, K, TT])
        past = sb("past", [P, NT, E])
        tabf = sb("tabf", [P, NT + 2])
        prank = ctx.enter_context(nc.psum_tensor(tag + "prank", [P, 512], F32))
        pcnt = ctx.enter_context(nc.psum_tensor(tag + "pcnt", [P, 512], F32))
        loaded, chain, counted, zeroed, zero_set = (top.semaphore(tag + n) for n in (
            "loaded", "chain", "counted", "zeroed", "zero_set"))
        scattered = top.for_indirect(tag + "scattered")
        block = ctx.enter_context(nc.Block())

        @block.sync
        def _(sp):
            sp.dma_start(thr[:, :], io["thr"]).then_inc(loaded, 16)
            sp.dma_start(index[:, :], io["index"][:, 0:NT]).then_inc(loaded, 16)
            sp.dma_start(below[:, :], io["below"]).then_inc(loaded, 16)
            sp.wait_ge(zero_set, 1)
            sp.dma_start(xs.rearrange("(n p) d -> p n d", p=P),
                         zeros[:, :].unsqueeze(1).to_broadcast([P, NT, D])).then_inc(zeroed, 16)

        @block.vector
        def _(dve):
            dve.memset(zeros[:, :], 0.0).then_inc(zero_set, 1)
            dve.wait_ge(loaded, 48)
            step = chained(dve, chain)
            step(dve.tensor_copy(belowb[:, :], below[:, :]))
            step(dve.tensor_copy(onesb[:, :], consts["ones"][:, :]))
            if K == 2:
                step(dve.tensor_tensor(hot[:, :, :], hots[0][:, :, :], hots[1][:, :, :], ALU.add))
            else:
                step(dve.tensor_copy(hot[:, :, :], hots[0][:, :, :]))
            step(dve.tensor_copy(hotb[:, :, :], hot[:, :, :]))
            dve.wait_ge(counted, 1)
            step(dve.tensor_copy(cnt[:, :, :], pcnt[:, 0:TT * E].rearrange("p (t e) -> p t e", e=E)))
            a, b = cnt, pre_a
            n = 1
            while n < TT:
                step(dve.tensor_tensor(b[:, n:, :], a[:, n:, :], a[:, :TT - n, :], ALU.add))
                step(dve.tensor_copy(b[:, :n, :], a[:, :n, :]))
                a, b = b, (pre_a if b is pre_b else pre_b)
                n *= 2
            step(dve.tensor_tensor(over[:, :, :], a[:, TT - 1, :].unsqueeze(2).to_broadcast([P, E, TT]),
                                   thr[:, :].unsqueeze(1).to_broadcast([P, E, TT]), ALU.is_gt))
            step(dve.tensor_reduce(tiles[:, :], over[:, :, :], AX.X, ALU.add))
            u, v = tiles, end_a
            n = 1
            while n < E:
                step(dve.tensor_tensor(v[:, n:], u[:, n:], u[:, :E - n], ALU.add))
                step(dve.tensor_copy(v[:, :n], u[:, :n]))
                u, v = v, (end_a if v is end_b else end_b)
                n *= 2
            step(dve.tensor_tensor(base[:, :], u[:, :], tiles[:, :], ALU.subtract))
            step(dve.tensor_scalar(base[:, :], base[:, :], float(P), None, ALU.mult))
            step(dve.tensor_tensor(pos[:, :, :], a[:, :, :], cnt[:, :, :], ALU.subtract))
            step(dve.tensor_tensor(pos[:, :, :], pos[:, :, :],
                                   prank[:, 0:TT * E].rearrange("p (t e) -> p t e", e=E), ALU.add))
            step(dve.tensor_tensor(pos[:, :, :], pos[:, :, :], base[:, :].unsqueeze(1).to_broadcast([P, TT, E]), ALU.add))
            for c in range(K):
                step(dve.tensor_tensor(mine[:, :, :], pos[:, :, :], hots[c][:, :, :], ALU.mult))
                step(dve.tensor_reduce(destf[:, c, :], mine[:, :, :], AX.X, ALU.add))
            step(dve.tensor_copy(dest[:, :, :], destf[:, :, :]))
            step(dve.tensor_tensor(past[:, :, :], u[:, :].unsqueeze(1).to_broadcast([P, NT, E]),
                                   index[:, :].unsqueeze(2).to_broadcast([P, NT, E]), ALU.is_le))
            step(dve.memset(tabf[:, 0:2], -1.0))
            step(dve.tensor_reduce(tabf[:, 2:], past[:, :, :], AX.X, ALU.add))
            step(dve.tensor_scalar(table[:, :], tabf[0:1, :], E - 1.0, None, ALU.min))

        @block.tensor
        def _(pe):
            pe.wait_ge(chain, 4)
            pe.matmul(prank[:, 0:TT * E], belowb[:, :], hotb[:, :, :].rearrange("p t e -> p (t e)"),
                      start=True, stop=True)
            pe.matmul(pcnt[:, 0:TT * E], onesb[:, :], hotb[:, :, :].rearrange("p t e -> p (t e)"),
                      start=True, stop=True).then_inc(counted, 1)

        @block.gpsimd
        def _(pool):
            pool.wait_ge(chain, 27 + 2 * K)
            pool.wait_ge(zeroed, 16)
            for t in range(TT):
                for c in range(K):
                    pool.indirect_dma_start(xs, bass.IndirectOffsetOnAxis(ap=dest[:, c, t:t + 1], axis=0),
                                            xn[:, t, :], None).then_inc(scattered, 16)
            pool.wait_ge(scattered, 16 * K * TT)


def expert_tiles(nc, top, tag, xs, ys, table, NT, io, consts, gated):
    NW = 3 if gated else 2
    Q = 2
    FQ = FT // Q
    with top.stage() as ctx:
        def sb(name, shape, dt=F32):
            return ctx.enter_context(nc.sbuf_tensor(tag + name, shape, dt))

        w1 = sb("w1", [P, 2, DK, F])
        w3 = sb("w3", [P, 2, DK, F]) if gated else None
        w2 = sb("w2", [P, 2, FT, D])
        b1 = None if gated else sb("b1", [P, E, FT])
        b2 = None if gated else sb("b2", [1, E, D])
        xg, yg = sb("xg", [P, 2, D]), sb("yg", [P, 2, D])
        xgT = sb("xgT", [P, 2, DK, P])
        hT = sb("hT", [P, 2, FT, P])
        gate_o = sb("gate_o", [P, Q, FQ * P]) if gated else None
        ph = ctx.enter_context(nc.psum_tensor(tag + "ph", [P, Q, 2 if gated else 1, 512], F32))
        px = ctx.enter_context(nc.psum_tensor(tag + "px", [P, 512], F32))
        py = ctx.enter_context(nc.psum_tensor(tag + "py", [P, 2, 512], F32))
        (bias_loaded, x_ready0, x_ready1, w_ready0, w_ready1, turned, turned_out, h_ready, gate_done, h_out0, h_out1,
         y_ready, y_out, stored0, stored1) = (top.semaphore(tag + n) for n in (
             "bias_loaded", "x_ready0", "x_ready1", "w_ready0", "w_ready1", "turned", "turned_out", "h_ready",
             "gate_done", "h_out0", "h_out1", "y_ready", "y_out", "stored0", "stored1"))
        x_ready, w_ready, h_out, stored = (x_ready0, x_ready1), (w_ready0, w_ready1), (h_out0, h_out1), (stored0, stored1)
        block = ctx.enter_context(nc.Block())

        def every_tile(engine, body):
            with engine.Fori(0, NT // 2) as pair:
                body(pair * 2, 0, pair)
                body(pair * 2 + 1, 1, pair)
            if NT % 2:
                body(NT - 1, 0, NT // 2)

        @block.sync
        def _(sp):
            if not gated:
                sp.dma_start(b1[:, :, :], io[tag + "b1"]).then_inc(bias_loaded, 16)
                sp.dma_start(b2[:, :, :], io[tag + "b2"]).then_inc(bias_loaded, 16)

            def load(i, s, half):
                sp.wait_ge(turned, i + 1)
                sp.dma_start(xg[:, s, :], xs[bass.ds(i * P, P), :]).then_inc(x_ready[s], 16)
                sp.wait_ge(y_ready, i + 1)
                e = sp.value_load(table[0:1, bass.ds(i + 2, 1)], min_val=0, max_val=E - 1)
                before = sp.value_load(table[0:1, bass.ds(i, 1)])
                with sp.If(e != before):
                    sp.dma_start(w1[:, s, :, :], io[tag + "w1"][bass.ds(e, 1)].rearrange("e (k p) f -> p (e k) f", p=P)
                                 ).then_inc(w_ready[s], 16)
                    if gated:
                        sp.dma_start(w3[:, s, :, :], io[tag + "w3"][bass.ds(e, 1)].rearrange(
                            "e (k p) f -> p (e k) f", p=P)).then_inc(w_ready[s], 16)
                    sp.dma_start(w2[:, s, :, :], io[tag + "w2"][bass.ds(e, 1)].rearrange("e (k p) d -> p (e k) d", p=P)
                                 ).then_inc(w_ready[s], 16)
                with sp.Else():
                    sp.sem_inc(w_ready[s], 16 * NW)
            every_tile(sp, load)

        @block.tensor
        def _(pe):
            pe.sem_inc(turned, 2)
            pe.sem_inc(y_ready, 2)
            if not gated:
                pe.wait_ge(bias_loaded, 32)

            def turn(i, s, half):
                pe.wait_ge(x_ready[s], half * 16 + 16)
                pe.wait_ge(turned_out, i + 1)
                for k in range(DK):
                    mm = pe.transpose(px[:, k * P:(k + 1) * P], xg[:, s, k * P:(k + 1) * P], consts["ident"][:, :])
                mm.then_inc(turned, 1)

            def multiply(i, s, half, last=False):
                e = None if gated else pe.value_load(table[0:1, bass.ds(i + 2, 1)], min_val=0, max_val=E - 1)
                pe.wait_ge(turned_out, i + 2)
                pe.wait_ge(w_ready[s], (half + 1) * (16 * NW))
                for q in range(Q):
                    pe.wait_ge(h_out[q], i + 1)
                    for f in range(FQ):
                        for n, w in enumerate((w1, w3) if gated else (w1,)):
                            for k in range(DK):
                                mm = pe.matmul(ph[:, q, n, f * P:(f + 1) * P],
                                               w[:, s, k, (q * FQ + f) * P:(q * FQ + f + 1) * P], xgT[:, s, k, :],
                                               start=(k == 0), stop=(k == DK - 1))
                    mm.then_inc(h_ready, 1)
                if not last:
                    turn(i + 1, 1 - s, half + s)
                pe.wait_ge(y_out, i + 1)
                for q in range(Q):
                    pe.wait_ge(h_out[q], i + 2)
                    for f in range(q * FQ, (q + 1) * FQ):
                        mm = pe.matmul(py[:, s, 0:D], hT[:, s, f, :], w2[:, s, f, :],
                                       start=(f == 0), stop=(gated and f == FT - 1))
                if not gated:
                    mm = pe.matmul(py[:, s, 0:D], consts["ones"][0:1, 0:P], b2[:, bass.ds(e, 1), :].rearrange(
                        "p e d -> p (e d)"), start=False, stop=True)
                mm.then_inc(y_ready, 1)

            turn(0, 0, 0)
            with pe.Fori(0, (NT - 1) // 2) as pair:
                multiply(pair * 2, 0, pair)
                multiply(pair * 2 + 1, 1, pair)
            if NT % 2 == 0:
                multiply(NT - 2, 0, NT // 2 - 1)
            multiply(NT - 1, (NT - 1) % 2, (NT - 1) // 2, last=True)

        @block.scalar
        def _(act):
            act.sem_inc(turned_out, 1)
            if not gated:
                act.sem_inc(h_out[0], 1)
                act.wait_ge(bias_loaded, 32)

            def turn_out(i, s, half):
                act.wait_ge(turned, i + 3)
                act.activation(xgT[:, s, :, :].rearrange("p k n -> p (k n)"), px[:, 0:D], ACT.Copy
                               ).then_inc(turned_out, 1)

            def gate(i, s, half, last=False):
                if gated:
                    for q in range(Q):
                        act.wait_ge(h_ready, i * 2 + (q + 1))
                        act.wait_ge(h_out[q], i + 1)
                        act.activation(gate_o[:, q, :], ph[:, q, 0, :], ACT.Silu).then_inc(gate_done, 1)
                else:
                    e = act.value_load(table[0:1, bass.ds(i + 2, 1)], min_val=0, max_val=E - 1)
                    act.wait_ge(h_ready, i * 2 + 1)
                    act.wait_ge(y_ready, i + 1)
                    for f in range(FQ):
                        a = act.activation(hT[:, s, f, :], ph[:, 0, 0, f * P:(f + 1) * P], ACT.Relu,
                                           bias=b1[:, e, f:f + 1])
                    a.then_inc(h_out[0], 1)
                if not last:
                    act.wait_ge(h_ready, i * 2 + 1)
                    turn_out(i + 1, 1 - s, half + s)
                act.wait_ge(y_out, i + 3)
                act.dma_start(ys[bass.ds(i * P, P), :], yg[:, s, :]).then_inc(stored[s], 16)

            act.sem_inc(stored[0], 16)
            act.sem_inc(stored[1], 16)
            turn_out(0, 0, 0)
            with act.Fori(0, (NT - 1) // 2) as pair:
                gate(pair * 2, 0, pair)
                gate(pair * 2 + 1, 1, pair)
            if NT % 2 == 0:
                gate(NT - 2, 0, NT // 2 - 1)
            gate(NT - 1, (NT - 1) % 2, (NT - 1) // 2, last=True)
            act.wait_ge(stored[0], 16 + 16 * ((NT + 1) // 2))
            act.wait_ge(stored[1], 16 + 16 * (NT // 2))

        @block.vector
        def _(dve):
            dve.sem_inc(y_out, 2)
            dve.sem_inc(h_out[1], 1)
            if gated:
                dve.sem_inc(h_out[0], 1)
            else:
                dve.wait_ge(bias_loaded, 32)

            def finish(i, s, half):
                if gated:
                    for q in range(Q):
                        dve.wait_ge(gate_done, i * 2 + (q + 1))
                        dve.wait_ge(y_ready, i + 1)
                        dve.tensor_tensor(hT[:, s, q * FQ:(q + 1) * FQ, :].rearrange("p f n -> p (f n)"),
                                          ph[:, q, 1, :], gate_o[:, q, :], ALU.mult).then_inc(h_out[q], 1)
                else:
                    e = dve.value_load(table[0:1, bass.ds(i + 2, 1)], min_val=0, max_val=E - 1)
                    dve.wait_ge(h_ready, i * 2 + 2)
                    dve.wait_ge(y_ready, i + 1)
                    for f in range(FQ):
                        a = dve.tensor_scalar(hT[:, s, FQ + f, :], ph[:, 1, 0, f * P:(f + 1) * P],
                                              b1[:, e, FQ + f:FQ + f + 1], 0.0, ALU.add, ALU.max)
                    a.then_inc(h_out[1], 1)
                dve.wait_ge(y_ready, i + 3)
                dve.wait_ge(stored[s], half * 16 + 16)
                dve.tensor_copy(yg[:, s, :], py[:, s, 0:D]).then_inc(y_out, 1)
            every_tile(dve, finish)


def combine(nc, top, tag, x, ys, dest, weights):
    with top.stage() as ctx:
        K = len(weights)
        yt = ctx.enter_context(nc.sbuf_tensor(tag + "yt", [P, TT, K, D], F32))
        gathered = [top.for_indirect(tag + f"gathered{n}") for n in range(8)]
        added = top.semaphore(tag + "added")
        block = ctx.enter_context(nc.Block())

        @block.gpsimd
        def _(pool):
            for t in range(TT):
                if t >= 8:
                    pool.wait_ge(added, K * (t - 7))
                for c in range(K):
                    pool.indirect_dma_start(yt[:, t, c, :], None, ys,
                                            bass.IndirectOffsetOnAxis(ap=dest[:, c, t:t + 1], axis=0)
                                            ).then_inc(gathered[t % 8], 16)

        @block.vector
        def _(dve):
            for t in range(TT):
                dve.wait_ge(gathered[t % 8], 16 * K * (t // 8 + 1))
                for c in range(K):
                    if c:
                        dve.wait_ge(added, K * t + c)
                    dve.scalar_tensor_tensor(out=x[:, t, :], in0=yt[:, t, c, :], scalar=weights[c][:, t:t + 1],
                                             in1=x[:, t, :], op0=ALU.mult, op1=ALU.add).then_inc(added, 1)


def linear_attention(nc, top, x, xt, io):
    with top.stage() as ctx:
        def sb(name, shape, dt=F32):
            return ctx.enter_context(nc.sbuf_tensor("a2_" + name, shape, dt))

        cx, xb, kv = (sb(n, [P, 2, TB, D]) for n in ("cx", "xb", "kv"))
        pk = ctx.enter_context(nc.psum_tensor("a2_pk", [P, 2, DK, D], F32))
        po = ctx.enter_context(nc.psum_tensor("a2_po", [P, 2, TB, D], F32))
        loaded0, loaded1, copied, kv_ready, kv_out, o_ready, resid_done = (
            top.semaphore("a2_" + n) for n in (
                "loaded0", "loaded1", "copied", "kv_ready", "kv_out", "o_ready", "resid_done"))
        block = ctx.enter_context(nc.Block())

        @block.sync
        def _(sp):
            with sp.Fori(0, B // 2) as pair:
                for s, sem in enumerate((loaded0, loaded1)):
                    sp.wait_ge(kv_ready, 2 * pair + s + 1 - 1)
                    sp.dma_start(cx[:, s, :, :], io["ctx"][bass.ds(pair * 2 + s, 1)].rearrange(
                        "b (t p) d -> p (b t) d", p=P)).then_inc(sem, 16)

        @block.gpsimd
        def _(pool):
            with pool.Fori(0, B // 2) as pair:
                for s in range(2):
                    pool.wait_ge(o_ready, 2 * pair + s + 1)
                    pool.tensor_copy(xb[:, s, :, :], xt[:, :, bass.ds((pair * 2 + s) * S, S)]).then_inc(copied, 1)

        @block.tensor
        def _(pe):
            pe.sem_inc(o_ready, 2)
            pe.sem_inc(kv_ready, 1)
            with pe.Fori(0, B // 2) as pair:
                for s, sem in enumerate((loaded0, loaded1)):
                    b = pair * 2 + s
                    pe.wait_ge(sem, 16 * pair + 16)
                    pe.wait_ge(kv_out, b + 1)
                    for k in range(DK):
                        for t in range(TB):
                            mm = pe.matmul(pk[:, s, k, :], cx[:, s, t, k * P:(k + 1) * P], cx[:, s, t, :],
                                           start=(t == 0), stop=(t == TB - 1))
                    mm.then_inc(kv_ready, 1)
                    pe.wait_ge(kv_out, b + 3)
                    pe.wait_ge(copied, b + 1)
                    pe.wait_ge(resid_done, b + 1)
                    for t in range(TB):
                        for k in range(DK):
                            mm = pe.matmul(po[:, s, t, :], xb[:, s, k, t * P:(t + 1) * P], kv[:, s, k, :],
                                           start=(k == 0), stop=(k == DK - 1))
                    mm.then_inc(o_ready, 1)

        @block.scalar
        def _(act):
            act.sem_inc(kv_out, 2)
            with act.Fori(0, B // 2) as pair:
                for s in range(2):
                    b = pair * 2 + s
                    act.wait_ge(kv_ready, b + 2)
                    act.wait_ge(o_ready, b + 1)
                    act.mul(kv[:, s, :, :], pk[:, s, :, :], 1.0 / S).then_inc(kv_out, 1)

        @block.vector
        def _(dve):
            dve.sem_inc(resid_done, 2)
            with dve.Fori(0, B // 2) as pair:
                for s in range(2):
                    b = pair * 2 + s
                    dve.wait_ge(o_ready, b + 3)
                    xs = x[:, bass.ds(b * TB, TB), :]
                    dve.tensor_tensor(xs, po[:, s, :, :], xs, ALU.add).then_inc(resid_done, 1)


def scaled_linear(nc, top, x, xt, io):
    with top.stage() as ctx:
        def sb(name, shape, dt=F32):
            return ctx.enter_context(nc.sbuf_tensor("f2_" + name, shape, dt))

        cb = sb("cb", [P, DK, D])
        scb, scale, bias = (sb(n, [P, D]) for n in ("scb", "scale", "bias"))
        xb, o1, o2 = (sb(n, [P, 2, TB, D]) for n in ("xb", "o1", "o2"))
        po = ctx.enter_context(nc.psum_tensor("f2_po", [P, 2, TB, D], F32))
        loaded, scaled, copied, o_ready, o1_done, o2_done, resid_done = (
            top.semaphore("f2_" + n) for n in (
                "loaded", "scaled", "copied", "o_ready", "o1_done", "o2_done", "resid_done"))
        block = ctx.enter_context(nc.Block())

        @block.sync
        def _(sp):
            sp.dma_start(cb[:, :, :], io["f2_cb"].rearrange("(k p) n -> p k n", p=P)).then_inc(loaded, 16)
            sp.dma_start(scb[:, :], io["f2_scb"]).then_inc(loaded, 16)
            sp.dma_start(bias[:, :], io["f2_bias"]).then_inc(loaded, 16)

        @block.gpsimd
        def _(pool):
            with pool.Fori(0, B // 2) as pair:
                for s in range(2):
                    pool.wait_ge(o_ready, 2 * pair + s + 1)
                    pool.tensor_copy(xb[:, s, :, :], xt[:, :, bass.ds((pair * 2 + s) * S, S)]).then_inc(copied, 1)

        @block.tensor
        def _(pe):
            pe.sem_inc(o_ready, 2)
            pe.wait_ge(loaded, 48)
            with pe.Fori(0, B // 2) as pair:
                for s in range(2):
                    b = pair * 2 + s
                    pe.wait_ge(copied, b + 1)
                    pe.wait_ge(o1_done, b + 1)
                    for t in range(TB):
                        for k in range(DK):
                            mm = pe.matmul(po[:, s, t, :], xb[:, s, k, t * P:(t + 1) * P], cb[:, k, :],
                                           start=(k == 0), stop=(k == DK - 1))
                    mm.then_inc(o_ready, 1)

        @block.vector
        def _(dve):
            dve.sem_inc(o1_done, 2)
            dve.wait_ge(loaded, 48)
            dve.tensor_scalar(scale[:, :], scb[:, :], 1.0 / 127.0, None, ALU.mult).then_inc(scaled, 1)
            dve.wait_ge(scaled, 1)
            with dve.Fori(0, B // 2) as pair:
                for s in range(2):
                    b = pair * 2 + s
                    dve.wait_ge(o_ready, b + 3)
                    dve.wait_ge(o2_done, b)
                    dve.tensor_tensor(o1[:, s, :, :], po[:, s, :, :],
                                      scale[:, :].unsqueeze(1).to_broadcast([P, TB, D]), ALU.mult).then_inc(o1_done, 1)
                    dve.wait_ge(o1_done, b + 3)
                    dve.wait_ge(resid_done, b)
                    dve.tensor_tensor(o2[:, s, :, :], o1[:, s, :, :],
                                      bias[:, :].unsqueeze(1).to_broadcast([P, TB, D]), ALU.add).then_inc(o2_done, 1)
                    dve.wait_ge(o2_done, b + 1)
                    xs = x[:, bass.ds(b * TB, TB), :]
                    dve.tensor_tensor(xs, o2[:, s, :, :], xs, ALU.add).then_inc(resid_done, 1)


def attention3(nc, top, x, xt, io, consts):
    with top.stage() as ctx:
        def sb(name, shape, dt=F32):
            return ctx.enter_context(nc.sbuf_tensor("a3_" + name, shape, dt))

        wq, wk, wv = (sb(n, [P, DK, D]) for n in ("wq", "wk", "wv"))
        bq, bk = sb("bq", [P, DK]), sb("bk", [P, DK])
        bv = sb("bv", [1, D])
        ctxT = sb("ctxT", [P, DK, S])
        qT, kT = sb("qT", [P, DK, S]), sb("kT", [P, DK, S])
        V = sb("V", [P, TB, D])
        top_s, shift, l, rl = (sb(n, [P, TB]) for n in ("top_s", "shift", "l", "rl"))
        pr, pT = sb("pr", [P, TB, S]), sb("pT", [P, TB, S])
        bank = [ctx.enter_context(nc.psum_tensor(f"a3_{n}", [P, 2, S], F32)) for n in ("q", "k", "v", "s", "t", "o")]
        pq, pk, pv, pS, pt, po = bank
        (weights, ctx_loaded, q_proj, k_proj, v_proj, q_out, k_out, v_out, s_ready, max_done, shift_done,
         exp_done, t_ready, t_out, l_done, o_ready, resid_done) = (
            top.semaphore("a3_" + n) for n in (
                "weights", "ctx_loaded", "q_proj", "k_proj", "v_proj", "q_out", "k_out", "v_out", "s_ready",
                "max_done", "shift_done", "exp_done", "t_ready", "t_out", "l_done", "o_ready", "resid_done"))
        block = ctx.enter_context(nc.Block())

        @block.sync
        def _(sp):
            for dst, name in ((wq, "a3_wq"), (wk, "a3_wk"), (wv, "a3_wv")):
                sp.dma_start(dst[:, :, :], io[name].rearrange("(k p) n -> p k n", p=P)).then_inc(weights, 16)
            for dst, name in ((bq, "a3_bq"), (bk, "a3_bk"), (bv, "a3_bv")):
                sp.dma_start(dst[:, :], io[name]).then_inc(weights, 16)
            with sp.Fori(0, B) as b:
                sp.wait_ge(v_proj, b)
                sp.dma_start(ctxT[:, :, :], io["ctxT"][bass.ds(b, 1)].rearrange("b (k p) s -> p (b k) s", p=P)
                             ).then_inc(ctx_loaded, 16)

        @block.tensor
        def _(pe):
            pe.wait_ge(weights, 16 * 6)
            with pe.Fori(0, B) as b:
                pe.wait_ge(q_out, 2 * b)
                for n in range(DK):
                    for k in range(DK):
                        mm = pe.matmul(pq[:, n, :], wq[:, k, n * P:(n + 1) * P], xt[:, k, bass.ds(b * S, S)],
                                       start=(k == 0), stop=(k == DK - 1))
                mm.then_inc(q_proj, 1)
                pe.wait_ge(ctx_loaded, 16 * b + 16)
                pe.wait_ge(k_out, 2 * b)
                for n in range(DK):
                    for k in range(DK):
                        mm = pe.matmul(pk[:, n, :], wk[:, k, n * P:(n + 1) * P], ctxT[:, k, :],
                                       start=(k == 0), stop=(k == DK - 1))
                mm.then_inc(k_proj, 1)
                pe.wait_ge(v_out, b)
                for t in range(TB):
                    for k in range(DK):
                        pe.matmul(pv[:, t, :], ctxT[:, k, t * P:(t + 1) * P], wv[:, k, :],
                                  start=(k == 0), stop=False)
                    mm = pe.matmul(pv[:, t, :], consts["ones"][0:1, 0:P], bv[:, :], start=False, stop=True)
                mm.then_inc(v_proj, 1)
                pe.wait_ge(q_out, 2 * b + 2)
                pe.wait_ge(k_out, 2 * b + 2)
                pe.wait_ge(exp_done, 2 * b)
                for t in range(TB):
                    for k in range(DK):
                        mm = pe.matmul(pS[:, t, :], qT[:, k, t * P:(t + 1) * P], kT[:, k, :],
                                       start=(k == 0), stop=(k == DK - 1))
                mm.then_inc(s_ready, 1)
                pe.wait_ge(exp_done, 2 * b + 2)
                pe.wait_ge(t_out, b)
                for t in range(TB):
                    for q in range(TB):
                        mm = pe.transpose(pt[:, t, q * P:(q + 1) * P], pr[:, q, t * P:(t + 1) * P],
                                          consts["ident"][:, :])
                mm.then_inc(t_ready, 1)
                pe.wait_ge(t_out, b + 1)
                pe.wait_ge(v_out, b + 1)
                pe.wait_ge(resid_done, 2 * b)
                for q in range(TB):
                    for t in range(TB):
                        mm = pe.matmul(po[:, q, :], pT[:, t, q * P:(q + 1) * P], V[:, t, :],
                                       start=(t == 0), stop=(t == TB - 1))
                mm.then_inc(o_ready, 1)

        @block.scalar
        def _(act):
            act.wait_ge(weights, 16 * 6)
            with act.Fori(0, B) as b:
                act.wait_ge(q_proj, b + 1)
                act.wait_ge(s_ready, b)
                for n in range(DK):
                    act.activation(qT[:, n, :], pq[:, n, :], ACT.Identity, bias=bq[:, n:n + 1]).then_inc(q_out, 1)
                act.wait_ge(v_proj, b + 1)
                act.wait_ge(o_ready, b)
                act.activation(V[:, :, :], pv[:, :, :], ACT.Copy).then_inc(v_out, 1)
                act.wait_ge(shift_done, b + 1)
                act.wait_ge(t_ready, b)
                act.wait_ge(l_done, b)
                for q in range(TB):
                    act.activation(pr[:, q, :], pS[:, q, :], ACT.Exp, bias=shift[:, q:q + 1],
                                   scale=float(D) ** -0.5, accum_out=l[:, q:q + 1]).then_inc(exp_done, 1)

        @block.vector
        def _(dve):
            dve.wait_ge(weights, 16 * 6)
            with dve.Fori(0, B) as b:
                dve.wait_ge(k_proj, b + 1)
                dve.wait_ge(s_ready, b)
                for n in range(DK):
                    dve.tensor_scalar(kT[:, n, :], pk[:, n, :], bk[:, n:n + 1], None, ALU.add).then_inc(k_out, 1)
                dve.wait_ge(s_ready, b + 1)
                dve.tensor_reduce(top_s[:, :], pS[:, :, :], AX.X, ALU.max).then_inc(max_done, 1)
                dve.wait_ge(max_done, b + 1)
                dve.tensor_scalar(shift[:, :], top_s[:, :], -float(D) ** -0.5, None, ALU.mult).then_inc(shift_done, 1)
                dve.wait_ge(exp_done, 2 * b + 2)
                dve.wait_ge(resid_done, 2 * b)
                dve.reciprocal(rl[:, :], l[:, :]).then_inc(l_done, 1)
                dve.wait_ge(t_ready, b + 1)
                dve.wait_ge(o_ready, b)
                dve.tensor_copy(pT[:, :, :], pt[:, :, :]).then_inc(t_out, 1)
                dve.wait_ge(o_ready, b + 1)
                dve.wait_ge(l_done, b + 1)
                for q in range(TB):
                    xs = x[:, b * TB + q, :]
                    dve.scalar_tensor_tensor(out=xs, in0=po[:, q, :], scalar=rl[:, q:q + 1], in1=xs,
                                             op0=ALU.mult, op1=ALU.add).then_inc(resid_done, 1)


def bit_ffn(nc, top, x, ident, io, consts, out):
    with top.stage() as ctx:
        def sb(name, shape, dt=F32):
            return ctx.enter_context(nc.sbuf_tensor("f3_" + name, shape, dt))

        def sem(name):
            return top.semaphore("f3_" + name)

        w1, w1t, w2, w2t = sb("w1", [P, DK * F]), sb("w1t", [P, DK * F]), sb("w2", [P, FT * D]), sb("w2t", [P, FT * D])
        w1q, w2q = sb("w1q", [P, DK, F], BF16), sb("w2q", [P, FT, D], BF16)
        asum, unit, scale = sb("asum", [P, 2]), sb("unit", [P, 2]), sb("scale", [P, 2])
        cw, cb = sb("cw", [P, FT, 3]), sb("cb", [P, FT])
        stats = sb("stats", [P, TT, 6])
        total, diff, m2, mean, diff2, var, vareps, rstd, hi, lo, amax, amaxc, rec, qs, qr, root, guess = (
            sb(n, [P, TT]) for n in ("total", "diff", "m2", "mean", "diff2", "var", "vareps", "rstd", "hi", "lo",
                                     "amax", "amaxc", "rec", "qs", "qr", "root", "guess"))
        xn = sb("xn", [P, TT, D])
        q1, q2 = sb("q1", [P, TB, D]), sb("q2", [P, TB, D])
        xq = sb("xq", [P, TB, D], BF16)
        xqT = sb("xqT", [P, DK, S], BF16)
        rb = sb("rb", [P, TB, P])
        rs = sb("rs", [P, S])
        h = sb("h", [P, FT, S + 2])
        y0, y1, y2, sT = (sb(n, [P, FT, S]) for n in ("y0", "y1", "y2", "sT"))
        shi, slo, sax, saxc, srec, sqs, sqr = (sb(n, [P, TB]) for n in ("shi", "slo", "sax", "saxc", "srec", "sqs", "sqr"))
        s1, s2 = sb("s1", [P, TB, F]), sb("s2", [P, TB, F])
        sq = sb("sq", [P, TB, F], BF16)
        sqT = sb("sqT", [P, FT, S], BF16)
        ptr = ctx.enter_context(nc.psum_tensor("f3_ptr", [P, DK, S], BF16))
        pr = ctx.enter_context(nc.psum_tensor("f3_pr", [P, 512], F32))
        pn = ctx.enter_context(nc.psum_tensor("f3_pn", [P, TB, F], F32))
        pb = pn[:, 0, :].bitcast(BF16).rearrange("p (f n) -> p f n", f=FT)
        ph = pn[:, :, :].rearrange("p t (a n) -> p (t a) n", a=2)
        po = ctx.enter_context(nc.psum_tensor("f3_po", [P, TB, D], F32))
        (loaded, wchain, asum_done, sum_ready, stats_done, comb, normed, chain, q_done, q_sub, rb_done, pads, trans1,
         xqT_out, r_ready, rs_done, h_ready, h_done, y0_done, y1_done, y2_done, silu_done, trans2, red_done,
         s1_done, s2_done, sq_done, trans3, sqT_out, o_ready, resid_done, stored, rooted) = (sem(n) for n in (
             "loaded", "wchain", "asum_done", "sum_ready", "stats_done", "comb", "normed", "chain", "q_done", "q_sub",
             "rb_done", "pads", "trans1", "xqT_out", "r_ready", "rs_done", "h_ready", "h_done", "y0_done", "y1_done",
             "y2_done", "silu_done", "trans2", "red_done", "s1_done", "s2_done", "sq_done", "trans3", "sqT_out",
             "o_ready", "resid_done", "stored", "rooted"))
        block = ctx.enter_context(nc.Block())

        @block.sync
        def _(sp):
            sp.dma_start(w1[:, :].rearrange("p (k f) -> p k f", k=DK), io["f3_w1"].rearrange("(k p) f -> p k f", p=P)
                         ).then_inc(loaded, 16)
            sp.dma_start(w2[:, :].rearrange("p (k d) -> p k d", k=FT), io["f3_w2"].rearrange("(k p) d -> p k d", p=P)
                         ).then_inc(loaded, 16)
            sp.dma_start(cw[:, :, :], io["f3_cw"].rearrange("(t p) k -> p t k", p=P)).then_inc(loaded, 16)
            sp.dma_start(cb[:, :], io["f3_cb"]).then_inc(loaded, 16)
            with sp.Fori(0, B) as b:
                sp.wait_ge(resid_done, 2 * b + 2)
                sp.dma_start(out[bass.ds(b, 1)].rearrange("b (t p) d -> p (b t) d", p=P), x[:, bass.ds(b * TB, TB), :]
                             ).then_inc(stored, 16)
            sp.wait_ge(stored, 16 * B)

        @block.vector
        def _(dve):
            wstep = chained(dve, wchain)
            dve.memset(h[:, :, 0:1], 0.0).then_inc(pads, 1)
            dve.memset(h[:, :, S + 1:S + 2], 0.0).then_inc(pads, 1)
            dve.wait_ge(loaded, 64)
            dve.tensor_reduce(asum[:, 0:1], w1[:, :], AX.X, ALU.add, apply_absolute_value=True).then_inc(asum_done, 1)
            dve.tensor_reduce(asum[:, 1:2], w2[:, :], AX.X, ALU.add, apply_absolute_value=True).then_inc(asum_done, 1)
            dve.wait_ge(sum_ready, 1)
            step = wstep
            step(dve.tensor_scalar(unit[:, :], pr[:, 0:2], 1.0 / (D * F), 1e-5, ALU.mult, ALU.max))
            step(dve.reciprocal(scale[:, :], unit[:, :]))
            for n, (w, wt, wq) in enumerate(((w1, w1t, w1q), (w2, w2t, w2q))):
                step(dve.tensor_scalar(wt[:, :], w[:, :], scale[:, n:n + 1], MAGIC, ALU.mult, ALU.add))
                step(dve.tensor_scalar(w[:, :], wt[:, :], MAGIC, 1.0, ALU.subtract, ALU.min))
                step(dve.tensor_scalar(wq[:, :, :].rearrange("p a b -> p (a b)"), w[:, :], -1.0, None, ALU.max))
            with dve.Fori(0, TT) as t:
                dve.bn_stats(stats[:, t, :], x[:, t, :]).then_inc(stats_done, 1)
            dve.wait_ge(stats_done, TT)
            step = chained(dve, comb)
            step(dve.tensor_tensor(total[:, :], stats[:, :, 1], stats[:, :, 4], ALU.add))
            step(dve.tensor_tensor(diff[:, :], stats[:, :, 1], stats[:, :, 4], ALU.subtract))
            step(dve.tensor_tensor(m2[:, :], stats[:, :, 2], stats[:, :, 5], ALU.add))
            step(dve.tensor_scalar(mean[:, :], total[:, :], 0.5, None, ALU.mult))
            step(dve.tensor_tensor(diff2[:, :], diff[:, :], diff[:, :], ALU.mult))
            step(dve.scalar_tensor_tensor(out=var[:, :], in0=diff2[:, :], scalar=D / 4.0, in1=m2[:, :],
                                          op0=ALU.mult, op1=ALU.add))
            step(dve.tensor_scalar(vareps[:, :], var[:, :], 1.0 / D, EPS, ALU.mult, ALU.add))
            dve.wait_ge(rooted, 1)
            step(dve.reciprocal(guess[:, :], root[:, :]))
            step(dve.tensor_tensor(total[:, :], guess[:, :], guess[:, :], ALU.mult))
            step(dve.tensor_tensor(diff[:, :], total[:, :], vareps[:, :], ALU.mult))
            step(dve.tensor_scalar(total[:, :], diff[:, :], -0.5, 1.5, ALU.mult, ALU.add))
            step(dve.tensor_tensor(rstd[:, :], guess[:, :], total[:, :], ALU.mult))
            with dve.Fori(0, TT) as t:
                dve.tensor_scalar(xn[:, t, :], x[:, t, :], mean[:, bass.ds(t, 1)], rstd[:, bass.ds(t, 1)],
                                  ALU.subtract, ALU.mult).then_inc(normed, 1)
            dve.wait_ge(normed, TT)
            step = chained(dve, chain)
            step(dve.tensor_reduce(amax[:, :], xn[:, :, :], AX.X, ALU.max, apply_absolute_value=True))
            step(dve.tensor_scalar(amaxc[:, :], amax[:, :], 1e-5, None, ALU.max))
            step(dve.reciprocal(rec[:, :], amaxc[:, :]))
            step(dve.tensor_scalar(qs[:, :], rec[:, :], 127.0, None, ALU.mult))
            step(dve.tensor_scalar(qr[:, :], amaxc[:, :], 1.0 / 127.0, None, ALU.mult))
            with dve.Fori(0, B) as b:
                for t in range(TB):
                    dve.wait_ge(q_sub, 2 * b)
                    dve.tensor_scalar(q1[:, t, :], xn[:, b * TB + t, :], qs[:, bass.ds(b * TB + t, 1)], MAGIC,
                                      ALU.mult, ALU.add).then_inc(q_done, 1)
                for t in range(TB):
                    dve.wait_ge(q_done, 4 * b + t + 1)
                    if t == 1:
                        dve.wait_ge(q_done, 4 * b + 3)
                    dve.tensor_scalar(q2[:, t, :], q1[:, t, :], MAGIC + 127.0, MAGIC - 128.0, ALU.min, ALU.max
                                      ).then_inc(q_done, 1)
                for t in range(TB):
                    dve.wait_ge(r_ready, b)
                    dve.tensor_scalar(rb[:, t, :], consts["ones"][:, :], qr[:, bass.ds(b * TB + t, 1)], None, ALU.mult
                                      ).then_inc(rb_done, 1)
                dve.wait_ge(r_ready, b + 1)
                dve.wait_ge(h_done, 8 * b)
                dve.tensor_scalar(rs[:, :], pr[:, 0:S], unit[:, 0:1], None, ALU.mult).then_inc(rs_done, 1)
                dve.wait_ge(rs_done, b + 1)
                for f in range(FT):
                    dve.wait_ge(h_ready, 8 * b + f + 1)
                    dve.wait_ge(y2_done, 8 * b)
                    dve.wait_ge(y0_done, 8 * b)
                    dve.tensor_tensor(h[:, f, 1:S + 1], ph[:, f % 4, 0:S], rs[:, :], ALU.mult).then_inc(h_done, 1)
                dve.wait_ge(silu_done, b)
                dve.wait_ge(pads, 2)
                for f in range(FT):
                    dve.wait_ge(h_done, 8 * b + f + 1)
                    dve.wait_ge(y0_done, 8 * b + f + 1)
                    dve.scalar_tensor_tensor(out=y1[:, f, :], in0=h[:, f, 0:S], scalar=cw[:, f, 0:1], in1=y0[:, f, :],
                                             op0=ALU.mult, op1=ALU.add).then_inc(y1_done, 1)
                for f in range(FT):
                    dve.wait_ge(y1_done, 8 * b + f + 1)
                    dve.scalar_tensor_tensor(out=y2[:, f, :], in0=h[:, f, 2:S + 2], scalar=cw[:, f, 2:3],
                                             in1=y1[:, f, :], op0=ALU.mult, op1=ALU.add).then_inc(y2_done, 1)
                dve.wait_ge(trans2, b + 1)
                dve.wait_ge(resid_done, 2 * b)
                chain_at = 5 * b
                dve.tensor_reduce(sax[:, :], pn[:, :, :], AX.X, ALU.max, apply_absolute_value=True
                                  ).then_inc(red_done, 1)
                dve.wait_ge(red_done, chain_at + 1)
                dve.tensor_scalar(saxc[:, :], sax[:, :], 1e-5, None, ALU.max).then_inc(red_done, 1)
                dve.wait_ge(red_done, chain_at + 2)
                dve.reciprocal(srec[:, :], saxc[:, :]).then_inc(red_done, 1)
                dve.wait_ge(red_done, chain_at + 3)
                dve.tensor_scalar(sqs[:, :], srec[:, :], 127.0, None, ALU.mult).then_inc(red_done, 1)
                dve.tensor_scalar(sqr[:, :], saxc[:, :], 1.0 / 127.0, unit[:, 1:2], ALU.mult, ALU.mult
                                  ).then_inc(red_done, 1)
                dve.wait_ge(red_done, chain_at + 5)
                for t in range(TB):
                    dve.wait_ge(s2_done, 2 * b)
                    dve.tensor_scalar(s1[:, t, :], pn[:, t, :], sqs[:, t:t + 1], MAGIC, ALU.mult, ALU.add
                                      ).then_inc(s1_done, 1)
                for t in range(TB):
                    dve.wait_ge(s1_done, 2 * b + t + 1)
                    dve.wait_ge(sq_done, 2 * b)
                    dve.tensor_scalar(s2[:, t, :], s1[:, t, :], MAGIC + 127.0, MAGIC - 128.0, ALU.min, ALU.max
                                      ).then_inc(s2_done, 1)
                dve.wait_ge(trans3, b + 1)
                dve.wait_ge(o_ready, b)
                dve.tensor_copy(sqT[:, :, :], pb).then_inc(sqT_out, 1)
                for t in range(TB):
                    xs = x[:, b * TB + t, :]
                    dve.wait_ge(o_ready, b + 1)
                    dve.scalar_tensor_tensor(out=xs, in0=po[:, t, :], scalar=sqr[:, t:t + 1], in1=xs,
                                             op0=ALU.mult, op1=ALU.add).then_inc(resid_done, 1)

        @block.scalar
        def _(act):
            act.wait_ge(comb, 7)
            act.activation(root[:, :], vareps[:, :], ACT.Sqrt).then_inc(rooted, 1)
            with act.Fori(0, B) as b:
                act.wait_ge(q_done, 4 * b + 4)
                act.wait_ge(trans1, b)
                act.activation(xq[:, :, :], q2[:, :, :], ACT.Copy, bias=-MAGIC).then_inc(q_sub, 2)
                act.wait_ge(trans1, b + 1)
                act.wait_ge(h_ready, 8 * b)
                act.activation(xqT[:, :, :], ptr[:, :, :], ACT.Copy).then_inc(xqT_out, 1)
                for f in range(FT):
                    act.wait_ge(h_done, 8 * b + f + 1)
                    act.wait_ge(y1_done, 8 * b)
                    act.activation(y0[:, f, :], h[:, f, 1:S + 1], ACT.Identity, bias=cb[:, f:f + 1],
                                   scale=cw[:, f, 1:2]).then_inc(y0_done, 1)
                act.wait_ge(y2_done, 8 * b + 8)
                act.wait_ge(trans2, b)
                act.activation(sT[:, :, :], y2[:, :, :], ACT.Silu).then_inc(silu_done, 1)
                act.wait_ge(s2_done, 2 * b + 2)
                act.wait_ge(trans3, b)
                act.activation(sq[:, :, :], s2[:, :, :], ACT.Copy, bias=-MAGIC).then_inc(sq_done, 2)

        @block.tensor
        def _(pe):
            pe.wait_ge(asum_done, 2)
            pe.matmul(pr[:, 0:2], consts["ones"][:, :], asum[:, :], start=True, stop=True).then_inc(sum_ready, 1)
            pe.wait_ge(wchain, 8)
            with pe.Fori(0, B) as b:
                pe.wait_ge(rb_done, 2 * b + 2)
                pe.wait_ge(rs_done, b)
                for t in range(TB):
                    mm = pe.matmul(pr[:, t * P:(t + 1) * P], rb[:, t, :], ident[:, :], start=True, stop=True)
                mm.then_inc(r_ready, 1)
                pe.wait_ge(q_sub, 2 * b + 2)
                pe.wait_ge(xqT_out, b)
                for k in range(DK):
                    for t in range(TB):
                        mm = pe.transpose(ptr[:, k, t * P:(t + 1) * P], xq[:, t, k * P:(k + 1) * P],
                                          consts["identb"][:, :])
                mm.then_inc(trans1, 1)
                pe.wait_ge(xqT_out, b + 1)
                pe.wait_ge(sqT_out, b)
                for f in range(FT):
                    if f >= 4:
                        pe.wait_ge(h_done, 8 * b + f - 3)
                    for k in range(DK):
                        mm = pe.matmul(ph[:, f % 4, 0:S], w1q[:, k, f * P:(f + 1) * P], xqT[:, k, :],
                                       start=(k == 0), stop=(k == DK - 1))
                    mm.then_inc(h_ready, 1)
                pe.wait_ge(silu_done, b + 1)
                for t in range(TB):
                    for f in range(FT):
                        mm = pe.transpose(pn[:, t, f * P:(f + 1) * P], sT[:, f, t * P:(t + 1) * P], ident[:, :])
                mm.then_inc(trans2, 1)
                pe.wait_ge(sq_done, 2 * b + 2)
                pe.wait_ge(s1_done, 2 * b + 2)
                for f in range(FT):
                    for t in range(TB):
                        mm = pe.transpose(pb[:, f, t * P:(t + 1) * P], sq[:, t, f * P:(f + 1) * P],
                                          consts["identb"][:, :])
                mm.then_inc(trans3, 1)
                pe.wait_ge(sqT_out, b + 1)
                pe.wait_ge(resid_done, 2 * b)
                for t in range(TB):
                    for f in range(FT):
                        mm = pe.matmul(po[:, t, :], sqT[:, f, t * P:(t + 1) * P], w2q[:, f, :],
                                       start=(f == 0), stop=(f == FT - 1))
                mm.then_inc(o_ready, 1)


def build(nc, io, out, sublayers=8, first=0):
    with ExitStack() as top:
        def sb(name, shape, dt=F32):
            return top.enter_context(nc.sbuf_tensor(name, shape, dt))

        x, xt = sb("x", [P, TT, D]), sb("xt", [P, DK, B * S])
        xn = sb("xn", [P, TT, D])
        logits, hot1, hot2 = (sb(n, [P, TT, E]) for n in ("logits", "hot1", "hot2"))
        share1, share2 = sb("share1", [P, TT]), sb("share2", [P, TT])
        dest = sb("dest", [P, 2, TT], U32)
        NT0, NT1 = TT + E - 1, 2 * TT + E - 1
        table = sb("table", [1, NT1 + 2], I32)
        xs0, ys0 = (nc.dram_tensor(n, (NT0 * P, D), F32).ap() for n in ("sorted_x0", "sorted_y0"))
        xs1, ys1 = (nc.dram_tensor(n, (NT1 * P, D), F32).ap() for n in ("sorted_x1", "sorted_y1"))
        rw0, rw1 = sb("rw0", [P, DK, E]), sb("rw1", [P, DK, E])
        ident, identb = sb("ident", [P, P]), sb("identb", [P, P], BF16)
        ones = sb("ones", [P, P])
        trif, tri = sb("trif", [P, 2, P]), sb("tri", [P, 2, P], BF16)
        x_loaded, consts_loaded, consts_made = (top.enter_context(nc.semaphore(n)) for n in (
            "x_loaded", "consts_loaded", "consts_made"))
        stages = Stages(nc)
        consts = {"ident": ident, "identb": identb, "ones": ones, "tri": tri}

        with nc.Block() as block:
            @block.sync
            def _(sp):
                sp.dma_start(ident[:, :], io["ident"]).then_inc(consts_loaded, 16)
                sp.dma_start(trif[:, :, :], io["tri"].rearrange("t p n -> p t n")).then_inc(consts_loaded, 16)
                sp.dma_start(rw0[:, :, :], io["f0_rw"].rearrange("(k p) e -> p k e", p=P)).then_inc(consts_loaded, 16)
                sp.dma_start(rw1[:, :, :], io["f1_rw"].rearrange("(k p) e -> p k e", p=P)).then_inc(consts_loaded, 16)
                sp.dma_start(x[:, :, :], io["x"].rearrange("b (t p) d -> p (b t) d", p=P)).then_inc(x_loaded, 16)
                sp.wait_ge(consts_loaded, 64)
                sp.wait_ge(x_loaded, 16)

            @block.vector
            def _(dve):
                dve.memset(ones[:, :], 1.0).then_inc(consts_made, 1)
                dve.wait_ge(consts_loaded, 64)
                dve.tensor_copy(identb[:, :], ident[:, :]).then_inc(consts_made, 1)
                dve.tensor_scalar(tri[:, :, :], trif[:, :, :], NEG, None, ALU.mult).then_inc(consts_made, 1)

        if first <= 0 < sublayers:
            layer_norm(nc, stages, "n0_", x, xt, ident, first=x_loaded)
            attention0(nc, stages, x, xt, io, consts)
        if first <= 1 < sublayers:
            layer_norm(nc, stages, "n1_", x, xt, ident, router=(rw0, logits, xn))
            gates0(nc, stages, logits, hot1, share1, io)
            dispatch(nc, stages, "d0_", xn, [hot1], dest[:, 0:1, :], table[:, 0:NT0 + 2], NT0, xs0, io, consts)
            expert_tiles(nc, stages, "f0_", xs0, ys0, table, NT0, io, consts, gated=False)
            combine(nc, stages, "c0_", x, ys0, dest, [share1])
        if first <= 2 < sublayers:
            layer_norm(nc, stages, "n2_", x, xt, ident)
            attention1(nc, stages, x, xt, io, consts)
        if first <= 3 < sublayers:
            layer_norm(nc, stages, "n3_", x, xt, ident, router=(rw1, logits, xn))
            gates1(nc, stages, logits, hot1, hot2, share1, share2, io)
            dispatch(nc, stages, "d1_", xn, [hot1, hot2], dest, table, NT1, xs1, io, consts)
            expert_tiles(nc, stages, "f1_", xs1, ys1, table, NT1, io, consts, gated=True)
            combine(nc, stages, "c1_", x, ys1, dest, [share1, share2])
        if first <= 4 < sublayers:
            layer_norm(nc, stages, "n4_", x, xt, ident)
            linear_attention(nc, stages, x, xt, io)
        if first <= 5 < sublayers:
            layer_norm(nc, stages, "n5_", x, xt, ident)
            scaled_linear(nc, stages, x, xt, io)
        if first <= 6 < sublayers:
            layer_norm(nc, stages, "n6_", x, xt, ident)
            attention3(nc, stages, x, xt, io, consts)
        if sublayers > 7:
            bit_ffn(nc, stages, x, ident, io, consts, out)
        else:
            stored = top.enter_context(nc.semaphore("stored"))
            with nc.Block() as block:
                @block.sync
                def _(sp):
                    sp.dma_start(out.rearrange("b (t p) d -> p (b t) d", p=P), x[:, :, :]).then_inc(stored, 16)
                    sp.wait_ge(stored, 16)


def lay_out(i):
    import numpy as np

    def t(a):
        return np.ascontiguousarray(np.swapaxes(a, -1, -2))

    def rows(a):
        return np.ascontiguousarray(np.broadcast_to(a, (P, a.shape[0])))

    def padded(a):
        out = np.zeros(a.shape[:-1] + (H, 32), np.float32)
        out[..., :D0] = a.reshape(a.shape[:-1] + (H, D0))
        return out

    f = {k: np.asarray(v) for k, v in i.items()}
    io = {"x": f["x"], "ctx": f["ctx_1024"], "ctxT": t(f["ctx_1024"]),
          "mask": f["mask_BxSxS2_ik1"], "maskT": t(f["mask_BxSxS2_ik1"])}
    for n in "qkv":
        io["a0_w" + n] = t(f["L0_xattn_W" + n]).reshape(DK, P, D)
    for n in "qk":
        io["a0_w" + n] = t(io["a0_w" + n].reshape(D, DK, P // D0, D0)).reshape(DK, P, D)
    io["a0_bqk"] = np.stack([t(t(f["L0_xattn_b" + n].reshape(DK, P // D0, D0)).reshape(DK, P)) for n in "qk"], 1)
    io["a0_bv"] = rows(f["L0_xattn_bv"])
    wo = padded(f["L0_xattn_Wo"])
    wo[:, 0, D0] = f["L0_xattn_bo"]
    io["a0_wo"] = t(wo.reshape(D, H * 32)).reshape(H * 32 // P, P, D)
    sel = np.zeros((4, 32, 4, 32), np.float32)
    for g in range(4):
        sel[g, D0, g, :] = 1.0
    io["a0_sel"] = sel.reshape(P, P)
    for n in "qkv":
        io["a1_w" + n] = t(f["L1_xattn_w_" + n]).reshape(DK, P, H * D1)
    io["a1_wo"] = t(f["L1_xattn_w_o"]).reshape(H * D1 // P, P, D)
    sel = np.zeros((D1 + 1, D1), np.float32)
    sel[D1] = 1.0
    io["a1_sel"] = sel
    io["ident"] = np.eye(P, dtype=np.float32)
    io["tri"] = np.stack([np.triu(np.ones((P, P), np.float32), 1), np.tril(np.ones((P, P), np.float32), -1)])
    io["below"] = np.triu(np.ones((P, P), np.float32), 1)
    io["thr"] = rows(np.arange(TT, dtype=np.float32) * P)
    io["index"] = rows(np.arange(2 * TT + E, dtype=np.float32))
    io["rank"] = rows(np.arange(E, 0, -1).astype(np.float32))
    io["f0_rw"], io["f0_rb"] = f["L0_ffn_router_W"], rows(f["L0_ffn_router_b"])
    io["f0_w1"], io["f0_b1"] = f["L0_ffn_W1"], f["L0_ffn_b1"].reshape(E, FT, P).transpose(2, 0, 1)
    io["f0_w2"], io["f0_b2"] = f["L0_ffn_W2"], f["L0_ffn_b2"][None]
    io["f1_rw"] = t(f["L1_ffn_gate_w"])
    io["f1_w1"], io["f1_w3"], io["f1_w2"] = t(f["L1_ffn_w1"]), t(f["L1_ffn_w3"]), t(f["L1_ffn_w2"])
    io["f2_cb"], io["f2_scb"], io["f2_bias"] = t(f["L2_ffn_CB"]), rows(f["L2_ffn_SCB"]), rows(f["L2_ffn_bias"])
    for n in "qkv":
        io["a3_w" + n] = t(f["L3_xattn_W" + n])
    io["a3_bq"], io["a3_bk"] = (t(f["L3_xattn_b" + n].reshape(DK, P)) for n in "qk")
    io["a3_bv"] = f["L3_xattn_bv"][None]
    io["f3_w1"], io["f3_w2"] = t(f["L3_ffn_w1"]), t(f["L3_ffn_w2"])
    io["f3_cw"], io["f3_cb"] = f["L3_ffn_conv_w"].reshape(F, 3), t(f["L3_ffn_conv_b"].reshape(FT, P))
    return {k: np.ascontiguousarray(v) for k, v in io.items()}


def kernel(**inputs):
    import concourse.bacc as bacc
    from concourse.bass_utils import run_bass_kernel_spmd

    nc = bacc.Bacc("TRN2", target_bir_lowering=False, num_devices=1)
    arrays = lay_out(inputs)
    io = {k: nc.dram_tensor("in_" + k, v.shape, mybir.dt.from_np(v.dtype), kind="ExternalInput").ap()
          for k, v in arrays.items()}
    out = nc.dram_tensor("out", (B, S, D), F32, kind="ExternalOutput").ap()
    build(nc, io, out)
    r = run_bass_kernel_spmd(nc, [{"in_" + k: v for k, v in arrays.items()}], core_ids=[0])
    return r.results[0]["out"]
```

```python
from contextlib import ExitStack, contextmanager

import concourse.bass as bass
from concourse import mybir

F32 = mybir.dt.float32
F32R = mybir.dt.float32r
BF16 = mybir.dt.bfloat16
I32 = mybir.dt.int32
U32 = mybir.dt.uint32
ALU = mybir.AluOpType
ACT = mybir.ActivationFunctionType
AX = mybir.AxisListType

P = 128
B, S, D = 8, 256, 256
DK = D // P
TT = B * S // P
TB = S // P
H = 16
D0, D1 = D // H, 64
E, F = 8, 1024
FT = F // P
EPS = 1e-5
NEG = -float(2 ** 100)
MAGIC = 1.5 * 2 ** 23


class Stages:

    def __init__(self, nc):
        self.nc, self.ours, self.cleared = nc, [], []

    def for_indirect(self, name):
        return self.nc.alloc_semaphore(name=name)

    def semaphore(self, name):
        self.ours.append(self.nc.alloc_semaphore(name=name))
        return self.ours[-1]

    @contextmanager
    def stage(self):
        with ExitStack() as ctx:
            yield ctx
        for s in self.cleared:
            self.nc.release_semaphore(s)
        for s in self.ours:
            self.nc.gpsimd.sem_clear(s)
        self.cleared, self.ours = self.ours, []


def layer_norm(nc, top, tag, x, xt, ident, first=None, router=None):
    SLOTS = 2
    with top.stage() as ctx:
        def sb(name, shape, dt=F32):
            return ctx.enter_context(nc.sbuf_tensor(tag + name, shape, dt))

        stats = sb("stats", [P, TT, 6])
        total, diff, m2, mean, diff2, var, vareps, rstd, root, guess = (
            sb(n, [P, TT]) for n in ("total", "diff", "m2", "mean", "diff2", "var", "vareps", "rstd", "root", "guess"))
        xn = router[2] if router else sb("xn", [P, SLOTS * TB, D])
        tp = ctx.enter_context(nc.psum_tensor(tag + "tp", [P, SLOTS, DK, S], F32))
        lg = ctx.enter_context(nc.psum_tensor(tag + "lg", [P, 512], F32)) if router else None
        stats_done, comb, rooted, normed, transposed, evacuated, logits_done, logits_out, zeroed = (
            top.semaphore(tag + n) for n in ("stats_done", "comb", "rooted", "normed", "transposed", "evacuated",
                                             "logits_done", "logits_out", "zeroed"))
        block = ctx.enter_context(nc.Block())

        if router:
            @block.sync
            def _(sp):
                rows = router[3].rearrange("(n p) d -> p n d", p=P)
                sp.dma_start(rows, router[4][:, :].unsqueeze(1).to_broadcast([P, rows.shape[1], D])
                             ).then_inc(zeroed, 16)
                sp.wait_ge(zeroed, 16)

        @block.vector
        def _(dve):
            if first:
                dve.wait_ge(first, 16)
            for t in range(TT):
                dve.bn_stats(stats[:, t, :], x[:, t, :]).then_inc(stats_done, 1)
            dve.wait_ge(stats_done, TT)
            dve.tensor_tensor(total[:, :], stats[:, :, 1], stats[:, :, 4], ALU.add).then_inc(comb, 1)
            dve.tensor_tensor(diff[:, :], stats[:, :, 1], stats[:, :, 4], ALU.subtract).then_inc(comb, 1)
            dve.tensor_tensor(m2[:, :], stats[:, :, 2], stats[:, :, 5], ALU.add).then_inc(comb, 1)
            dve.wait_ge(comb, 2)
            dve.tensor_tensor(diff2[:, :], diff[:, :], diff[:, :], ALU.mult).then_inc(comb, 1)
            dve.wait_ge(comb, 4)
            dve.scalar_tensor_tensor(out=var[:, :], in0=diff2[:, :], scalar=D / 4.0, in1=m2[:, :],
                                     op0=ALU.mult, op1=ALU.add).then_inc(comb, 1)
            dve.wait_ge(comb, 5)
            dve.tensor_scalar(vareps[:, :], var[:, :], 1.0 / D, EPS, ALU.mult, ALU.add).then_inc(comb, 1)
            dve.tensor_scalar(mean[:, :], total[:, :], 0.5, None, ALU.mult).then_inc(comb, 1)
            dve.wait_ge(comb, 7)
            dve.wait_ge(rooted, 1)
            dve.reciprocal(guess[:, :], root[:, :]).then_inc(comb, 1)
            dve.wait_ge(comb, 8)
            dve.tensor_tensor(total[:, :], guess[:, :], guess[:, :], ALU.mult).then_inc(comb, 1)
            dve.wait_ge(comb, 9)
            dve.tensor_tensor(diff[:, :], total[:, :], vareps[:, :], ALU.mult).then_inc(comb, 1)
            dve.wait_ge(comb, 10)
            dve.tensor_scalar(total[:, :], diff[:, :], -0.5, 1.5, ALU.mult, ALU.add).then_inc(comb, 1)
            dve.wait_ge(comb, 11)
            dve.tensor_tensor(rstd[:, :], guess[:, :], total[:, :], ALU.mult).then_inc(comb, 1)
            dve.wait_ge(comb, 12)
            for b in range(B):
                if b >= SLOTS and not router:
                    dve.wait_ge(transposed, b - SLOTS + 1)
                for t in range(b * TB, (b + 1) * TB):
                    dve.tensor_scalar(xn[:, t if router else t % (SLOTS * TB), :], x[:, t, :], mean[:, t:t + 1],
                                      rstd[:, t:t + 1], ALU.subtract, ALU.mult).then_inc(normed, 1)

        @block.tensor
        def _(pe):
            def logits(b):
                pe.wait_ge(evacuated, b + 1)
                for t in range(b * TB, (b + 1) * TB):
                    for k in range(DK):
                        mm = pe.matmul(lg[:, t * E:(t + 1) * E], xt[:, k, t * P:(t + 1) * P], router[0][:, k, :],
                                       start=(k == 0), stop=(k == DK - 1))
                return mm

            for b in range(B):
                if b >= SLOTS:
                    pe.wait_ge(evacuated, b - SLOTS + 1)
                for t in range(TB):
                    pe.wait_ge(normed, b * TB + t + 1)
                    row = b * TB + t
                    for k in range(DK):
                        mm = pe.transpose(tp[:, b % SLOTS, k, t * P:(t + 1) * P],
                                          xn[:, row if router else row % (SLOTS * TB), k * P:(k + 1) * P], ident[:, :])
                mm.then_inc(transposed, 1)
                if router and b >= 1:
                    logits(b - 1)
            if router:
                logits(B - 1).then_inc(logits_done, 1)

        @block.scalar
        def _(act):
            act.wait_ge(comb, 6)
            act.activation(root[:, :], vareps[:, :], ACT.Sqrt).then_inc(rooted, 1)
            for b in range(B):
                act.wait_ge(transposed, b + 1)
                act.activation(xt[:, :, b * S:(b + 1) * S], tp[:, b % SLOTS, :, :], ACT.Copy).then_inc(evacuated, 1)
            if router:
                act.wait_ge(logits_done, 1)
                act.activation(router[1][:, :, :], lg[:, 0:TT * E].rearrange("p (t e) -> p t e", t=TT), ACT.Copy
                               ).then_inc(logits_out, 1)


def attention0(nc, top, x, xt, io, consts):
    G, NG, W = 4, H // 4, 32
    U = H // 2
    PARTS = ((0, 0, 0, 1, 1, 2), (0, 1, 2, 0, 1, 0))
    R = len(PARTS[0]) * D0
    LAND = 16 * 2 * len(PARTS[0])
    HB = P // D0
    with top.stage() as ctx:
        def sb(name, shape, dt=F32):
            return ctx.enter_context(nc.sbuf_tensor("a0_" + name, shape, dt))

        wq, wk, wv = (sb(n, [P, DK, D]) for n in ("wq", "wk", "wv"))
        wo = sb("wo", [P, NG, D])
        bqk = sb("bqk", [P, 2, DK])
        bv = sb("bv", [P, D])
        sel = sb("sel", [P, P])
        ctxT = sb("ctxT", [P, 2, DK, S])
        mask, maskT = sb("mask", [P, TB, S], I32), sb("maskT", [P, TB, S], I32)
        neg, negT = sb("neg", [P, 2, TB, S], BF16), sb("negT", [P, 2, TB, S], BF16)
        part = sb("part", [P, 3, 2, DK, S], BF16)
        rest = sb("rest", [P, 2, DK, S])
        qs, ks = sb("qs", [P, 2, H, S], BF16), sb("ks", [P, 2, H, S], BF16)
        V = sb("V", [P, 2, TB, H, W])
        top_s = sb("top_s", [P, TB, H])
        mpart, mrest = sb("mpart", [H, 3, S], BF16), sb("mrest", [H, S])
        pT = sb("pT", [P, 2, 2, TB, S])
        sums, recip = sb("sums", [P, NG * S // W]), sb("recip", [P, NG * S // W])
        rrow = sb("rrow", [P, NG, S])
        oraw, onorm = sb("oraw", [P, NG, S]), sb("onorm", [P, NG, S])
        ps = ctx.enter_context(nc.psum_tensor("a0_ps", [P, 8, 512], F32))
        O = ps[:, 4:6, :].rearrange("p a (c n) -> p (a c) n", c=2)

        (weights, ctx_in0, ctx_in1, mask_in, ones_set, q_proj, k_proj, v_proj, hi_done, rest_done, mid_done, lo_done,
         stacked, v_out, neg_ready, s_ready, max_done, mt_ready, mhi_done, mrest_done, mmid_done, mlo_done,
         mrow_landed, st_ready, exp_done, pv_done, o_out, sums_landed, recip_landed, l_ready, recip_done, norm_done,
         wo_ready, resid_done) = (
             top.semaphore("a0_" + n) for n in (
                 "weights", "ctx_in0", "ctx_in1", "mask_in", "ones_set", "q_proj", "k_proj", "v_proj", "hi_done",
                 "rest_done", "mid_done", "lo_done", "stacked", "v_out", "neg_ready", "s_ready", "max_done",
                 "mt_ready", "mhi_done", "mrest_done", "mmid_done", "mlo_done", "mrow_landed", "st_ready",
                 "exp_done", "pv_done", "o_out", "sums_landed", "recip_landed", "l_ready", "recip_done", "norm_done",
                 "wo_ready", "resid_done"))
        gate, gate_set = sb("gate", [1, 4]), top.semaphore("a0_gate_set")
        k_stacked = top.for_indirect("a0_k_stacked")
        ctx_in = (ctx_in0, ctx_in1)
        block = ctx.enter_context(nc.Block())

        def to_stack(engine, w, n, s):
            for t, which in enumerate(PARTS[w]):
                if which == n:
                    for k in range(DK):
                        engine.dma_start((qs, ks)[w][t * D0:(t + 1) * D0, s, k * HB:(k + 1) * HB, :],
                                         part[:, n, w, k, :]).then_inc((stacked, k_stacked)[w], 16)

        def every_batch(engine, body):
            with engine.Fori(0, B // 2 - 1) as pair:
                body(pair * 2, 0, pair, False)
                body(pair * 2 + 1, 1, pair, False)
            body(B - 2, 0, B // 2 - 1, False)
            body(B - 1, 1, B // 2 - 1, True)

        @block.sync
        def _(sp):
            sp.sem_inc(stacked, 16)
            sp.sem_inc(mrow_landed, 16)

            def load(b, s):
                sp.wait_ge(v_proj, b + 1)
                sp.dma_start(ctxT[:, s, :, :], io["ctxT"][bass.ds(b, 1)].rearrange("b (k p) s -> p (b k) s", p=P)
                             ).then_inc(ctx_in[s], 16)
                sp.wait_ge(neg_ready, b + 1)
                sp.dma_start(mask[:, :, :], io["mask"][bass.ds(b, 1)].rearrange("b (t p) s -> p (b t) s", p=P)
                             ).then_inc(mask_in, 16)
                sp.dma_start(maskT[:, :, :], io["maskT"][bass.ds(b, 1)].rearrange("b (t p) s -> p (b t) s", p=P)
                             ).then_inc(mask_in, 16)

            def stack(b, s):
                for n, ready in enumerate((hi_done, mid_done, lo_done)):
                    sp.wait_ge(ready, b * 2 + 1)
                    to_stack(sp, 0, n, s)

            def shift_rows(b, s):
                sp.wait_ge(mlo_done, b + 1)
                for n in range(3):
                    sp.dma_start(qs[R + n:R + n + 1, s, :, :], mpart[:, n, :]).then_inc(mrow_landed, 16)

            def turn_sums(b):
                sp.wait_ge(o_out, b * 2 + 2)
                for g in range(G):
                    sp.dma_start(sums[g * W:(g + 1) * W, :], oraw[g * W + D0:g * W + D0 + 1, :, :]
                                 ).then_inc(sums_landed, 16)
                sp.wait_ge(recip_done, b + 1)
                for g in range(G):
                    sp.dma_start(rrow[g * W + D0:g * W + D0 + 1, :, :], recip[g * W:(g + 1) * W, :]
                                 ).then_inc(recip_landed, 16)

            def feed(b, s):
                sp.wait_ge(pv_done, b * U + 2)
                stack(b + 1, 1 - s)
                turn_sums(b)
                shift_rows(b + 1, 1 - s)

            for dst, name in ((wq, "a0_wq"), (wk, "a0_wk"), (wv, "a0_wv"), (wo, "a0_wo")):
                sp.dma_start(dst[:, :, :], io[name].rearrange("k p n -> p k n")).then_inc(weights, 16)
            sp.dma_start(bqk[:, :, :], io["a0_bqk"]).then_inc(weights, 16)
            for dst, name in ((bv, "a0_bv"), (sel, "a0_sel")):
                sp.dma_start(dst[:, :], io[name]).then_inc(weights, 16)
            load(0, 0)
            load(1, 1)
            stack(0, 0)
            shift_rows(0, 0)
            with sp.Fori(0, B // 2 - 1) as pair:
                for s in range(2):
                    load(pair * 2 + (2 + s), s)
                    feed(pair * 2 + s, s)
            feed(B - 2, 0)
            turn_sums(B - 1)

        @block.tensor
        def _(pe):
            pe.sem_inc(v_proj, 2)
            pe.sem_inc(pv_done, 2)
            pe.sem_inc(l_ready, 1)
            pe.sem_inc(wo_ready, 1)
            pe.wait_ge(weights, 16 * 7)

            def project(b, s, half, left=1):
                pe.wait_ge(ctx_in[s], half * 16 + 16)
                pe.wait_ge(norm_done, left)
                for n, (w, src, done) in enumerate(((wq, xt, q_proj), (wk, ctxT, k_proj))):
                    for c in range(DK):
                        for k in range(DK):
                            mm = pe.matmul(ps[:, 6 + n, c * S:(c + 1) * S], w[:, k, c * P:(c + 1) * P],
                                           xt[:, k, bass.ds(b * S, S)] if src is xt else ctxT[:, s, k, :],
                                           start=(k == 0), stop=(k == DK - 1))
                    mm.then_inc(done, 1)
                pe.wait_ge(rest_done, b * 2 + 1)
                for t in range(TB):
                    for k in range(DK):
                        mm = pe.matmul(ps[:, 6, t * S:(t + 1) * S], ctxT[:, s, k, t * P:(t + 1) * P], wv[:, k, :],
                                       start=(k == 0), stop=(k == DK - 1))
                mm.then_inc(v_proj, 1)

            def scores(b, s, before):
                pe.wait_ge(stacked, (b + 1) * LAND + 16)
                pe.wait_ge(k_stacked, (b + 1) * LAND)
                pe.wait_ge(neg_ready, b + 2)
                pe.wait_ge(ones_set, 5)
                for u in range(U):
                    if u >= 2:
                        pe.wait_ge(max_done, b * U + (u - 1))
                    elif before is not None:
                        pe.wait_ge(exp_done, before * U + (U - 1 + u))
                    for j in range(2):
                        h, bank = 2 * u + j, ps[:, 2 * (u % 2) + j, :]
                        for t in range(TB):
                            pe.matmul(bank[:, t * S:(t + 1) * S], qs[0:R, s, h, t * P:(t + 1) * P], ks[0:R, s, h, :],
                                      start=True, stop=False)
                            mm = pe.matmul(bank[:, t * S:(t + 1) * S], consts["identb"][:, :], neg[:, s, t, :],
                                           start=False, stop=True)
                    mm.then_inc(s_ready, 1)

            def turn_maxima(b):
                pe.wait_ge(max_done, b * U + U)
                for t in range(TB):
                    mm = pe.transpose(ps[0:H, 4, t * P:(t + 1) * P], top_s[:, t, :], consts["ident"][:, :])
                mm.then_inc(mt_ready, 1)

            def weigh(b, s):
                pe.wait_ge(mrow_landed, (b + 1) * 48 + 16)
                pe.wait_ge(v_out, b + 1)
                for u in range(U + 1):
                    if u < U:
                        if u >= 2:
                            pe.wait_ge(exp_done, b * U + (u - 1))
                        else:
                            pe.wait_ge(max_done, b * U + (U - 1 + u))
                        for j in range(2):
                            h, bank = 2 * u + j, ps[:, 2 * (u % 2) + j, :]
                            for t in range(TB):
                                pe.matmul(bank[:, t * S:(t + 1) * S], ks[0:R + 3, s, h, t * P:(t + 1) * P],
                                          qs[0:R + 3, s, h, :], start=True, stop=False)
                                mm = pe.matmul(bank[:, t * S:(t + 1) * S], consts["identb"][:, :], negT[:, s, t, :],
                                               start=False, stop=True)
                        mm.then_inc(st_ready, 1)
                    if u > 0:
                        m = u - 1
                        n, g0 = m // 2, 2 * (m % 2)
                        pe.wait_ge(exp_done, b * U + (m + 1))
                        if m == U // 2:
                            pe.wait_ge(resid_done, b + 1)
                        for t in range(TB):
                            for j in range(2):
                                mm = pe.matmul(O[W * (g0 + j):W * (g0 + j + 1), n, :], V[:, s, t, 4 * n + g0 + j, :],
                                               pT[:, m % 2, j, t, :], start=(t == 0), stop=(t == TB - 1))
                        mm.then_inc(pv_done, 1)

            def spread_sums(b):
                pe.wait_ge(recip_landed, b * (16 * G) + 16 * G)
                for c in range(2):
                    pe.matmul(ps[:, 6 + c, :], sel[:, :], rrow[:, 2 * c:2 * c + 2, :].rearrange("p a n -> p (a n)"),
                              start=True, stop=True).then_inc(l_ready, 1)

            def output(b):
                pe.wait_ge(norm_done, b * 2 + 3)
                for t in range(TB):
                    for n in range(NG):
                        mm = pe.matmul(ps[:, 5, t * S:(t + 1) * S], onorm[:, n, t * P:(t + 1) * P], wo[:, n, :],
                                       start=(n == 0), stop=(n == NG - 1))
                mm.then_inc(wo_ready, 1)

            def batch(b, s, half, last):
                if not last:
                    project(b + 1, 1 - s, half + s, b * 2 + 1)
                weigh(b, s)
                if not last:
                    scores(b + 1, 1 - s, b)
                pe.wait_ge(v_out, b + 1 if last else b + 2)
                pe.wait_ge(lo_done, b * 2 + 2 if last else b * 2 + 4)
                spread_sums(b)
                if not last:
                    turn_maxima(b + 1)
                output(b)

            project(0, 0, 0)
            scores(0, 0, None)
            turn_maxima(0)
            every_batch(pe, batch)

        @block.gpsimd
        def _(pool):
            def stack(b, s):
                for n, ready in enumerate((hi_done, mid_done, lo_done)):
                    pool.wait_ge(gate_set, b * 3 + (n + 1))
                    pool.wait_ge(ready, b * 2 + 2)
                    pool.tensor_tensor(gate[:, n:n + 1], gate[:, 3:4], gate[:, 3:4], ALU.add).then_inc(gate_set, 1)
                    to_stack(pool, 1, n, s)

            pool.memset(gate[:, :], 0.0).then_inc(gate_set, 1)
            stack(0, 0)

            def batch(b, s, half, last):
                if not last:
                    pool.wait_ge(pv_done, b * U + 2)
                    stack(b + 1, 1 - s)

            every_batch(pool, batch)

        @block.scalar
        def _(act):
            act.wait_ge(weights, 16 * 7)

            def split(b, first=False):
                if not first:
                    act.wait_ge(stacked, b * LAND + 16)
                    act.wait_ge(k_stacked, b * LAND)
                for n, done in enumerate((q_proj, k_proj)):
                    act.wait_ge(done, b + 1)
                    for c in range(DK):
                        a = act.activation(part[:, 0, n, c, :], ps[:, 6 + n, c * S:(c + 1) * S], ACT.Identity,
                                           bias=bqk[:, n, c:c + 1])
                    a.then_inc(hi_done, 1)
                for n in range(2):
                    act.wait_ge(rest_done, b * 2 + (n + 1))
                    act.activation(part[:, 1, n, :, :], rest[:, n, :, :], ACT.Copy).then_inc(mid_done, 1)

            def split_maxima(b):
                act.wait_ge(mt_ready, b + 1)
                act.wait_ge(mrow_landed, b * 48 + 16)
                act.mul(mpart[:, 0, :], ps[0:H, 4, 0:S], -1.0).then_inc(mhi_done, 1)
                act.wait_ge(mrest_done, b + 1)
                act.activation(mpart[:, 1, :], mrest[:, :], ACT.Copy).then_inc(mmid_done, 1)

            def batch(b, s, half, last):
                if not last:
                    split(b + 1)
                for u in range(U):
                    act.wait_ge(st_ready, b * U + (u + 1))
                    act.wait_ge(pv_done, b * U + (u + 1))
                    act.activation(pT[:, u % 2, :, :, :].rearrange("p j t n -> p j (t n)"),
                                   ps[:, 2 * (u % 2):2 * (u % 2) + 2, :], ACT.Exp,
                                   scale=float(D0) ** -0.5).then_inc(exp_done, 1)
                if not last:
                    split_maxima(b + 1)

            split(0, first=True)
            split_maxima(0)
            every_batch(act, batch)

        @block.vector
        def _(dve):
            dve.sem_inc(neg_ready, 1)
            dve.sem_inc(norm_done, 1)
            dve.sem_inc(resid_done, 1)
            for s in range(2):
                dve.memset(V[:, s, :, :, :], 0.0).then_inc(ones_set, 1)
            dve.memset(ks[R:P, :, :, :], 1.0).then_inc(ones_set, 1)
            dve.memset(rrow[:, :, :], 0.0).then_inc(ones_set, 1)
            dve.wait_ge(ones_set, 4)
            dve.memset(V[:, :, :, :, D0:D0 + 1].rearrange("p s t h w -> p (s t) h w"), 1.0).then_inc(ones_set, 1)
            dve.wait_ge(weights, 16 * 7)

            def prepare(b, s, half):
                dve.wait_ge(mask_in, b * 32 + 32)
                dve.tensor_scalar(neg[:, s, :, :], mask[:, :, :], 0.0, NEG, ALU.is_equal, ALU.mult)
                dve.tensor_scalar(negT[:, s, :, :], maskT[:, :, :], 0.0, NEG, ALU.is_equal, ALU.mult
                                  ).then_inc(neg_ready, 1)
                for n in range(2):
                    dve.wait_ge(hi_done, b * 2 + (n + 1))
                    for c in range(DK):
                        a = dve.scalar_tensor_tensor(out=rest[:, n, c, :], in0=ps[:, 6 + n, c * S:(c + 1) * S],
                                                     scalar=bqk[:, n, c:c + 1], in1=part[:, 0, n, c, :],
                                                     op0=ALU.add, op1=ALU.subtract)
                    a.then_inc(rest_done, 1)
                for n in range(2):
                    dve.wait_ge(mid_done, b * 2 + (n + 1))
                    dve.tensor_tensor(part[:, 2, n, :, :], rest[:, n, :, :], part[:, 1, n, :, :], ALU.subtract
                                      ).then_inc(lo_done, 1)
                dve.wait_ge(v_proj, b + 3)
                dve.wait_ge(ones_set, 5)
                dve.tensor_tensor(V[:, s, :, :, 0:D0], ps[:, 6, :].rearrange("p (t h w) -> p t h w", t=TB, h=H),
                                  bv[:, :].rearrange("p (h w) -> p h w", h=H).unsqueeze(1).to_broadcast([P, TB, H, D0]),
                                  ALU.add).then_inc(v_out, 1)

            def reciprocals(b):
                dve.wait_ge(sums_landed, b * (16 * G) + 16 * G)
                dve.reciprocal(recip[:, :], sums[:, :]).then_inc(recip_done, 1)

            def maxima(b, before):
                for u in range(U):
                    if u == 3 and before is not None:
                        reciprocals(before)
                    dve.wait_ge(s_ready, b * U + (u + 1))
                    dve.tensor_reduce(top_s[:, :, 2 * u:2 * u + 2].rearrange("p t j -> p j t"),
                                      ps[:, 2 * (u % 2):2 * (u % 2) + 2, :].rearrange("p j (t k) -> p j t k", t=TB),
                                      AX.X, ALU.max).then_inc(max_done, 1)

            def split_maxima(b):
                dve.wait_ge(mhi_done, b + 1)
                dve.scalar_tensor_tensor(out=mrest[:, :], in0=ps[0:H, 4, 0:S], scalar=-1.0, in1=mpart[:, 0, :],
                                         op0=ALU.mult, op1=ALU.subtract).then_inc(mrest_done, 1)
                dve.wait_ge(mmid_done, b + 1)
                dve.tensor_tensor(mpart[:, 2, :], mrest[:, :], mpart[:, 1, :], ALU.subtract).then_inc(mlo_done, 1)

            def batch(b, s, half, last):
                if not last:
                    dve.wait_ge(pv_done, b * U + 2)
                    prepare(b + 1, 1 - s, half)
                for c in range(2):
                    dve.wait_ge(pv_done, b * U + (4 * c + 6))
                    dve.wait_ge(l_ready, b * 2 + 1)
                    dve.tensor_copy(oraw[:, 2 * c:2 * c + 2, :].rearrange("p a n -> p (a n)"), ps[:, 4 + c, :]
                                    ).then_inc(o_out, 1)
                if last:
                    reciprocals(b)
                else:
                    maxima(b + 1, b)
                for c in range(2):
                    dve.wait_ge(l_ready, b * 2 + (c + 2))
                    dve.wait_ge(wo_ready, b + 1)
                    dve.tensor_tensor(onorm[:, 2 * c:2 * c + 2, :].rearrange("p a n -> p (a n)"),
                                      oraw[:, 2 * c:2 * c + 2, :].rearrange("p a n -> p (a n)"), ps[:, 6 + c, :],
                                      ALU.mult).then_inc(norm_done, 1)
                if not last:
                    split_maxima(b + 1)
                dve.wait_ge(wo_ready, b + 2)
                xs = x[:, bass.ds(b * TB, TB), :]
                dve.tensor_tensor(xs, ps[:, 5, :].rearrange("p (t d) -> p t d", t=TB), xs, ALU.add
                                  ).then_inc(resid_done, 1)

            prepare(0, 0, 0)
            maxima(0, None)
            split_maxima(0)
            every_batch(dve, batch)


def attention1(nc, top, x, xt, io, consts):
    U, W = H // 2, D1
    TRI = S + P
    SCORE, TURN, VALUE, OUT = 2, 4, 5, 10
    PASSES = ((0, 0), (1, 0), (0, 1))
    QB, KB, SB, TB_, VB, OB = 0, 1, 2, 4, 6, 7
    with top.stage() as ctx:
        def sb(name, shape, dt=F32):
            return ctx.enter_context(nc.sbuf_tensor("a1_" + name, shape, dt))

        high = [sb("w%s_high" % n, [P, DK, H * W], F32R) for n in "qkv"] + [sb("wo_high", [P, U, D], F32R)]
        low = [sb("w%s_low" % n, [P, DK, H * W], F32R) for n in "qkv"] + [sb("wo_low", [P, U, D], F32R)]
        wq, wk, wv, wo = ((h[:, :, :], l[:, :, :]) for h, l in zip(high, low))
        ctx_raw = sb("ctx_raw", [P, 2, DK, S])
        src = sb("src", [P, 2, 2, 2, DK, S], F32R)
        q = sb("q", [P, 2, 2, 2, S], F32R)
        k = sb("k", [P, 2, 2, S], F32R)
        V = sb("V", [P, TB, H, W])
        work = sb("work", [P, 2 * 2 * 2 * TRI])
        top_s, bias, total, recip = (sb(n, [P, 2, TB, 2]) for n in ("top_s", "bias", "total", "recip"))
        prob, pT = (work[:, i * 4 * TRI:(i + 1) * 4 * TRI].rearrange("p (s i n) -> p s i n", s=2, i=2)
                    for i in range(2))
        in_V = V[:, :, :, :].rearrange("p t h w -> p (t h w)")
        raw = [r.rearrange("p (a n) -> p a n", a=w.shape[1])
               for r, w in zip((in_V, work[:, 0:DK * H * W]) * 2, high)]
        diag = sb("diag", [P, 2, TB * 2, P])
        o = [sb("o_" + n, [P, 2 * U, S], F32R) for n in ("high", "low")]
        ps = ctx.enter_context(nc.psum_tensor("a1_ps", [P, 8, 512], F32))

        (wq_in, wk_in, wv_in, wo_in, wq_high, wk_high, wv_high, wo_high, wq_split, wk_split, wv_split, wo_split,
         pads_set, ctx_in0, ctx_in1, src_high, src_split, q_proj, k_proj, v_proj, q_high, k_high, q_low, k_low,
         v_out, s_ready, max_done, bias_done, exp_done, recip_done, diag_done, t_ready, t_out0, t_out1, pv_done,
         o_high, o_low, wo_ready, resid_done) = (
             top.semaphore("a1_" + n) for n in (
                 "wq_in", "wk_in", "wv_in", "wo_in", "wq_high", "wk_high", "wv_high", "wo_high", "wq_split",
                 "wk_split", "wv_split", "wo_split", "pads_set", "ctx_in0", "ctx_in1", "src_high", "src_split",
                 "q_proj", "k_proj", "v_proj", "q_high", "k_high", "q_low", "k_low", "v_out", "s_ready",
                 "max_done", "bias_done", "exp_done", "recip_done", "diag_done", "t_ready", "t_out0", "t_out1",
                 "pv_done", "o_high", "o_low", "wo_ready", "resid_done"))
        ctx_in = (ctx_in0, ctx_in1)
        block = ctx.enter_context(nc.Block())

        def every_step(engine, step):
            for n in range(OUT):
                step(0, n)
            with engine.Fori(0, B // 2 - 1) as pair:
                for n in range(OUT, OUT + 2 * U):
                    step(pair, n)
            for n in range(OUT + (B - 2) * U, OUT + B * U):
                step(0, n)

        def is_unit(n):
            return 0 <= n < B * U

        def upto(pair, n, each=1, of=1):
            return pair * (2 * U // of * each) + (n + 1) * each

        @block.sync
        def _(sp):
            def load(b, s):
                sp.dma_start(ctx_raw[:, s, :, :], io["ctxT"][bass.ds(b, 1)].rearrange("b (k p) s -> p (b k) s", p=P)
                             ).then_inc(ctx_in[s], 16)

            for n, (name, w_in, before) in enumerate((("a1_wq", wq_in, None), ("a1_wk", wk_in, None),
                                                      ("a1_wv", wv_in, wq_split), ("a1_wo", wo_in, wk_split))):
                if before is not None:
                    sp.wait_ge(before, 1)
                sp.dma_start(raw[n], io[name].rearrange("k p n -> p k n")).then_inc(w_in, 16)
                if n < 2:
                    load(n, n)
            with sp.Fori(0, B // 2 - 1) as pair:
                for s in range(2):
                    sp.wait_ge(src_split, pair * 4 + (2 * s + 2))
                    load(pair * 2 + (2 + s), s)

        @block.tensor
        def _(pe):
            pe.sem_inc(wo_ready, 12)

            def three(out, left, right, start=True, stop=True):
                todo = [(a, b, c) for a, b in PASSES for c in range(len(left[0]))]
                for i, (a, b, c) in enumerate(todo):
                    mm = pe.matmul(out, left[a][c], right[b][c], start=start and i == 0,
                                   stop=stop and i == len(todo) - 1)
                return mm

            def values(pair, u):
                h, s = u % U * 2, u % 2
                pe.wait_ge(t_out0, upto(pair, u))
                pe.wait_ge(t_out1, upto(pair, u))
                pe.wait_ge(v_out, upto(pair, u // 4, 2, 4))
                if u >= 1:
                    pe.wait_ge(o_low, upto(pair, u - 1))
                for c in range(TB):
                    for i in range(2):
                        mm = pe.matmul(ps[i * W:(i + 1) * W, VB, c * P:S], V[:, c, h + i, :],
                                       pT[:, s, i, c * S:(S if c == 0 else TRI)], start=(c == 0), stop=(c == TB - 1))
                mm.then_inc(pv_done, 1)

            def output(pair, m):
                t, c0 = m // 4 % TB, m % 4 * 2
                pe.wait_ge(o_low, upto(pair, m // U * U + c0 + 1))
                if m == 0:
                    pe.wait_ge(wo_split, 1)
                if m % U == 0:
                    pe.wait_ge(resid_done, 1 + upto(pair, m // U - 1, 1, U))
                for c in (c0, c0 + 1):
                    mm = three(ps[:, OB, t * S:(t + 1) * S],
                               [[a[:, m // U % 2 * U + c, t * P:(t + 1) * P]] for a in o], [[w[:, c, :]] for w in wo],
                               start=(c == 0), stop=(c == U - 1))
                mm.then_inc(wo_ready, 1)

            def turn(pair, u):
                s = u % 2
                pe.wait_ge(diag_done, upto(pair, u))
                if u >= 1:
                    pe.wait_ge(t_out0, upto(pair, u - 1))
                    pe.wait_ge(t_out1, upto(pair, u - 1))
                for i in range(2):
                    for n, t in enumerate((0, 1, 1)):
                        mm = pe.matmul(ps[:, TB_ + i, n * P:(n + 1) * P], prob[:, s, i, n * P:(n + 1) * P],
                                       diag[:, s, 2 * t + i, :], start=True, stop=True)
                mm.then_inc(t_ready, 1)

            def scores(pair, u):
                s = u % 2
                pe.wait_ge(q_low, upto(pair, u, 2))
                pe.wait_ge(k_low, upto(pair, u))
                if u >= 1:
                    pe.wait_ge(exp_done, upto(pair, u - 1, 4))
                for i in range(2):
                    for t in range(TB):
                        three(ps[:, SB + i, t * S:(t + 1) * S], [[q[:, s, i, a, t * P:(t + 1) * P]] for a in range(2)],
                              [[k[:, s, a, :]] for a in range(2)], stop=False)
                        diagonal = t * (S + P)
                        mm = pe.matmul(ps[:, SB + i, diagonal:diagonal + P], consts["identb"][:, :],
                                       consts["tri"][:, 0, :], start=False, stop=True)
                mm.then_inc(s_ready, 1)

            def project(pair, u):
                slot, c0 = u // U % 2, u % U
                if u % U == 0:
                    pe.wait_ge(src_split, upto(pair, u // U, 2, U))
                if u == 0:
                    pe.wait_ge(wq_split, 1)
                    pe.wait_ge(wk_split, 1)
                elif u % 4 == 1:
                    pe.wait_ge(v_out, upto(pair, u // 4, 2, 4))
                else:
                    pe.wait_ge(q_low, upto(pair, u - 1, 2))
                    pe.wait_ge(k_low, upto(pair, u - 1))
                for bank, w, which, done in ((QB, wq, 0, q_proj), (KB, wk, 1, k_proj)):
                    three(ps[:, bank, 0:S], [[a[:, c, c0 * P:(c0 + 1) * P] for c in range(DK)] for a in w],
                          [[src[:, slot, which, a, c, :] for c in range(DK)] for a in range(2)]).then_inc(done, 1)

            def project_values(pair, u):
                slot, half = u // U % 2, u // 4 % 2
                pe.wait_ge(q_low, upto(pair, u - 1, 2))
                pe.wait_ge(k_low, upto(pair, u - 1))
                if u == 1:
                    pe.wait_ge(wv_split, 1)
                for t in range(TB):
                    three(ps[:, t, :],
                          [[src[:, slot, 1, a, c, t * P:(t + 1) * P] for c in range(DK)] for a in range(2)],
                          [[w[:, c, half * 512:(half + 1) * 512] for c in range(DK)] for w in wv]
                          ).then_inc(v_proj, 1)

            def step(pair, n):
                for behind, work in ((VALUE, values), (TURN, turn), (SCORE, scores), (0, project_values), (OUT, output), (0, project)):
                    if is_unit(n - behind) and (work is not project_values or n % 4 == 1):
                        work(pair, n - behind)

            every_step(pe, step)

        @block.scalar
        def _(act):
            def split(pair, b):
                s = b % 2
                act.wait_ge(ctx_in[s], pair * 16 + (b // 2 + 1) * 16)
                if b >= 2:
                    act.wait_ge(k_proj, upto(pair, (b - 1) * U - 1))
                act.activation(src[:, s, 1, 0, :, :], ctx_raw[:, s, :, :], ACT.Copy).then_inc(src_high, 1)
                act.activation(src[:, s, 0, 0, :, :], xt[:, :, bass.ds(pair * (2 * S) + b * S, S)], ACT.Copy
                               ).then_inc(src_high, 1)

            split(0, 0)
            for n, (w_in, done) in ((1, (wk_in, wk_high)), (2, (wv_in, wv_high)), (3, (wo_in, wo_high))):
                act.wait_ge(w_in, 16)
                act.activation(high[n][:, :, :], raw[n], ACT.Copy).then_inc(done, 1)

            def turned(pair, u):
                act.wait_ge(t_ready, upto(pair, u))
                if u >= 2:
                    act.wait_ge(pv_done, upto(pair, u - 2))
                act.activation(pT[:, u % 2, 0, :], ps[:, TB_, 0:TRI], ACT.Copy).then_inc(t_out0, 1)

            def exps(pair, u):
                s = u % 2
                act.wait_ge(s_ready, upto(pair, u))
                act.wait_ge(bias_done, upto(pair, u))
                if u == 0:
                    act.wait_ge(wo_split, 1)
                if u >= 2:
                    act.wait_ge(t_ready, upto(pair, u - 2))
                    act.wait_ge(recip_done, upto(pair, u - 2))
                for i in range(2):
                    for t in range(TB):
                        act.activation(prob[:, s, i, t * P:(P if t == 0 else TRI)],
                                       ps[:, SB + i, t * S:(t * S + P * (t + 1))], ACT.Exp,
                                       bias=bias[:, s, t, i:i + 1], scale=float(D1) ** -0.5,
                                       accum_out=total[:, s, t, i:i + 1]).then_inc(exp_done, 1)

            def value_half(pair, u):
                act.wait_ge(v_proj, pair * (8 * 1) + (u // 4 * 2 + 1))
                if u == 1:
                    act.wait_ge(wv_split, 1)
                if u >= 5:
                    act.wait_ge(pv_done, upto(pair, u - 5 - (u % 4 - 1)))
                act.activation(V[:, 0, 8 * (u // 4 % 2):8 * (u // 4 % 2) + 8, :],
                               ps[:, 0, :].rearrange("p (h w) -> p h w", w=W), ACT.Copy).then_inc(v_out, 1)

            def parts(pair, u):
                s = u % 2
                act.wait_ge(q_proj, upto(pair, u))
                if u == 0:
                    act.wait_ge(pads_set, 1)
                if u >= 2:
                    act.wait_ge(s_ready, upto(pair, u - 2))
                for i in range(2):
                    r = slice(i * W, (i + 1) * W)
                    act.activation(q[r, s, i, 0, :], ps[r, QB, 0:S], ACT.Copy).then_inc(q_high, 1)
                act.wait_ge(k_proj, upto(pair, u))
                act.activation(k[:, s, 0, :], ps[:, KB, 0:S], ACT.Copy).then_inc(k_high, 1)

            def step(pair, n):
                if is_unit(n - TURN):
                    turned(pair, n - TURN)
                if is_unit(n) and n % 4 == 1:
                    value_half(pair, n)
                if is_unit(n - SCORE):
                    exps(pair, n - SCORE)
                if is_unit(n):
                    parts(pair, n)
                if n % U == 2 and is_unit(n + 6):
                    split(pair, (n + 6) // U)

            every_step(act, step)

        @block.vector
        def _(dve):
            dve.sem_inc(resid_done, 1)
            dve.tensor_scalar(q[:, :, :, :, :].rearrange("p s i a (t n) -> p (s i a t) n", n=P),
                              consts["ident"][:, :].unsqueeze(1).to_broadcast([P, 8 * TB, P]), 0.0, None, ALU.mult
                              ).then_inc(pads_set, 1)
            dve.wait_ge(wq_in, 16)
            dve.tensor_copy(high[0][:, :, :], raw[0]).then_inc(wq_high, 1)
            dve.wait_ge(wq_high, 1)
            dve.tensor_tensor(low[0][:, :, :], raw[0], high[0][:, :, :], ALU.subtract).then_inc(wq_split, 1)
            dve.wait_ge(wk_high, 1)
            dve.tensor_tensor(low[1][:, :, :], raw[1], high[1][:, :, :], ALU.subtract).then_inc(wk_split, 1)
            dve.wait_ge(wv_high, 1)
            dve.tensor_tensor(low[2][:, :, :], raw[2], high[2][:, :, :], ALU.subtract).then_inc(wv_split, 1)

            def out_parts(pair, u):
                s, before = u % (2 * U), u - 2 * U
                dve.wait_ge(pv_done, upto(pair, u))
                dve.wait_ge(wo_ready, 12 + upto(pair, before // U * U + 4 + before % U // 2))
                dve.tensor_copy(o[0][:, s, :], ps[:, VB, 0:S]).then_inc(o_high, 1)
                dve.wait_ge(o_high, upto(pair, u))
                dve.tensor_tensor(o[1][:, s, :], ps[:, VB, 0:S], o[0][:, s, :], ALU.subtract).then_inc(o_low, 1)

            def residual(pair, u):
                dve.wait_ge(wo_ready, 12 + upto(pair, u))
                xs = x[:, bass.ds(pair * (2 * TB) + u // U * TB, TB), :]
                dve.tensor_tensor(xs, ps[:, OB, :].rearrange("p (t d) -> p t d", t=TB), xs, ALU.add
                                  ).then_inc(resid_done, 1)

            def turned(pair, u):
                dve.wait_ge(t_ready, upto(pair, u))
                if u >= 2:
                    dve.wait_ge(pv_done, upto(pair, u - 2))
                dve.tensor_copy(pT[:, u % 2, 1, :], ps[:, TB_ + 1, 0:TRI]).then_inc(t_out1, 1)

            def maxima(pair, u):
                s = u % 2
                dve.wait_ge(s_ready, upto(pair, u))
                if u >= 2:
                    dve.wait_ge(bias_done, upto(pair, u - 2))
                    dve.wait_ge(exp_done, upto(pair, u - 2, 4))
                for t in range(TB):
                    dve.tensor_reduce(top_s[:, s, t, :], ps[:, SB:SB + 2, t * S:t * S + P * (t + 1)], AX.X, ALU.max
                                      ).then_inc(max_done, 1)
                dve.wait_ge(max_done, upto(pair, u, 2))
                dve.tensor_scalar(bias[:, s, :, :], top_s[:, s, :, :], -float(D1) ** -0.5, None, ALU.mult
                                  ).then_inc(bias_done, 1)

            def value_half(pair, u):
                dve.wait_ge(v_proj, upto(pair, u // 4, 2, 4))
                if u >= 5:
                    dve.wait_ge(pv_done, upto(pair, u - 5 - (u % 4 - 1)))
                dve.tensor_copy(V[:, 1, 8 * (u // 4 % 2):8 * (u // 4 % 2) + 8, :],
                                ps[:, 1, :].rearrange("p (h w) -> p h w", w=W)).then_inc(v_out, 1)

            def reciprocals(pair, u):
                s = u % 2
                dve.wait_ge(exp_done, upto(pair, u, 4))
                if u >= 2:
                    dve.wait_ge(diag_done, upto(pair, u - 2))
                dve.reciprocal(recip[:, s, :, :], total[:, s, :, :]).then_inc(recip_done, 1)

            def parts(pair, u):
                s = u % 2
                dve.wait_ge(q_high, upto(pair, u, 2))
                for i in range(2):
                    r = slice(i * W, (i + 1) * W)
                    dve.tensor_tensor(q[r, s, i, 1, :], ps[r, QB, 0:S], q[r, s, i, 0, :], ALU.subtract
                                      ).then_inc(q_low, 1)
                dve.wait_ge(k_high, upto(pair, u))
                dve.tensor_tensor(k[:, s, 1, :], ps[:, KB, 0:S], k[:, s, 0, :], ALU.subtract).then_inc(k_low, 1)

            def step(pair, n):
                if is_unit(n - VALUE):
                    out_parts(pair, n - VALUE)
                if is_unit(n - TURN):
                    turned(pair, n - TURN)
                if is_unit(n) and n % 4 == 1:
                    value_half(pair, n)
                if is_unit(n - SCORE):
                    maxima(pair, n - SCORE)
                    reciprocals(pair, n - SCORE)
                if is_unit(n - OUT) and (n - OUT) % U == U - 1:
                    residual(pair, n - OUT)
                if is_unit(n):
                    parts(pair, n)

            every_step(dve, step)

        @block.gpsimd
        def _(pool):
            def split(pair, b):
                s = b % 2
                pool.wait_ge(src_high, upto(pair, b, 2, U))
                pool.tensor_tensor(src[:, s, 1, 1, :, :], ctx_raw[:, s, :, :], src[:, s, 1, 0, :, :], ALU.subtract
                                   ).then_inc(src_split, 1)
                pool.tensor_tensor(src[:, s, 0, 1, :, :], xt[:, :, bass.ds(pair * (2 * S) + b * S, S)],
                                   src[:, s, 0, 0, :, :], ALU.subtract).then_inc(src_split, 1)

            def diagonals(pair, u):
                s = u % 2
                pool.wait_ge(recip_done, upto(pair, u))
                if u >= 2:
                    pool.wait_ge(t_ready, upto(pair, u - 2))
                pool.tensor_tensor(diag[:, s, :, :], consts["ident"][:, :].unsqueeze(1).to_broadcast([P, 2 * TB, P]),
                                   recip[:, s, :, :].rearrange("p t i -> p (t i)").unsqueeze(2
                                                                                  ).to_broadcast([P, 2 * TB, P]),
                                   ALU.mult).then_inc(diag_done, 1)

            split(0, 0)

            def step(pair, n):
                if is_unit(n - SCORE):
                    diagonals(pair, n - SCORE)
                if n % U == 2 and is_unit(n + 6):
                    split(pair, (n + 6) // U)
                if n == 1:
                    pool.wait_ge(wo_high, 1)
                    pool.tensor_tensor(low[3][:, :, :], raw[3], high[3][:, :, :], ALU.subtract).then_inc(wo_split, 1)

            every_step(pool, step)


def chained(engine, sem):
    count = [0]

    def step(ins):
        count[0] += 1
        ins.then_inc(sem, 1)
        engine.wait_ge(sem, count[0])
    return step


def gates0(nc, top, logits, hot, weight, consts):
    with top.stage() as ctx:
        def sb(name, shape, dt=F32):
            return ctx.enter_context(nc.sbuf_tensor("g0_" + name, shape, dt))

        bias, rank = consts["rb0"], consts["rank"]
        lb, ex, pr, eq = (sb(n, [P, TT, E]) for n in ("lb", "ex", "pr", "eq"))
        m, s, r = (sb(n, [P, TT]) for n in ("m", "s", "r"))
        chain, shifted, exped = (top.semaphore("g0_" + n) for n in ("chain", "shifted", "exped"))
        block = ctx.enter_context(nc.Block())

        def over_e(a):
            return a[:, :].unsqueeze(2).to_broadcast([P, TT, E])

        def over_t(a):
            return a[:, :].unsqueeze(1).to_broadcast([P, TT, E])

        @block.scalar
        def _(act):
            act.wait_ge(shifted, 1)
            act.activation(ex[:, :, :], lb[:, :, :], ACT.Exp).then_inc(exped, 1)

        @block.vector
        def _(dve):
            step = chained(dve, chain)
            step(dve.tensor_tensor(lb[:, :, :], logits[:, :, :], over_t(bias), ALU.add))
            step(dve.tensor_reduce(m[:, :], lb[:, :, :], AX.X, ALU.max))
            dve.tensor_tensor(lb[:, :, :], lb[:, :, :], over_e(m), ALU.subtract).then_inc(shifted, 1)
            dve.wait_ge(exped, 1)
            step(dve.tensor_reduce(s[:, :], ex[:, :, :], AX.X, ALU.add))
            step(dve.reciprocal(r[:, :], s[:, :]))
            step(dve.tensor_tensor(pr[:, :, :], ex[:, :, :], over_e(r), ALU.mult))
            step(dve.tensor_reduce(weight[:, :], pr[:, :, :], AX.X, ALU.max))
            step(dve.tensor_tensor(eq[:, :, :], pr[:, :, :], over_e(weight), ALU.is_equal))
            step(dve.tensor_tensor(eq[:, :, :], eq[:, :, :], over_t(rank), ALU.mult))
            step(dve.tensor_reduce(s[:, :], eq[:, :, :], AX.X, ALU.max))
            step(dve.tensor_tensor(hot[:, :, :], eq[:, :, :], over_e(s), ALU.is_equal))


def over_experts(a):
    return a[:, :].unsqueeze(2).to_broadcast([P, TT, E])


def gates1(nc, top, logits, hot1, hot2, m1, m2, consts):
    with top.stage() as ctx:
        rest = ctx.enter_context(nc.sbuf_tensor("g1_rest", [P, TT, E], F32))
        s = ctx.enter_context(nc.sbuf_tensor("g1_s", [P, TT], F32))
        chain = top.semaphore("g1_chain")
        block = ctx.enter_context(nc.Block())

        @block.vector
        def _(dve):
            step = chained(dve, chain)

            def first_hot(out, values, largest):
                step(dve.tensor_tensor(out[:, :, :], values[:, :, :], over_experts(largest), ALU.is_equal))
                step(dve.tensor_tensor(out[:, :, :], out[:, :, :],
                                       consts["rank"][:, :].unsqueeze(1).to_broadcast([P, TT, E]), ALU.mult))
                step(dve.tensor_reduce(s[:, :], out[:, :, :], AX.X, ALU.max))
                step(dve.tensor_tensor(out[:, :, :], out[:, :, :], over_experts(s), ALU.is_equal))

            step(dve.tensor_reduce(m1[:, :], logits[:, :, :], AX.X, ALU.max))
            first_hot(hot1, logits, m1)
            step(dve.scalar_tensor_tensor(out=rest[:, :, :], in0=hot1[:, :, :], scalar=NEG, in1=logits[:, :, :],
                                          op0=ALU.mult, op1=ALU.add))
            step(dve.tensor_reduce(m2[:, :], rest[:, :, :], AX.X, ALU.max))
            first_hot(hot2, rest, m2)


def shares1(nc, top, logits, hot1, m1, m2, r1, r2, ctx):
    def sb(name):
        return ctx.enter_context(nc.sbuf_tensor("s1_" + name, [P, TT, E], F32))

    ab, rest, t1, t2, ex1, ex2, keep = (sb(n) for n in ("ab", "rest", "t1", "t2", "ex1", "ex2", "keep"))
    s = ctx.enter_context(nc.sbuf_tensor("s1_s", [P, TT], F32))
    chain, shifted, exped = (top.semaphore("s1_" + n) for n in ("chain", "shifted", "exped"))

    def scalar_work(act):
        act.wait_ge(shifted, 1)
        act.activation(ex1[:, :, :], t1[:, :, :], ACT.Exp).then_inc(exped, 1)
        act.activation(ex2[:, :, :], t2[:, :, :], ACT.Exp).then_inc(exped, 1)

    def vector_work(dve):
        step = chained(dve, chain)

        def share(r, m, ex, dropped):
            step(dve.tensor_tensor(keep[:, :, :], ab[:, :, :], over_experts(m), ALU.max))
            step(dve.tensor_scalar(keep[:, :, :], keep[:, :, :], 0.02, None, ALU.mult))
            step(dve.tensor_tensor(rest[:, :, :], over_experts(m), logits[:, :, :], ALU.subtract))
            step(dve.tensor_tensor(keep[:, :, :], rest[:, :, :], keep[:, :, :], ALU.is_le))
            if dropped is not None:
                step(dve.tensor_tensor(rest[:, :, :], keep[:, :, :], dropped[:, :, :], ALU.mult))
                step(dve.tensor_tensor(keep[:, :, :], keep[:, :, :], rest[:, :, :], ALU.subtract))
            step(dve.tensor_tensor(keep[:, :, :], keep[:, :, :], ex[:, :, :], ALU.mult))
            step(dve.tensor_reduce(s[:, :], keep[:, :, :], AX.X, ALU.add))
            step(dve.reciprocal(r[:, :], s[:, :]))

        step(dve.tensor_tensor(t1[:, :, :], logits[:, :, :], over_experts(m1), ALU.subtract))
        step(dve.tensor_tensor(t2[:, :, :], logits[:, :, :], over_experts(m2), ALU.subtract))
        step(dve.scalar_tensor_tensor(out=ab[:, :, :], in0=logits[:, :, :], scalar=-1.0, in1=logits[:, :, :],
                                      op0=ALU.mult, op1=ALU.max))
        dve.tensor_scalar(t2[:, :, :], t2[:, :, :], 0.0, None, ALU.min).then_inc(shifted, 1)
        dve.wait_ge(exped, 2)
        share(r1, m1, ex1, None)
        share(r2, m2, ex2, hot1)

    return scalar_work, vector_work


def dispatch(nc, top, tag, xn, hots, dest, table, NT, xs, consts, meanwhile=None):
    with top.stage() as ctx:
        def sb(name, shape, dt=F32):
            return ctx.enter_context(nc.sbuf_tensor(tag + name, shape, dt))

        K = len(hots)
        thr, index, below = consts["thr"], consts["index"][:, 0:NT], consts["below"]
        belowb, onesb, hotb = sb("belowb", [P, P], BF16), sb("onesb", [P, P], BF16), sb("hotb", [P, TT, E], BF16)
        hot, cnt, pre_a, pre_b, pos, mine = (sb(n, [P, TT, E]) for n in ("hot", "cnt", "pre_a", "pre_b", "pos", "mine"))
        over = sb("over", [P, E, TT])
        tiles, end_a, end_b, base = (sb(n, [P, E]) for n in ("tiles", "end_a", "end_b", "base"))
        destf = sb("destf", [P, K, TT])
        past = sb("past", [P, NT, E])
        tabf = sb("tabf", [P, NT + 2])
        prank = ctx.enter_context(nc.psum_tensor(tag + "prank", [P, 512], F32))
        pcnt = ctx.enter_context(nc.psum_tensor(tag + "pcnt", [P, 512], F32))
        chain, counted = (top.semaphore(tag + n) for n in ("chain", "counted"))
        scattered = top.for_indirect(tag + "scattered")
        block = ctx.enter_context(nc.Block())

        scalar_work, vector_work = meanwhile(ctx) if meanwhile else (None, None)
        if meanwhile:
            @block.scalar
            def _(act):
                scalar_work(act)

        @block.vector
        def _(dve):
            step = chained(dve, chain)
            step(dve.tensor_copy(belowb[:, :], below[:, :]))
            step(dve.tensor_copy(onesb[:, :], consts["ones"][:, :]))
            if K == 2:
                step(dve.tensor_tensor(hot[:, :, :], hots[0][:, :, :], hots[1][:, :, :], ALU.add))
            else:
                step(dve.tensor_copy(hot[:, :, :], hots[0][:, :, :]))
            step(dve.tensor_copy(hotb[:, :, :], hot[:, :, :]))
            dve.wait_ge(counted, 1)
            step(dve.tensor_copy(cnt[:, :, :], pcnt[:, 0:TT * E].rearrange("p (t e) -> p t e", e=E)))
            a, b = cnt, pre_a
            n = 1
            while n < TT:
                step(dve.tensor_tensor(b[:, n:, :], a[:, n:, :], a[:, :TT - n, :], ALU.add))
                step(dve.tensor_copy(b[:, :n, :], a[:, :n, :]))
                a, b = b, (pre_a if b is pre_b else pre_b)
                n *= 2
            step(dve.tensor_tensor(over[:, :, :], a[:, TT - 1, :].unsqueeze(2).to_broadcast([P, E, TT]),
                                   thr[:, :].unsqueeze(1).to_broadcast([P, E, TT]), ALU.is_gt))
            step(dve.tensor_reduce(tiles[:, :], over[:, :, :], AX.X, ALU.add))
            u, v = tiles, end_a
            n = 1
            while n < E:
                step(dve.tensor_tensor(v[:, n:], u[:, n:], u[:, :E - n], ALU.add))
                step(dve.tensor_copy(v[:, :n], u[:, :n]))
                u, v = v, (end_a if v is end_b else end_b)
                n *= 2
            step(dve.tensor_tensor(base[:, :], u[:, :], tiles[:, :], ALU.subtract))
            step(dve.tensor_scalar(base[:, :], base[:, :], float(P), None, ALU.mult))
            step(dve.tensor_tensor(pos[:, :, :], a[:, :, :], cnt[:, :, :], ALU.subtract))
            step(dve.tensor_tensor(pos[:, :, :], pos[:, :, :],
                                   prank[:, 0:TT * E].rearrange("p (t e) -> p t e", e=E), ALU.add))
            step(dve.tensor_tensor(pos[:, :, :], pos[:, :, :], base[:, :].unsqueeze(1).to_broadcast([P, TT, E]), ALU.add))
            for c in range(K):
                step(dve.tensor_tensor(mine[:, :, :], pos[:, :, :], hots[c][:, :, :], ALU.mult))
                step(dve.tensor_reduce(destf[:, c, :], mine[:, :, :], AX.X, ALU.add))
            step(dve.tensor_copy(dest[:, :, :], destf[:, :, :]))
            step(dve.tensor_tensor(past[:, :, :], u[:, :].unsqueeze(1).to_broadcast([P, NT, E]),
                                   index.unsqueeze(2).to_broadcast([P, NT, E]), ALU.is_le))
            step(dve.memset(tabf[:, 0:2], -1.0))
            step(dve.tensor_reduce(tabf[:, 2:], past[:, :, :], AX.X, ALU.add))
            step(dve.tensor_scalar(table[:, :], tabf[0:1, :], E - 1.0, None, ALU.min))
            if meanwhile:
                vector_work(dve)

        @block.tensor
        def _(pe):
            pe.wait_ge(chain, 4)
            pe.matmul(prank[:, 0:TT * E], belowb[:, :], hotb[:, :, :].rearrange("p t e -> p (t e)"),
                      start=True, stop=True)
            pe.matmul(pcnt[:, 0:TT * E], onesb[:, :], hotb[:, :, :].rearrange("p t e -> p (t e)"),
                      start=True, stop=True).then_inc(counted, 1)

        @block.gpsimd
        def _(pool):
            pool.wait_ge(chain, 27 + 2 * K)
            for t in range(TT):
                for c in range(K):
                    pool.indirect_dma_start(xs, bass.IndirectOffsetOnAxis(ap=dest[:, c, t:t + 1], axis=0),
                                            xn[:, t, :], None).then_inc(scattered, 16)
            pool.wait_ge(scattered, 16 * K * TT)


def expert_tiles(nc, top, tag, xs, ys, table, NT, io, consts, gated):
    NW = 3 if gated else 2
    Q = 2
    FQ = FT // Q
    with top.stage() as ctx:
        def sb(name, shape, dt=F32):
            return ctx.enter_context(nc.sbuf_tensor(tag + name, shape, dt))

        w1 = sb("w1", [P, 2, DK, F])
        w3 = sb("w3", [P, 2, DK, F]) if gated else None
        w2 = sb("w2", [P, 2, FT, D])
        b1 = None if gated else sb("b1", [P, E, FT])
        b2 = None if gated else sb("b2", [P, E, D])
        xg, yg = sb("xg", [P, 2, D]), sb("yg", [P, 2, D])
        xgT = sb("xgT", [P, 2, DK, P])
        hT = sb("hT", [P, 2, FT, P])
        gate_o = sb("gate_o", [P, Q, FQ * P]) if gated else None
        ph = ctx.enter_context(nc.psum_tensor(tag + "ph", [P, Q, 2 if gated else 1, 512], F32))
        px = ctx.enter_context(nc.psum_tensor(tag + "px", [P, 512], F32))
        py = ctx.enter_context(nc.psum_tensor(tag + "py", [P, 2, 512], F32))
        (bias_loaded, x_ready0, x_ready1, w_ready0, w_ready1, turned, turned_out, h_ready, gate_done, h_out0, h_out1,
         y_ready, y_out, stored0, stored1) = (top.semaphore(tag + n) for n in (
             "bias_loaded", "x_ready0", "x_ready1", "w_ready0", "w_ready1", "turned", "turned_out", "h_ready",
             "gate_done", "h_out0", "h_out1", "y_ready", "y_out", "stored0", "stored1"))
        x_ready, w_ready, h_out, stored = (x_ready0, x_ready1), (w_ready0, w_ready1), (h_out0, h_out1), (stored0, stored1)
        block = ctx.enter_context(nc.Block())

        def tiles_but_last(engine, body):
            with engine.Fori(0, (NT - 1) // 4) as four:
                for j in range(4):
                    body(four * 4 + j, j % 2, four * 2 + j // 2)
            for i in range((NT - 1) // 4 * 4, NT - 1):
                body(i, i % 2, i // 2)
            body(NT - 1, (NT - 1) % 2, (NT - 1) // 2, last=True)

        def every_tile(engine, body):
            with engine.Fori(0, NT // 2) as pair:
                body(pair * 2, 0, pair)
                body(pair * 2 + 1, 1, pair)
            if NT % 2:
                body(NT - 1, 0, NT // 2)

        @block.sync
        def _(sp):
            if not gated:
                sp.dma_start(b1[:, :, :], io[tag + "b1"]).then_inc(bias_loaded, 16)
                sp.dma_start(b2[:, :, :], io[tag + "b2"]).then_inc(bias_loaded, 16)

            def load(i, s, half):
                sp.wait_ge(turned, i + 1)
                sp.dma_start(xg[:, s, :], xs[bass.ds(i * P, P), :]).then_inc(x_ready[s], 16)
                sp.wait_ge(turned, i + 2)
                e = sp.value_load(table[0:1, bass.ds(i + 2, 1)], min_val=0, max_val=E - 1)
                before = sp.value_load(table[0:1, bass.ds(i, 1)])
                with sp.If(e != before):
                    sp.dma_start(w1[:, s, :, :], io[tag + "w1"][bass.ds(e, 1)].rearrange("e (k p) f -> p (e k) f", p=P)
                                 ).then_inc(w_ready[s], 16)
                    if gated:
                        sp.dma_start(w3[:, s, :, :], io[tag + "w3"][bass.ds(e, 1)].rearrange(
                            "e (k p) f -> p (e k) f", p=P)).then_inc(w_ready[s], 16)
                    sp.wait_ge(y_ready, i + 1)
                    sp.dma_start(w2[:, s, :, :], io[tag + "w2"][bass.ds(e, 1)].rearrange("e (k p) d -> p (e k) d", p=P)
                                 ).then_inc(w_ready[s], 16)
                with sp.Else():
                    sp.sem_inc(w_ready[s], 16 * NW)
            every_tile(sp, load)

        @block.tensor
        def _(pe):
            pe.sem_inc(turned, 2)
            pe.sem_inc(y_ready, 2)

            def turn(i, s, half):
                pe.wait_ge(x_ready[s], half * 16 + 16)
                pe.wait_ge(turned_out, i + 1)
                for k in range(DK):
                    mm = pe.transpose(px[:, k * P:(k + 1) * P], xg[:, s, k * P:(k + 1) * P], consts["ident"][:, :])
                mm.then_inc(turned, 1)

            def multiply(i, s, half, last=False):
                pe.wait_ge(turned_out, i + 2)
                pe.wait_ge(w_ready[s], (half + 1) * (16 * NW))
                for q in range(Q):
                    pe.wait_ge(h_out[q], i + 1)
                    for f in range(FQ):
                        for n, w in enumerate((w1, w3) if gated else (w1,)):
                            for k in range(DK):
                                mm = pe.matmul(ph[:, q, n, f * P:(f + 1) * P],
                                               w[:, s, k, (q * FQ + f) * P:(q * FQ + f + 1) * P], xgT[:, s, k, :],
                                               start=(k == 0), stop=(k == DK - 1))
                    mm.then_inc(h_ready, 1)
                if not last:
                    turn(i + 1, 1 - s, half + s)
                pe.wait_ge(y_out, i + 1)
                for q in range(Q):
                    pe.wait_ge(h_out[q], i + 2)
                    for f in range(q * FQ, (q + 1) * FQ):
                        mm = pe.matmul(py[:, s, 0:D], hT[:, s, f, :], w2[:, s, f, :],
                                       start=(f == 0), stop=(f == FT - 1))
                mm.then_inc(y_ready, 1)

            turn(0, 0, 0)
            tiles_but_last(pe, multiply)

        @block.scalar
        def _(act):
            act.sem_inc(turned_out, 1)
            if not gated:
                act.sem_inc(h_out[0], 1)
                act.wait_ge(bias_loaded, 32)

            def turn_out(i, s, half):
                act.wait_ge(turned, i + 3)
                act.activation(xgT[:, s, :, :].rearrange("p k n -> p (k n)"), px[:, 0:D], ACT.Copy
                               ).then_inc(turned_out, 1)

            def gate(i, s, half, last=False):
                if gated:
                    for q in range(Q):
                        act.wait_ge(h_ready, i * 2 + (q + 1))
                        act.wait_ge(h_out[q], i + 1)
                        act.activation(gate_o[:, q, :], ph[:, q, 0, :], ACT.Silu).then_inc(gate_done, 1)
                else:
                    e = act.value_load(table[0:1, bass.ds(i + 2, 1)], min_val=0, max_val=E - 1)
                    act.wait_ge(h_ready, i * 2 + 1)
                    act.wait_ge(y_ready, i + 1)
                    for f in range(FQ):
                        a = act.activation(hT[:, s, f, :], ph[:, 0, 0, f * P:(f + 1) * P], ACT.Relu,
                                           bias=b1[:, e, f:f + 1])
                    a.then_inc(h_out[0], 1)
                if not last:
                    act.wait_ge(h_ready, i * 2 + 1)
                    turn_out(i + 1, 1 - s, half + s)
                act.wait_ge(y_out, i + 3)
                act.dma_start(ys[bass.ds(i * P, P), :], yg[:, s, :]).then_inc(stored[s], 16)

            act.sem_inc(stored[0], 16)
            act.sem_inc(stored[1], 16)
            turn_out(0, 0, 0)
            tiles_but_last(act, gate)
            act.wait_ge(stored[0], 16 + 16 * ((NT + 1) // 2))
            act.wait_ge(stored[1], 16 + 16 * (NT // 2))

        @block.vector
        def _(dve):
            dve.sem_inc(y_out, 2)
            dve.sem_inc(h_out[1], 1)
            if gated:
                dve.sem_inc(h_out[0], 1)
            else:
                dve.wait_ge(bias_loaded, 32)

            def finish(i, s, half):
                if gated:
                    for q in range(Q):
                        dve.wait_ge(gate_done, i * 2 + (q + 1))
                        dve.wait_ge(y_ready, i + 1)
                        dve.tensor_tensor(hT[:, s, q * FQ:(q + 1) * FQ, :].rearrange("p f n -> p (f n)"),
                                          ph[:, q, 1, :], gate_o[:, q, :], ALU.mult).then_inc(h_out[q], 1)
                else:
                    e = dve.value_load(table[0:1, bass.ds(i + 2, 1)], min_val=0, max_val=E - 1)
                    dve.wait_ge(h_ready, i * 2 + 2)
                    dve.wait_ge(y_ready, i + 1)
                    for f in range(FQ):
                        a = dve.tensor_scalar(hT[:, s, FQ + f, :], ph[:, 1, 0, f * P:(f + 1) * P],
                                              b1[:, e, FQ + f:FQ + f + 1], 0.0, ALU.add, ALU.max)
                    a.then_inc(h_out[1], 1)
                dve.wait_ge(y_ready, i + 3)
                dve.wait_ge(stored[s], half * 16 + 16)
                if gated:
                    dve.tensor_copy(yg[:, s, :], py[:, s, 0:D]).then_inc(y_out, 1)
                else:
                    dve.tensor_tensor(yg[:, s, :], py[:, s, 0:D], b2[:, e, :], ALU.add).then_inc(y_out, 1)
            every_tile(dve, finish)


def combine(nc, top, tag, x, ys, dest, weights):
    with top.stage() as ctx:
        K = len(weights)
        yt = ctx.enter_context(nc.sbuf_tensor(tag + "yt", [P, TT, K, D], F32))
        gathered = [top.for_indirect(tag + f"gathered{n}") for n in range(8)]
        added = top.semaphore(tag + "added")
        block = ctx.enter_context(nc.Block())

        @block.gpsimd
        def _(pool):
            for t in range(TT):
                if t >= 8:
                    pool.wait_ge(added, K * (t - 7))
                for c in range(K):
                    pool.indirect_dma_start(yt[:, t, c, :], None, ys,
                                            bass.IndirectOffsetOnAxis(ap=dest[:, c, t:t + 1], axis=0)
                                            ).then_inc(gathered[t % 8], 16)

        @block.vector
        def _(dve):
            for t in range(TT):
                dve.wait_ge(gathered[t % 8], 16 * K * (t // 8 + 1))
                for c in range(K):
                    if c:
                        dve.wait_ge(added, K * t + c)
                    dve.scalar_tensor_tensor(out=x[:, t, :], in0=yt[:, t, c, :], scalar=weights[c][:, t:t + 1],
                                             in1=x[:, t, :], op0=ALU.mult, op1=ALU.add).then_inc(added, 1)


def linear_attention(nc, top, x, xt, io):
    with top.stage() as ctx:
        def sb(name, shape, dt=F32):
            return ctx.enter_context(nc.sbuf_tensor("a2_" + name, shape, dt))

        cx, xb, kv = (sb(n, [P, 2, TB, D]) for n in ("cx", "xb", "kv"))
        pk = ctx.enter_context(nc.psum_tensor("a2_pk", [P, 2, DK, D], F32))
        po = ctx.enter_context(nc.psum_tensor("a2_po", [P, 2, TB, D], F32))
        loaded0, loaded1, copied, kv_ready, kv_out, o_ready, resid_done = (
            top.semaphore("a2_" + n) for n in (
                "loaded0", "loaded1", "copied", "kv_ready", "kv_out", "o_ready", "resid_done"))
        block = ctx.enter_context(nc.Block())

        @block.sync
        def _(sp):
            with sp.Fori(0, B // 2) as pair:
                for s, sem in enumerate((loaded0, loaded1)):
                    sp.wait_ge(kv_ready, 2 * pair + (s + 1))
                    sp.dma_start(cx[:, s, :, :], io["ctx"][bass.ds(pair * 2 + s, 1)].rearrange(
                        "b (t p) d -> p (b t) d", p=P)).then_inc(sem, 16)

        @block.gpsimd
        def _(pool):
            with pool.Fori(0, B // 2) as pair:
                for s in range(2):
                    pool.wait_ge(o_ready, 2 * pair + s + 1)
                    pool.tensor_copy(xb[:, s, :, :], xt[:, :, bass.ds((pair * 2 + s) * S, S)]).then_inc(copied, 1)

        @block.tensor
        def _(pe):
            pe.sem_inc(o_ready, 2)
            pe.sem_inc(kv_ready, 2)
            with pe.Fori(0, B // 2) as pair:
                for s, sem in enumerate((loaded0, loaded1)):
                    b = pair * 2 + s
                    pe.wait_ge(sem, 16 * pair + 16)
                    pe.wait_ge(kv_out, b + 1)
                    for k in range(DK):
                        for t in range(TB):
                            mm = pe.matmul(pk[:, s, k, :], cx[:, s, t, k * P:(k + 1) * P], cx[:, s, t, :],
                                           start=(t == 0), stop=(t == TB - 1))
                    mm.then_inc(kv_ready, 1)
                    pe.wait_ge(kv_out, b + 3)
                    pe.wait_ge(copied, b + 1)
                    pe.wait_ge(resid_done, b + 1)
                    for t in range(TB):
                        for k in range(DK):
                            mm = pe.matmul(po[:, s, t, :], xb[:, s, k, t * P:(t + 1) * P], kv[:, s, k, :],
                                           start=(k == 0), stop=(k == DK - 1))
                    mm.then_inc(o_ready, 1)

        @block.scalar
        def _(act):
            act.sem_inc(kv_out, 2)
            with act.Fori(0, B // 2) as pair:
                for s in range(2):
                    b = pair * 2 + s
                    act.wait_ge(kv_ready, b + 3)
                    act.wait_ge(o_ready, b + 1)
                    act.mul(kv[:, s, :, :], pk[:, s, :, :], 1.0 / S).then_inc(kv_out, 1)

        @block.vector
        def _(dve):
            dve.sem_inc(resid_done, 2)
            with dve.Fori(0, B // 2) as pair:
                for s in range(2):
                    b = pair * 2 + s
                    dve.wait_ge(o_ready, b + 3)
                    xs = x[:, bass.ds(b * TB, TB), :]
                    dve.tensor_tensor(xs, po[:, s, :, :], xs, ALU.add).then_inc(resid_done, 1)


def scaled_linear(nc, top, x, xt, io):
    with top.stage() as ctx:
        def sb(name, shape, dt=F32):
            return ctx.enter_context(nc.sbuf_tensor("f2_" + name, shape, dt))

        cb = sb("cb", [P, DK, D])
        scb, scale, bias = (sb(n, [P, D]) for n in ("scb", "scale", "bias"))
        xb, o1, o2 = (sb(n, [P, 2, TB, D]) for n in ("xb", "o1", "o2"))
        po = ctx.enter_context(nc.psum_tensor("f2_po", [P, 2, TB, D], F32))
        loaded, scaled, copied, o_ready, o1_done, o2_done, resid_done = (
            top.semaphore("f2_" + n) for n in (
                "loaded", "scaled", "copied", "o_ready", "o1_done", "o2_done", "resid_done"))
        block = ctx.enter_context(nc.Block())

        @block.sync
        def _(sp):
            sp.dma_start(cb[:, :, :], io["f2_cb"].rearrange("(k p) n -> p k n", p=P)).then_inc(loaded, 16)
            sp.dma_start(scb[:, :], io["f2_scb"]).then_inc(loaded, 16)
            sp.dma_start(bias[:, :], io["f2_bias"]).then_inc(loaded, 16)

        @block.gpsimd
        def _(pool):
            with pool.Fori(0, B // 2) as pair:
                for s in range(2):
                    pool.wait_ge(o_ready, 2 * pair + s + 1)
                    pool.tensor_copy(xb[:, s, :, :], xt[:, :, bass.ds((pair * 2 + s) * S, S)]).then_inc(copied, 1)

        @block.tensor
        def _(pe):
            pe.sem_inc(o_ready, 2)
            pe.wait_ge(loaded, 48)
            with pe.Fori(0, B // 2) as pair:
                for s in range(2):
                    b = pair * 2 + s
                    pe.wait_ge(copied, b + 1)
                    pe.wait_ge(o1_done, b + 1)
                    for t in range(TB):
                        for k in range(DK):
                            mm = pe.matmul(po[:, s, t, :], xb[:, s, k, t * P:(t + 1) * P], cb[:, k, :],
                                           start=(k == 0), stop=(k == DK - 1))
                    mm.then_inc(o_ready, 1)

        @block.vector
        def _(dve):
            dve.sem_inc(o1_done, 2)
            dve.sem_inc(o2_done, 1)
            dve.sem_inc(resid_done, 1)
            dve.wait_ge(loaded, 48)
            dve.tensor_scalar(scale[:, :], scb[:, :], 1.0 / 127.0, None, ALU.mult).then_inc(scaled, 1)
            dve.wait_ge(scaled, 1)
            with dve.Fori(0, B // 2) as pair:
                for s in range(2):
                    b = pair * 2 + s
                    dve.wait_ge(o_ready, b + 3)
                    dve.wait_ge(o2_done, b + 1)
                    dve.tensor_tensor(o1[:, s, :, :], po[:, s, :, :],
                                      scale[:, :].unsqueeze(1).to_broadcast([P, TB, D]), ALU.mult).then_inc(o1_done, 1)
                    dve.wait_ge(o1_done, b + 3)
                    dve.wait_ge(resid_done, b + 1)
                    dve.tensor_tensor(o2[:, s, :, :], o1[:, s, :, :],
                                      bias[:, :].unsqueeze(1).to_broadcast([P, TB, D]), ALU.add).then_inc(o2_done, 1)
                    dve.wait_ge(o2_done, b + 2)
                    xs = x[:, bass.ds(b * TB, TB), :]
                    dve.tensor_tensor(xs, o2[:, s, :, :], xs, ALU.add).then_inc(resid_done, 1)


def attention3(nc, top, x, xt, io, consts):
    with top.stage() as ctx:
        def sb(name, shape, dt=F32):
            return ctx.enter_context(nc.sbuf_tensor("a3_" + name, shape, dt))

        wq, wk, wv = (sb(n, [P, DK, D]) for n in ("wq", "wk", "wv"))
        bq, bk = sb("bq", [P, DK]), sb("bk", [P, DK])
        bv = sb("bv", [P, D])
        ctxT = sb("ctxT", [P, DK, S])
        qT, kT = sb("qT", [P, DK, S]), sb("kT", [P, DK, S])
        V = sb("V", [P, TB, D])
        top_s, shift, l, rl = (sb(n, [P, TB]) for n in ("top_s", "shift", "l", "rl"))
        pr, pT = sb("pr", [P, TB, S]), sb("pT", [P, TB, S])
        bank = [ctx.enter_context(nc.psum_tensor(f"a3_{n}", [P, 2, S], F32)) for n in ("q", "k", "v", "s", "t", "o")]
        pq, pk, pv, pS, pt, po = bank
        (weights, ctx_loaded, q_proj, k_proj, v_proj, q_out, k_out, v_out, s_ready, max_done, shift_done,
         exp_done, t_ready, t_out, l_done, o_ready, resid_done) = (
            top.semaphore("a3_" + n) for n in (
                "weights", "ctx_loaded", "q_proj", "k_proj", "v_proj", "q_out", "k_out", "v_out", "s_ready",
                "max_done", "shift_done", "exp_done", "t_ready", "t_out", "l_done", "o_ready", "resid_done"))
        block = ctx.enter_context(nc.Block())

        @block.sync
        def _(sp):
            for dst, name in ((wq, "a3_wq"), (wk, "a3_wk"), (wv, "a3_wv")):
                sp.dma_start(dst[:, :, :], io[name].rearrange("(k p) n -> p k n", p=P)).then_inc(weights, 16)
            for dst, name in ((bq, "a3_bq"), (bk, "a3_bk"), (bv, "a3_bv")):
                sp.dma_start(dst[:, :], io[name]).then_inc(weights, 16)
            with sp.Fori(0, B) as b:
                sp.wait_ge(v_proj, b + 1)
                sp.dma_start(ctxT[:, :, :], io["ctxT"][bass.ds(b, 1)].rearrange("b (k p) s -> p (b k) s", p=P)
                             ).then_inc(ctx_loaded, 16)

        def every_batch(engine, body):
            with engine.Fori(0, B - 1) as b:
                body(b, False)
            body(B - 1, True)

        @block.tensor
        def _(pe):
            pe.sem_inc(v_proj, 1)
            pe.wait_ge(weights, 16 * 6)

            def queries_keys(b):
                for n in range(DK):
                    for k in range(DK):
                        mm = pe.matmul(pq[:, n, :], wq[:, k, n * P:(n + 1) * P], xt[:, k, bass.ds(b * S, S)],
                                       start=(k == 0), stop=(k == DK - 1))
                mm.then_inc(q_proj, 1)
                pe.wait_ge(ctx_loaded, 16 * b + 16)
                for n in range(DK):
                    for k in range(DK):
                        mm = pe.matmul(pk[:, n, :], wk[:, k, n * P:(n + 1) * P], ctxT[:, k, :],
                                       start=(k == 0), stop=(k == DK - 1))
                mm.then_inc(k_proj, 1)

            def values(b):
                pe.wait_ge(v_out, b + 1)
                for t in range(TB):
                    for k in range(DK):
                        mm = pe.matmul(pv[:, t, :], ctxT[:, k, t * P:(t + 1) * P], wv[:, k, :],
                                       start=(k == 0), stop=(k == DK - 1))
                mm.then_inc(v_proj, 1)

            def batch(b, last):
                pe.wait_ge(q_out, 2 * b + 2)
                pe.wait_ge(k_out, 2 * b + 2)
                pe.wait_ge(exp_done, 2 * b + 1)
                for t in range(TB):
                    for k in range(DK):
                        mm = pe.matmul(pS[:, t, :], qT[:, k, t * P:(t + 1) * P], kT[:, k, :],
                                       start=(k == 0), stop=(k == DK - 1))
                mm.then_inc(s_ready, 1)
                if not last:
                    queries_keys(b + 1)
                pe.wait_ge(exp_done, 2 * b + 3)
                pe.wait_ge(t_out, b + 1)
                for t in range(TB):
                    for q in range(TB):
                        mm = pe.transpose(pt[:, t, q * P:(q + 1) * P], pr[:, q, t * P:(t + 1) * P],
                                          consts["ident"][:, :])
                mm.then_inc(t_ready, 1)
                if not last:
                    values(b + 1)
                pe.wait_ge(t_out, b + 2)
                pe.wait_ge(v_out, b + 2)
                pe.wait_ge(resid_done, 2 * b + 1)
                for q in range(TB):
                    for t in range(TB):
                        mm = pe.matmul(po[:, q, :], pT[:, t, q * P:(q + 1) * P], V[:, t, :],
                                       start=(t == 0), stop=(t == TB - 1))
                mm.then_inc(o_ready, 1)

            queries_keys(0)
            values(0)
            every_batch(pe, batch)

        @block.scalar
        def _(act):
            act.sem_inc(exp_done, 1)
            act.wait_ge(weights, 16 * 6)

            def queries(b):
                act.wait_ge(q_proj, b + 1)
                for n in range(DK):
                    act.activation(qT[:, n, :], pq[:, n, :], ACT.Identity, bias=bq[:, n:n + 1]).then_inc(q_out, 1)

            def batch(b, last):
                act.wait_ge(shift_done, b + 1)
                act.wait_ge(l_done, b + 1)
                for q in range(TB):
                    act.activation(pr[:, q, :], pS[:, q, :], ACT.Exp, bias=shift[:, q:q + 1],
                                   scale=float(D) ** -0.5, accum_out=l[:, q:q + 1]).then_inc(exp_done, 1)
                if not last:
                    queries(b + 1)

            queries(0)
            every_batch(act, batch)

        @block.vector
        def _(dve):
            for sem in (v_out, t_out, resid_done, o_ready, l_done):
                dve.sem_inc(sem, 1)
            dve.wait_ge(weights, 16 * 6)

            def keys(b):
                dve.wait_ge(k_proj, b + 1)
                for n in range(DK):
                    dve.tensor_scalar(kT[:, n, :], pk[:, n, :], bk[:, n:n + 1], None, ALU.add).then_inc(k_out, 1)

            def values(b):
                dve.wait_ge(v_proj, b + 2)
                dve.wait_ge(o_ready, b + 1)
                dve.tensor_tensor(V[:, :, :], pv[:, :, :], bv[:, :].unsqueeze(1).to_broadcast([P, TB, D]), ALU.add
                                  ).then_inc(v_out, 1)

            def batch(b, last):
                dve.wait_ge(s_ready, b + 1)
                dve.tensor_reduce(top_s[:, :], pS[:, :, :], AX.X, ALU.max).then_inc(max_done, 1)
                dve.wait_ge(max_done, b + 1)
                dve.tensor_scalar(shift[:, :], top_s[:, :], -float(D) ** -0.5, None, ALU.mult).then_inc(shift_done, 1)
                if not last:
                    keys(b + 1)
                dve.wait_ge(t_ready, b + 1)
                dve.wait_ge(o_ready, b + 1)
                dve.tensor_copy(pT[:, :, :], pt[:, :, :]).then_inc(t_out, 1)
                dve.wait_ge(exp_done, 2 * b + 3)
                dve.reciprocal(rl[:, :], l[:, :]).then_inc(l_done, 1)
                dve.wait_ge(o_ready, b + 2)
                dve.wait_ge(l_done, b + 2)
                for q in range(TB):
                    xs = x[:, b * TB + q, :]
                    dve.scalar_tensor_tensor(out=xs, in0=po[:, q, :], scalar=rl[:, q:q + 1], in1=xs,
                                             op0=ALU.mult, op1=ALU.add).then_inc(resid_done, 1)
                if not last:
                    values(b + 1)

            keys(0)
            values(0)
            every_batch(dve, batch)


def bit_ffn(nc, top, x, ident, io, consts, out):
    BANKS = 3
    with top.stage() as ctx:
        def sb(name, shape, dt=F32):
            return ctx.enter_context(nc.sbuf_tensor("f3_" + name, shape, dt))

        w1, w2 = sb("w1", [P, DK * F]), sb("w2", [P, FT * D])
        wa, wb = sb("wa", [P, DK * F]), sb("wb", [P, FT * D])
        w1q, w2q = sb("w1q", [P, DK, F], F32R), sb("w2q", [P, FT, D], BF16)
        asum, unit, scale = sb("asum", [P, 2]), sb("unit", [P, 2]), sb("scale", [P, 2])
        cw, cwu, cb = sb("cw", [P, FT, 3]), sb("cwu", [P, FT, 3]), sb("cb", [P, FT])
        magic = sb("magic", [P, 1])
        stats = sb("stats", [P, TT, 6])
        total, diff, m2, mean, diff2, var, vareps, rstd, root, guess = (
            sb(n, [P, TT]) for n in ("total", "diff", "m2", "mean", "diff2", "var", "vareps", "rstd", "root", "guess"))
        xn, q1, q2 = (sb(n, [P, TB, D]) for n in ("xn", "q1", "q2"))
        amax, amaxc, rec, qs, qr = (sb(n, [P, TB]) for n in ("amax", "amaxc", "rec", "qs", "qr"))
        xh, xl = (sb(n, [P, 2, DK, S + 2], F32R) for n in ("xh", "xl"))
        y = sb("y", [P, FT, S])
        sT = sb("sT", [P, 2, FT, S])
        sax, saxc, srec, sqs, sqr = (sb(n, [P, TB]) for n in ("sax", "saxc", "srec", "sqs", "sqr"))
        s1, sq = sb("s1", [P, TB, F]), sb("sq", [P, TB, F], BF16)
        sqT = sb("sqT", [P, TB, FT, P], BF16)
        ph = ctx.enter_context(nc.psum_tensor("f3_ph", [P, BANKS, 512], F32))
        pn = ctx.enter_context(nc.psum_tensor("f3_pn", [P, F], F32))
        pb = ctx.enter_context(nc.psum_tensor("f3_pb", [P, FT, P], BF16))
        px = ctx.enter_context(nc.psum_tensor("f3_px", [P, DK, S], F32))
        po = ctx.enter_context(nc.psum_tensor("f3_po", [P, 512], F32))
        (w1_in, w2_in, conv_in, asum_done, sum_ready, wchain, w1_ready, w2_near, w2_ready, pads_set, magic_set,
         stats_done, comb, rooted, xn_done, prep, q1_done, q2_done, x_turned, x_high, x_low, h_ready, y0_done, y1_done,
         y2_done, silu_done, s_turned, red_done, s1_done, sq_done, q_turned, sqT_out, o_ready, resid_done, stored) = (
             top.semaphore("f3_" + n) for n in (
                 "w1_in", "w2_in", "conv_in", "asum_done", "sum_ready", "wchain", "w1_ready", "w2_near", "w2_ready",
                 "pads_set", "magic_set", "stats_done", "comb", "rooted", "xn_done", "prep", "q1_done", "q2_done",
                 "x_turned", "x_high", "x_low", "h_ready", "y0_done", "y1_done", "y2_done", "silu_done", "s_turned",
                 "red_done", "s1_done", "sq_done", "q_turned", "sqT_out", "o_ready", "resid_done", "stored"))
        block = ctx.enter_context(nc.Block())

        def every_step(engine, step):
            for n in range(4):
                step(0, n)
            with engine.Fori(0, (B - 4) // 2) as pair:
                step(pair, 4)
                step(pair, 5)
            for n in range(B, B + 4):
                step(0, n)

        def is_batch(n):
            return 0 <= n < B

        def upto(pair, i, of=1):
            return pair * (2 * of) + (i + 1)

        @block.sync
        def _(sp):
            sp.dma_start(w1[:, :].rearrange("p (k f) -> p k f", k=DK), io["f3_w1"].rearrange("(k p) f -> p k f", p=P)
                         ).then_inc(w1_in, 16)
            sp.dma_start(w2[:, :].rearrange("p (k d) -> p k d", k=FT), io["f3_w2"].rearrange("(k p) d -> p k d", p=P)
                         ).then_inc(w2_in, 16)
            sp.dma_start(cw[:, :, :], io["f3_cw"].rearrange("(t p) k -> p t k", p=P)).then_inc(conv_in, 16)
            sp.dma_start(cb[:, :], io["f3_cb"]).then_inc(conv_in, 16)
            with sp.Fori(0, B) as b:
                sp.wait_ge(resid_done, 2 * b + 2)
                sp.dma_start(out[bass.ds(b, 1)].rearrange("b (t p) d -> p (b t) d", p=P), x[:, bass.ds(b * TB, TB), :]
                             ).then_inc(stored, 16)
            sp.wait_ge(stored, 16 * B)

        @block.vector
        def _(dve):
            dve.memset(magic[:, :], MAGIC).then_inc(magic_set, 1)
            for i, part in enumerate((xh, xl)):
                for end in (0, S + 1):
                    dve.tensor_scalar(part[:, :, :, end:end + 1],
                                      consts["ones"][:, 0:2 * DK].rearrange("p (s k) -> p s k", k=DK).unsqueeze(3),
                                      0.0, None, ALU.mult).then_inc(pads_set, 1)
            for t in range(TT):
                dve.bn_stats(stats[:, t, :], x[:, t, :]).then_inc(stats_done, 1)
            dve.wait_ge(stats_done, TT)
            step = chained(dve, comb)
            step(dve.tensor_tensor(total[:, :], stats[:, :, 1], stats[:, :, 4], ALU.add))
            step(dve.tensor_tensor(diff[:, :], stats[:, :, 1], stats[:, :, 4], ALU.subtract))
            step(dve.tensor_tensor(m2[:, :], stats[:, :, 2], stats[:, :, 5], ALU.add))
            step(dve.tensor_scalar(mean[:, :], total[:, :], 0.5, None, ALU.mult))
            step(dve.tensor_tensor(diff2[:, :], diff[:, :], diff[:, :], ALU.mult))
            step(dve.scalar_tensor_tensor(out=var[:, :], in0=diff2[:, :], scalar=D / 4.0, in1=m2[:, :],
                                          op0=ALU.mult, op1=ALU.add))
            step(dve.tensor_scalar(vareps[:, :], var[:, :], 1.0 / D, EPS, ALU.mult, ALU.add))
            for n, (w, w_in) in enumerate(((w1, w1_in), (w2, w2_in))):
                dve.wait_ge(w_in, 16)
                dve.tensor_reduce(asum[:, n:n + 1], w[:, :], AX.X, ALU.add, apply_absolute_value=True
                                  ).then_inc(asum_done, 1)
            dve.wait_ge(rooted, 1)
            step(dve.reciprocal(guess[:, :], root[:, :]))
            step(dve.tensor_tensor(total[:, :], guess[:, :], guess[:, :], ALU.mult))
            step(dve.tensor_tensor(diff[:, :], total[:, :], vareps[:, :], ALU.mult))
            step(dve.tensor_scalar(total[:, :], diff[:, :], -0.5, 1.5, ALU.mult, ALU.add))
            step(dve.tensor_tensor(rstd[:, :], guess[:, :], total[:, :], ALU.mult))
            dve.wait_ge(sum_ready, 1)
            step = chained(dve, wchain)
            step(dve.tensor_scalar(unit[:, :], po[:, 0:2], 1.0 / (D * F), 1e-5, ALU.mult, ALU.max))
            step(dve.reciprocal(scale[:, :], unit[:, :]))
            step(dve.tensor_scalar(wa[:, :], w1[:, :], scale[:, 0:1], -1.0, ALU.mult, ALU.max))
            step(dve.tensor_scalar(w1[:, :], wa[:, :], 1.0, MAGIC, ALU.min, ALU.add))
            dve.wait_ge(conv_in, 32)
            step(dve.tensor_scalar(cwu[:, :, :], cw[:, :, :], unit[:, 0:1], None, ALU.mult))

            def norm(pair, b, t):
                row = pair * (2 * TB) + (b * TB + t)
                if b >= 1:
                    dve.wait_ge(q1_done, upto(pair, 2 * b - 1, 2))
                dve.tensor_scalar(xn[:, t, :], x[:, row, :], mean[:, bass.ds(row, 1)], rstd[:, bass.ds(row, 1)],
                                  ALU.subtract, ALU.mult).then_inc(xn_done, 1)

            def token_scale(pair, b, k):
                if k == 0:
                    dve.wait_ge(xn_done, upto(pair, 2 * b + 1, 2))
                    ins = dve.tensor_reduce(amax[:, :], xn[:, :, :], AX.X, ALU.max, apply_absolute_value=True)
                else:
                    dve.wait_ge(prep, upto(pair, 5 * b + k - 1, 5))
                if k == 1:
                    ins = dve.tensor_scalar(amaxc[:, :], amax[:, :], 1e-5, None, ALU.max)
                if k == 2:
                    ins = dve.reciprocal(rec[:, :], amaxc[:, :])
                if k == 3:
                    ins = dve.tensor_scalar(qs[:, :], rec[:, :], 127.0, None, ALU.mult)
                if k == 4:
                    ins = dve.tensor_scalar(qr[:, :], amaxc[:, :], 1.0 / 127.0, None, ALU.mult)
                ins.then_inc(prep, 1)

            def unrounded(pair, b, t):
                dve.wait_ge(q1_done, upto(pair, 2 * b + t, 2))
                if b >= 1:
                    dve.wait_ge(x_turned, upto(pair, b - 1))
                dve.wait_ge(prep, upto(pair, 5 * b + 4, 5))
                dve.tensor_scalar(q2[:, t, :], q1[:, t, :], MAGIC, qr[:, t:t + 1], ALU.subtract, ALU.mult
                                  ).then_inc(q2_done, 1)

            def low_part(pair, b):
                dve.wait_ge(x_high, upto(pair, b))
                dve.tensor_tensor(xl[:, b % 2, :, 1:S + 1], px[:, :, :], xh[:, b % 2, :, 1:S + 1], ALU.subtract
                                  ).then_inc(x_low, 1)

            def first_tap(pair, b, f):
                dve.wait_ge(y0_done, upto(pair, FT * b + f, FT))
                dve.scalar_tensor_tensor(out=y[:, f, :], in0=ph[:, f % BANKS, 0:S], scalar=cwu[:, f, 0:1],
                                         in1=y[:, f, :], op0=ALU.mult, op1=ALU.add).then_inc(y1_done, 1)

            def last_tap(pair, b, f):
                dve.wait_ge(y1_done, upto(pair, FT * b + f, FT))
                dve.scalar_tensor_tensor(out=y[:, f, :], in0=ph[:, f % BANKS, 2:S + 2], scalar=cwu[:, f, 2:3],
                                         in1=y[:, f, :], op0=ALU.mult, op1=ALU.add).then_inc(y2_done, 1)

            def tile_scale(pair, b, t, k):
                i = TB * b + t
                c = slice(t, t + 1)
                if k == 0:
                    dve.wait_ge(s_turned, upto(pair, i, TB))
                    dve.tensor_reduce(sax[:, c], pn[:, :], AX.X, ALU.max, apply_absolute_value=True
                                      ).then_inc(red_done, 1)
                    return
                dve.wait_ge(red_done, upto(pair, 5 * i + k - 1, 5 * TB))
                if k == 1:
                    dve.tensor_scalar(saxc[:, c], sax[:, c], 1e-5, None, ALU.max).then_inc(red_done, 1)
                if k == 2:
                    dve.reciprocal(srec[:, c], saxc[:, c]).then_inc(red_done, 1)
                if k == 3:
                    dve.tensor_scalar(sqs[:, c], srec[:, c], 127.0, None, ALU.mult).then_inc(red_done, 1)
                if k == 4:
                    if i >= TB:
                        dve.wait_ge(resid_done, upto(pair, i - TB, TB))
                    dve.tensor_scalar(sqr[:, c], saxc[:, c], 1.0 / 127.0, unit[:, 1:2], ALU.mult, ALU.mult
                                      ).then_inc(red_done, 1)
                if k == 5:
                    if i >= TB:
                        dve.wait_ge(sq_done, upto(pair, i - TB, TB))
                    dve.tensor_scalar(s1[:, t, :], pn[:, :], sqs[:, c], MAGIC, ALU.mult, ALU.add).then_inc(s1_done, 1)

            def residual(pair, b, t):
                xs = x[:, pair * (2 * TB) + (b * TB + t), :]
                dve.wait_ge(o_ready, upto(pair, TB * b + t, TB))
                if t == 0:
                    dve.wait_ge(red_done, upto(pair, 5 * (TB * b + 1) + 4, 5 * TB))
                dve.scalar_tensor_tensor(out=xs, in0=po[:, 0:D], scalar=sqr[:, t:t + 1], in1=xs,
                                         op0=ALU.mult, op1=ALU.add).then_inc(resid_done, 1)

            def step(pair, n):
                new, turn, hid, end, last = (is_batch(n - i) for i in range(5))
                for place in range(2 * FT + 2):
                    if turn and place < TB:
                        unrounded(pair, n - 1, place)
                    if end and 3 <= place < 9:
                        tile_scale(pair, n - 3, 0, place - 3)
                    if hid and place < 2 * FT:
                        (first_tap, last_tap)[place % 2](pair, n - 2, place // 2)
                    if end and place >= 12:
                        tile_scale(pair, n - 3, 1, place - 12)
                    if last and place in (3, 8):
                        residual(pair, n - 4, (3, 8).index(place))
                    if new and place in (5, 6):
                        norm(pair, n, place - 5)
                    if turn and place == 7:
                        low_part(pair, n - 1)
                    if new and place in (9, 10, 12, 14, 16):
                        token_scale(pair, n, (9, 10, 12, 14, 16).index(place))

            every_step(dve, step)

        @block.scalar
        def _(act):
            act.wait_ge(comb, 7)
            act.activation(root[:, :], vareps[:, :], ACT.Sqrt).then_inc(rooted, 1)
            act.wait_ge(wchain, 4)
            act.activation(w1q[:, :, :].rearrange("p a b -> p (a b)"), w1[:, :], ACT.Copy, bias=-MAGIC
                           ).then_inc(w1_ready, 1)
            act.wait_ge(magic_set, 1)

            def rounded(pair, b):
                for t in range(TB):
                    act.wait_ge(prep, upto(pair, 5 * b + 3, 5))
                    if b >= 1:
                        act.wait_ge(q2_done, upto(pair, 2 * b - 1, 2))
                    act.activation(q1[:, t, :], xn[:, t, :], ACT.Identity, bias=magic[:, 0:1], scale=qs[:, t:t + 1]
                                   ).then_inc(q1_done, 1)

            def high_part(pair, b):
                act.wait_ge(x_turned, upto(pair, b))
                if b >= 2:
                    act.wait_ge(h_ready, upto(pair, FT * (b - 1) - 1, FT))
                act.activation(xh[:, b % 2, :, 1:S + 1], px[:, :, :], ACT.Copy).then_inc(x_high, 1)

            def middle_tap(pair, b, f):
                i = FT * b + f
                act.wait_ge(h_ready, upto(pair, i, FT))
                if i == 0:
                    act.wait_ge(wchain, 5)
                if b >= 1:
                    act.wait_ge(silu_done, upto(pair, 2 * (b - 1) + f // 4, 2))
                act.activation(y[:, f, :], ph[:, f % BANKS, 1:S + 1], ACT.Identity, bias=cb[:, f:f + 1],
                               scale=cwu[:, f, 1:2]).then_inc(y0_done, 1)

            def silu(pair, b, half):
                fs = slice(4 * half, 4 * half + 4)
                act.wait_ge(y2_done, upto(pair, FT * b + 4 * half + 3, FT))
                if b >= 2:
                    act.wait_ge(s_turned, upto(pair, TB * (b - 1) - 1, TB))
                act.activation(sT[:, b % 2, fs, :], y[:, fs, :], ACT.Silu).then_inc(silu_done, 1)

            def turned_back(pair, b, t):
                i = TB * b + t
                act.wait_ge(q_turned, upto(pair, i, TB))
                if i >= TB:
                    act.wait_ge(o_ready, upto(pair, i - TB, TB))
                act.activation(sqT[:, t, :, :], pb[:, :, :], ACT.Copy).then_inc(sqT_out, 1)

            def step(pair, n):
                new, turn, hid, end, last = (is_batch(n - i) for i in range(5))
                for f in range(FT):
                    if last and f == 3:
                        turned_back(pair, n - 4, 1)
                    if hid:
                        middle_tap(pair, n - 2, f)
                    if turn and f == 3:
                        high_part(pair, n - 1)
                    if hid and f % 4 == 3:
                        silu(pair, n - 2, f // 4)
                    if end and f == 7:
                        turned_back(pair, n - 3, 0)
                if new:
                    rounded(pair, n)

            every_step(act, step)

        @block.gpsimd
        def _(pool):
            pool.wait_ge(wchain, 2)
            pool.tensor_scalar(wb[:, :], w2[:, :], scale[:, 1:2], -1.0, ALU.mult, ALU.max).then_inc(w2_near, 1)
            pool.wait_ge(w2_near, 1)
            pool.tensor_scalar(w2[:, :], wb[:, :], 1.0, MAGIC, ALU.min, ALU.add).then_inc(w2_near, 1)
            pool.wait_ge(w2_near, 2)
            pool.tensor_scalar(w2q[:, :, :].rearrange("p a b -> p (a b)"), w2[:, :], MAGIC, None, ALU.subtract
                               ).then_inc(w2_ready, 1)
            pool.wait_ge(magic_set, 1)

            def whole(pair, b, t):
                i = TB * b + t
                pool.wait_ge(s1_done, upto(pair, i, TB))
                if i >= TB:
                    pool.wait_ge(q_turned, upto(pair, i - TB, TB))
                pool.tensor_tensor(sq[:, t, :], s1[:, t, :], magic[:, 0:1].to_broadcast([P, F]), ALU.subtract
                                   ).then_inc(sq_done, 1)

            def step(pair, n):
                for t in range(TB):
                    if is_batch(n - 3):
                        whole(pair, n - 3, t)

            every_step(pool, step)

        @block.tensor
        def _(pe):
            pe.wait_ge(asum_done, 2)
            pe.matmul(po[:, 0:2], consts["ones"][:, :], asum[:, :], start=True, stop=True).then_inc(sum_ready, 1)

            def turn_tokens(pair, b):
                pe.wait_ge(q2_done, upto(pair, 2 * b + 1, 2))
                if b >= 1:
                    pe.wait_ge(x_low, upto(pair, b - 1))
                for k in range(DK):
                    for t in range(TB):
                        mm = pe.transpose(px[:, k, t * P:(t + 1) * P], q2[:, t, k * P:(k + 1) * P], ident[:, :])
                mm.then_inc(x_turned, 1)

            def hidden(pair, b, f):
                if f == 0:
                    pe.wait_ge(x_low, upto(pair, b))
                    if b == 0:
                        pe.wait_ge(w1_ready, 1)
                        pe.wait_ge(pads_set, 4)
                before = f - BANKS if f >= BANKS else (6, 7, 5)[f] - FT
                if FT * b + before >= 0:
                    pe.wait_ge(y2_done, upto(pair, FT * b + before, FT))
                for i, (part, k) in enumerate((part, k) for part in (xh, xl) for k in range(DK)):
                    mm = pe.matmul(ph[:, f % BANKS, 0:S + 2], w1q[:, k, f * P:(f + 1) * P], part[:, b % 2, k, :],
                                   start=(i == 0), stop=(i == 2 * DK - 1))
                mm.then_inc(h_ready, 1)

            def turn_silu(pair, b, t):
                i = TB * b + t
                if t == 0:
                    pe.wait_ge(silu_done, upto(pair, 2 * b + 1, 2))
                if i >= 1:
                    pe.wait_ge(s1_done, upto(pair, i - 1, TB))
                for f in range(FT):
                    mm = pe.transpose(pn[:, f * P:(f + 1) * P], sT[:, b % 2, f, t * P:(t + 1) * P], ident[:, :])
                mm.then_inc(s_turned, 1)

            def turn_back(pair, b, t):
                i = TB * b + t
                pe.wait_ge(sq_done, upto(pair, i, TB))
                if i >= 1:
                    pe.wait_ge(sqT_out, upto(pair, i - 1, TB))
                for f in range(FT):
                    mm = pe.transpose(pb[:, f, :], sq[:, t, f * P:(f + 1) * P], consts["identb"][:, :])
                mm.then_inc(q_turned, 1)

            def product(pair, b, t):
                i = TB * b + t
                pe.wait_ge(sqT_out, upto(pair, i, TB))
                if i >= 1:
                    pe.wait_ge(resid_done, upto(pair, i - 1, TB))
                else:
                    pe.wait_ge(w2_ready, 1)
                for f in range(FT):
                    mm = pe.matmul(po[:, 0:D], sqT[:, t, f, :], w2q[:, f, :], start=(f == 0), stop=(f == FT - 1))
                mm.then_inc(o_ready, 1)

            def step(pair, n):
                new, turn, hid, end, last = (is_batch(n - i) for i in range(5))
                for f in range(FT):
                    if end and f in (2, 6):
                        turn_silu(pair, n - 3, (2, 6).index(f))
                    if last and f == 2:
                        product(pair, n - 4, 0)
                    if turn and f == 3:
                        turn_tokens(pair, n - 1)
                    if last and f == 3:
                        turn_back(pair, n - 4, 1)
                    if last and f == 4:
                        product(pair, n - 4, 1)
                    if hid:
                        hidden(pair, n - 2, f)
                if end:
                    turn_back(pair, n - 3, 0)

            every_step(pe, step)


def build(nc, io, out, sublayers=8, first=0):
    with ExitStack() as top:
        def sb(name, shape, dt=F32):
            return top.enter_context(nc.sbuf_tensor(name, shape, dt))

        x, xt = sb("x", [P, TT, D]), sb("xt", [P, DK, B * S])
        logits, hot1, hot2 = (sb(n, [P, TT, E]) for n in ("logits", "hot1", "hot2"))
        share1, share2, largest1, largest2 = (sb(n, [P, TT]) for n in ("share1", "share2", "largest1", "largest2"))
        dest = sb("dest", [P, 2, TT], U32)
        NT0, NT1 = TT + E - 1, 2 * TT + E - 1
        table = sb("table", [1, NT1 + 2], I32)
        xs0, ys0 = (nc.dram_tensor(n, (NT0 * P, D), F32).ap() for n in ("sorted_x0", "sorted_y0"))
        xs1, ys1 = (nc.dram_tensor(n, (NT1 * P, D), F32).ap() for n in ("sorted_x1", "sorted_y1"))
        rw0, rw1 = sb("rw0", [P, DK, E]), sb("rw1", [P, DK, E])
        ident, identb = sb("ident", [P, P]), sb("identb", [P, P], BF16)
        ones = sb("ones", [P, P])
        zeros, thr, index, rank = sb("zeros", [P, D]), sb("thr", [P, TT]), sb("index", [P, NT1]), sb("rank", [P, E])
        below, rb0 = sb("below", [P, P]), sb("rb0", [P, E])
        trif, tri = sb("trif", [P, 2, P]), sb("tri", [P, 2, P], BF16)
        x_loaded, consts_loaded, routing_loaded, consts_made = (top.enter_context(nc.semaphore(n)) for n in (
            "x_loaded", "consts_loaded", "routing_loaded", "consts_made"))
        stages = Stages(nc)
        consts = {"ident": ident, "identb": identb, "ones": ones, "tri": tri, "zeros": zeros, "thr": thr,
                  "index": index, "rank": rank, "below": below, "rb0": rb0}

        with nc.Block() as block:
            @block.sync
            def _(sp):
                sp.dma_start(ident[:, :], io["ident"]).then_inc(consts_loaded, 16)
                sp.dma_start(trif[:, :, :], io["tri"].rearrange("t p n -> p t n")).then_inc(consts_loaded, 16)
                sp.dma_start(rw0[:, :, :], io["f0_rw"].rearrange("(k p) e -> p k e", p=P)).then_inc(consts_loaded, 16)
                sp.dma_start(rw1[:, :, :], io["f1_rw"].rearrange("(k p) e -> p k e", p=P)).then_inc(consts_loaded, 16)
                sp.dma_start(x[:, :, :], io["x"].rearrange("b (t p) d -> p (b t) d", p=P)).then_inc(x_loaded, 16)
                for dst, name in ((thr, "thr"), (rank, "rank"), (below, "below"), (rb0, "f0_rb")):
                    sp.dma_start(dst[:, :], io[name]).then_inc(routing_loaded, 16)
                sp.dma_start(index[:, :], io["index"][:, 0:NT1]).then_inc(routing_loaded, 16)
                sp.wait_ge(consts_loaded, 64)
                sp.wait_ge(x_loaded, 16)
                sp.wait_ge(routing_loaded, 80)

            @block.vector
            def _(dve):
                dve.memset(ones[:, :], 1.0).then_inc(consts_made, 1)
                dve.memset(zeros[:, :], 0.0).then_inc(consts_made, 1)
                dve.wait_ge(consts_loaded, 64)
                dve.tensor_copy(identb[:, :], ident[:, :]).then_inc(consts_made, 1)
                dve.tensor_scalar(tri[:, :, :], trif[:, :, :], NEG, None, ALU.mult).then_inc(consts_made, 1)

        if first <= 0 < sublayers:
            layer_norm(nc, stages, "n0_", x, xt, ident, first=x_loaded)
            attention0(nc, stages, x, xt, io, consts)
        if first <= 1 < sublayers:
            with nc.sbuf_tensor("xn0", [P, TT, D], F32) as xn:
                layer_norm(nc, stages, "n1_", x, xt, ident, router=(rw0, logits, xn, xs0, zeros))
                gates0(nc, stages, logits, hot1, share1, consts)
                dispatch(nc, stages, "d0_", xn, [hot1], dest[:, 0:1, :], table[:, 0:NT0 + 2], NT0, xs0, consts)
            expert_tiles(nc, stages, "f0_", xs0, ys0, table, NT0, io, consts, gated=False)
            combine(nc, stages, "c0_", x, ys0, dest, [share1])
        if first <= 2 < sublayers:
            layer_norm(nc, stages, "n2_", x, xt, ident)
            attention1(nc, stages, x, xt, io, consts)
        if first <= 3 < sublayers:
            with nc.sbuf_tensor("xn1", [P, TT, D], F32) as xn:
                layer_norm(nc, stages, "n3_", x, xt, ident, router=(rw1, logits, xn, xs1, zeros))
                gates1(nc, stages, logits, hot1, hot2, largest1, largest2, consts)
                dispatch(nc, stages, "d1_", xn, [hot1, hot2], dest, table, NT1, xs1, consts,
                         lambda ctx: shares1(nc, stages, logits, hot1, largest1, largest2, share1, share2, ctx))
            expert_tiles(nc, stages, "f1_", xs1, ys1, table, NT1, io, consts, gated=True)
            combine(nc, stages, "c1_", x, ys1, dest, [share1, share2])
        if first <= 4 < sublayers:
            layer_norm(nc, stages, "n4_", x, xt, ident)
            linear_attention(nc, stages, x, xt, io)
        if first <= 5 < sublayers:
            layer_norm(nc, stages, "n5_", x, xt, ident)
            scaled_linear(nc, stages, x, xt, io)
        if first <= 6 < sublayers:
            layer_norm(nc, stages, "n6_", x, xt, ident)
            attention3(nc, stages, x, xt, io, consts)
        if sublayers > 7:
            bit_ffn(nc, stages, x, ident, io, consts, out)
        else:
            stored = top.enter_context(nc.semaphore("stored"))
            with nc.Block() as block:
                @block.sync
                def _(sp):
                    sp.dma_start(out.rearrange("b (t p) d -> p (b t) d", p=P), x[:, :, :]).then_inc(stored, 16)
                    sp.wait_ge(stored, 16)


def lay_out(i):
    import numpy as np

    def t(a):
        return np.ascontiguousarray(np.swapaxes(a, -1, -2))

    def rows(a):
        return np.ascontiguousarray(np.broadcast_to(a, (P, a.shape[0])))

    def padded(a):
        out = np.zeros(a.shape[:-1] + (H, 32), np.float32)
        out[..., :D0] = a.reshape(a.shape[:-1] + (H, D0))
        return out

    f = {k: np.asarray(v) for k, v in i.items()}
    io = {"x": f["x"], "ctx": f["ctx_1024"], "ctxT": t(f["ctx_1024"]),
          "mask": f["mask_BxSxS2_ik1"], "maskT": t(f["mask_BxSxS2_ik1"])}
    for n in "qkv":
        io["a0_w" + n] = t(f["L0_xattn_W" + n]).reshape(DK, P, D)
    for n in "qk":
        io["a0_w" + n] = t(io["a0_w" + n].reshape(D, DK, P // D0, D0)).reshape(DK, P, D)
    io["a0_bqk"] = np.stack([t(t(f["L0_xattn_b" + n].reshape(DK, P // D0, D0)).reshape(DK, P)) for n in "qk"], 1)
    io["a0_bv"] = rows(f["L0_xattn_bv"])
    wo = padded(f["L0_xattn_Wo"])
    wo[:, 0, D0] = f["L0_xattn_bo"]
    io["a0_wo"] = t(wo.reshape(D, H * 32)).reshape(H * 32 // P, P, D)
    sel = np.zeros((4, 32, 4, 32), np.float32)
    for g in range(4):
        sel[g, D0, g, :] = 1.0
    io["a0_sel"] = sel.reshape(P, P)
    for n in "qkv":
        io["a1_w" + n] = t(f["L1_xattn_w_" + n]).reshape(DK, P, H * D1)
    io["a1_wo"] = t(f["L1_xattn_w_o"]).reshape(H * D1 // P, P, D)
    io["ident"] = np.eye(P, dtype=np.float32)
    io["tri"] = np.stack([np.triu(np.ones((P, P), np.float32), 1), np.tril(np.ones((P, P), np.float32), -1)])
    io["below"] = np.triu(np.ones((P, P), np.float32), 1)
    io["thr"] = rows(np.arange(TT, dtype=np.float32) * P)
    io["index"] = rows(np.arange(2 * TT + E, dtype=np.float32))
    io["rank"] = rows(np.arange(E, 0, -1).astype(np.float32))
    io["f0_rw"], io["f0_rb"] = f["L0_ffn_router_W"], rows(f["L0_ffn_router_b"])
    io["f0_w1"], io["f0_b1"] = f["L0_ffn_W1"], f["L0_ffn_b1"].reshape(E, FT, P).transpose(2, 0, 1)
    io["f0_w2"], io["f0_b2"] = f["L0_ffn_W2"], rows(f["L0_ffn_b2"].reshape(-1)).reshape(P, E, D)
    io["f1_rw"] = t(f["L1_ffn_gate_w"])
    io["f1_w1"], io["f1_w3"], io["f1_w2"] = t(f["L1_ffn_w1"]), t(f["L1_ffn_w3"]), t(f["L1_ffn_w2"])
    io["f2_cb"], io["f2_scb"], io["f2_bias"] = t(f["L2_ffn_CB"]), rows(f["L2_ffn_SCB"]), rows(f["L2_ffn_bias"])
    for n in "qkv":
        io["a3_w" + n] = t(f["L3_xattn_W" + n])
    io["a3_bq"], io["a3_bk"] = (t(f["L3_xattn_b" + n].reshape(DK, P)) for n in "qk")
    io["a3_bv"] = rows(f["L3_xattn_bv"])
    io["f3_w1"], io["f3_w2"] = t(f["L3_ffn_w1"]), t(f["L3_ffn_w2"])
    io["f3_cw"], io["f3_cb"] = f["L3_ffn_conv_w"].reshape(F, 3), t(f["L3_ffn_conv_b"].reshape(FT, P))
    return {k: np.ascontiguousarray(v) for k, v in io.items()}


def kernel(**inputs):
    import concourse.bacc as bacc
    from concourse.bass_utils import run_bass_kernel_spmd

    nc = bacc.Bacc("TRN2", target_bir_lowering=False, num_devices=1)
    arrays = lay_out(inputs)
    io = {k: nc.dram_tensor("in_" + k, v.shape, mybir.dt.from_np(v.dtype), kind="ExternalInput").ap()
          for k, v in arrays.items()}
    out = nc.dram_tensor("out", (B, S, D), F32, kind="ExternalOutput").ap()
    build(nc, io, out)
    r = run_bass_kernel_spmd(nc, [{"in_" + k: v for k, v in arrays.items()}], core_ids=[0])
    return r.results[0]["out"]
```
